# Optimizing a Trainium2 kernel written in Bass

```python
import numpy as np
import jax
import jax.numpy as jnp

def _softmax(x, axis=-1):
    return jax.nn.softmax(x, axis=axis)

def _gelu(x):
    return jax.nn.gelu(x, approximate=True)

def _silu(x):
    return jax.nn.silu(x)

def _sigmoid(x):
    return jax.nn.sigmoid(x)

def _layernorm(x, axis=-1, eps=1e-05):
    m = jnp.mean(x, axis=axis, keepdims=True)
    v = jnp.var(x, axis=axis, keepdims=True)
    return (x - m) / jnp.sqrt(v + eps)

def _scatter_add(tgt, idx, src, axis=0):
    return tgt.at[idx].add(src)

def _segment_sum(src, seg, n):
    return jax.ops.segment_sum(src, seg, n)
kernel_name = 'mk_gps_d4_gnn_r32_bcc245'

def setup_inputs(seed: int=0):
    np.random.seed(seed)
    _w = jnp.asarray

    def _rec_inputs():
        import jax
        import jax.numpy as jnp
        _gk = jax.random.key(seed)
        x = -0.0002117 + 1 * jax.random.normal(jax.random.fold_in(_gk, 1), (3125, 256), jnp.float32)
        _s = jax.random.randint(jax.random.fold_in(_gk, 2), (25000,), 0, 3125, jnp.int32)
        _d = jax.random.randint(jax.random.fold_in(_gk, 3), (25000,), 0, 3125, jnp.int32)
        _loop = jnp.arange(3125, dtype=jnp.int32)
        src = jnp.concatenate([_s, _d, _loop])
        dst = jnp.concatenate([_d, _s, _loop])
        _o = jnp.argsort(dst, stable=True)
        src = src[_o]
        dst = dst[_o]
        edge_type_64 = jax.random.randint(jax.random.fold_in(_gk, 13), (53125,), 0, 64, jnp.int32)
        edge_weight = jax.random.uniform(jax.random.fold_in(_gk, 14), (53125,), jnp.float32, 0.0, 1)
        return (x, src, dst, edge_type_64, edge_weight)
    x, src, dst, edge_type_64, edge_weight = _rec_inputs()

    def _L0_gnn_setup():
        import jax, jax.numpy as jnp
        import numpy as np
        N = 3125
        E = 100000
        N_IN = 256
        N_OUT = 256
        key = jax.random.key(seed)
        k1, k2, k3, k4, k5, k6 = jax.random.split(key, 6)
        x = jax.random.normal(k1, (N, N_IN), dtype=jnp.float32)
        edge_row = jax.random.randint(k2, (E,), 0, N, dtype=jnp.int32)
        edge_col = jax.random.randint(k3, (E,), 0, N, dtype=jnp.int32)
        edge_val = jax.random.uniform(k4, (E,), dtype=jnp.float32)
        bound = 1.0 / np.sqrt(N_IN)
        W = jax.random.uniform(k5, (N_OUT, N_IN), minval=-bound, maxval=bound, dtype=jnp.float32)
        b = jax.random.uniform(k6, (N_OUT,), minval=-bound, maxval=bound, dtype=jnp.float32)
        return {'x': x, 'edge_row': edge_row, 'edge_col': edge_col, 'edge_val': edge_val, 'W': W, 'b': b}
    _L0_gnn_all = _L0_gnn_setup()
    _L0_gnn_in = {k: v for k, v in _L0_gnn_all.items() if k in ('W', 'b')}
    del _L0_gnn_all

    def _L0_mix_setup():
        import jax, jax.numpy as jnp
        import numpy as np
        D_MODEL = 256
        NHEAD = 8
        D_HEAD = D_MODEL // NHEAD
        DIM_FF = 1024
        B, L = (4, 512)
        LN_EPS = 1e-05

        def _layernorm(x, g, b):
            mu = jnp.mean(x, axis=-1, keepdims=True)
            var = jnp.mean((x - mu) ** 2, axis=-1, keepdims=True)
            return (x - mu) * jax.lax.rsqrt(var + LN_EPS) * g + b

        def _phi(x):
            return jnp.where(x > 0, x + 1.0, jnp.exp(x))
        key = jax.random.key(seed)
        ks = jax.random.split(key, 16)
        s_in = 1.0 / np.sqrt(D_MODEL)
        s_ff = 1.0 / np.sqrt(DIM_FF)
        inp = {'x': jax.random.normal(ks[0], (B, L, D_MODEL), dtype=jnp.float32), 'Wq': jax.random.normal(ks[1], (D_MODEL, D_MODEL), dtype=jnp.float32) * s_in, 'bq': jnp.zeros((D_MODEL,), jnp.float32), 'Wk': jax.random.normal(ks[2], (D_MODEL, D_MODEL), dtype=jnp.float32) * s_in, 'bk': jnp.zeros((D_MODEL,), jnp.float32), 'Wv': jax.random.normal(ks[3], (D_MODEL, D_MODEL), dtype=jnp.float32) * s_in, 'bv': jnp.zeros((D_MODEL,), jnp.float32), 'Wo': jax.random.normal(ks[4], (D_MODEL, D_MODEL), dtype=jnp.float32) * s_in, 'bo': jnp.zeros((D_MODEL,), jnp.float32), 'W1': jax.random.normal(ks[5], (D_MODEL, DIM_FF), dtype=jnp.float32) * s_in, 'b1': jnp.zeros((DIM_FF,), jnp.float32), 'W2': jax.random.normal(ks[6], (DIM_FF, D_MODEL), dtype=jnp.float32) * s_ff, 'b2': jnp.zeros((D_MODEL,), jnp.float32), 'ln1_g': jnp.ones((D_MODEL,), jnp.float32), 'ln1_b': jnp.zeros((D_MODEL,), jnp.float32), 'ln2_g': jnp.ones((D_MODEL,), jnp.float32), 'ln2_b': jnp.zeros((D_MODEL,), jnp.float32)}
        return inp
    _L0_mix_all = _L0_mix_setup()
    _L0_mix_in = {k: v for k, v in _L0_mix_all.items() if k in ('Wq', 'bq', 'Wk', 'bk', 'Wv', 'bv', 'Wo', 'bo', 'W1', 'b1', 'W2', 'b2', 'ln1_g', 'ln1_b', 'ln2_g', 'ln2_b')}
    del _L0_mix_all

    def _L0_ffn_setup():
        import jax, jax.numpy as jnp
        import numpy as np
        C = 256
        HID = 1024
        E = 8
        TEMP = 1.0
        key = jax.random.key(seed)
        ks = jax.random.split(key, 7)
        x = jax.random.normal(ks[0], (8, 512, C), dtype=jnp.float32)
        W1 = jax.random.normal(ks[1], (C, HID), dtype=jnp.float32) * 0.02
        b1 = jnp.zeros((HID,), dtype=jnp.float32)
        Wg = jax.random.normal(ks[2], (HID, E), dtype=jnp.float32) * 0.02
        bg = jnp.zeros((E,), dtype=jnp.float32)
        Wd = jax.random.normal(ks[3], (E, HID, C), dtype=jnp.float32) * 0.02
        bd = jnp.zeros((E, C), dtype=jnp.float32)
        return {'x': x, 'W1': W1, 'b1': b1, 'Wg': Wg, 'bg': bg, 'Wd': Wd, 'bd': bd}
    _L0_ffn_all = _L0_ffn_setup()
    _L0_ffn_in = {k: v for k, v in _L0_ffn_all.items() if k in ('W1', 'b1', 'Wg', 'bg', 'Wd', 'bd')}
    del _L0_ffn_all

    def _L1_gnn_setup():
        import jax, jax.numpy as jnp
        import numpy as np
        N_NODES = 50000
        N_EDGES = 15625
        IN_DIM = 256
        HID = 64
        HEADS = 4
        N_REL = 64
        key = jax.random.key(seed)
        ks = jax.random.split(key, 16)
        s = 0.02
        return {'node_features': jax.random.normal(ks[0], (N_NODES, IN_DIM), jnp.float32), 'edge_index': jax.random.randint(ks[1], (2, N_EDGES), 0, N_NODES, jnp.int32), 'edge_relations': jax.random.randint(ks[2], (N_EDGES,), 0, N_REL, jnp.int32), 'query_emb': jax.random.normal(ks[3], (IN_DIM,), jnp.float32), 'Wq': jax.random.normal(ks[4], (IN_DIM, HID * HEADS), jnp.float32) * s, 'bq': jnp.zeros((HID * HEADS,), jnp.float32), 'Wk': jax.random.normal(ks[5], (IN_DIM, HID * HEADS), jnp.float32) * s, 'bk': jnp.zeros((HID * HEADS,), jnp.float32), 'Wv': jax.random.normal(ks[6], (IN_DIM, HID * HEADS), jnp.float32) * s, 'bv': jnp.zeros((HID * HEADS,), jnp.float32), 'rel_w': jax.random.normal(ks[7], (N_REL, HID), jnp.float32) * s, 'Wo': jax.random.normal(ks[8], (HID * HEADS, IN_DIM), jnp.float32) * s, 'bo': jnp.zeros((IN_DIM,), jnp.float32), 'gamma': jnp.ones((IN_DIM,), jnp.float32), 'beta': jnp.zeros((IN_DIM,), jnp.float32)}
    _L1_gnn_all = _L1_gnn_setup()
    _L1_gnn_in = {k: v for k, v in _L1_gnn_all.items() if k in ('query_emb', 'Wq', 'bq', 'Wk', 'bk', 'Wv', 'bv', 'rel_w', 'Wo', 'bo', 'gamma', 'beta')}
    del _L1_gnn_all

    def _L1_mix_setup():
        import jax, jax.numpy as jnp
        import numpy as np
        DIM = 256
        HEADS = 4
        DIM_HEAD = 32
        NUM_MEM = 4
        HIDDEN = HEADS * DIM_HEAD
        SCALE = DIM_HEAD ** (-0.5)

        def rmsnorm(x, g):
            n = jnp.linalg.norm(x, axis=-1, keepdims=True)
            return x / jnp.maximum(n, 1e-12) * g * x.shape[-1] ** 0.5
        key = jax.random.key(seed)
        ks = jax.random.split(key, 8)
        B, N = (4, 512)
        return {'x': jax.random.normal(ks[0], (B, N, DIM), jnp.float32), 't': jax.random.normal(ks[1], (B,), jnp.float32), 'w_qkv': jax.random.normal(ks[2], (DIM, 3 * HIDDEN), jnp.float32) * 0.02, 'mem_kv': jax.random.normal(ks[3], (2, HEADS, DIM_HEAD, NUM_MEM), jnp.float32), 'w_out': jax.random.normal(ks[4], (HIDDEN, DIM), jnp.float32) * 0.02, 'b_out': jnp.zeros((DIM,), jnp.float32), 'g_out': jnp.ones((DIM,), jnp.float32), 'g_pre': jnp.ones((DIM,), jnp.float32)}
    _L1_mix_all = _L1_mix_setup()
    _L1_mix_in = {k: v for k, v in _L1_mix_all.items() if k in ('t', 'w_qkv', 'mem_kv', 'w_out', 'b_out', 'g_out', 'g_pre')}
    del _L1_mix_all

    def _L1_ffn_setup():
        import jax, jax.numpy as jnp
        import numpy as np
        E = 8
        K = 2
        D = 256
        H = 512
        DOUT = 256
        EPS = 1e-05
        key = jax.random.key(seed)
        ks = jax.random.split(key, 9)
        s = 0.02
        return {'x': jax.random.normal(ks[0], (4, 256, D), jnp.float32), 'gamma': 1.0 + 0.05 * jax.random.normal(ks[1], (D,), jnp.float32), 'beta': 0.05 * jax.random.normal(ks[2], (D,), jnp.float32), 'Wr': 0.01 * jax.random.normal(ks[3], (D, E), jnp.float32), 'br': jnp.zeros((E,), jnp.float32), 'W1': s * jax.random.normal(ks[4], (E, D, H), jnp.float32), 'b1': s * jax.random.normal(ks[5], (E, H), jnp.float32), 'W2': s * jax.random.normal(ks[6], (E, H, DOUT), jnp.float32), 'b2': s * jax.random.normal(ks[7], (E, DOUT), jnp.float32)}
    _L1_ffn_all = _L1_ffn_setup()
    _L1_ffn_in = {k: v for k, v in _L1_ffn_all.items() if k in ('gamma', 'beta', 'Wr', 'br', 'W1', 'b1', 'W2', 'b2')}
    del _L1_ffn_all

    def _L2_gnn_setup():
        import jax, jax.numpy as jnp
        import numpy as np
        N = 50000
        E = 25000
        F_IN = 256
        K = 8
        F_OUT = 32
        NEG_SLOPE = 0.2
        key = jax.random.key(seed)
        k1, k2, k3, k4, k5, k6 = jax.random.split(key, 6)
        x = jax.random.normal(k1, (N, F_IN), dtype=jnp.float32)
        edge_index = jax.random.randint(k2, (2, E), 0, N, dtype=jnp.int64)
        W = jax.random.normal(k3, (F_IN, K * F_OUT), dtype=jnp.float32) * (2.0 / (F_IN + K * F_OUT)) ** 0.5
        b = jax.random.uniform(k4, (K * F_OUT,), dtype=jnp.float32)
        a_src = jax.random.normal(k5, (1, K, F_OUT), dtype=jnp.float32) * (2.0 / (K * F_OUT + 1)) ** 0.5
        a_trg = jax.random.normal(k6, (1, K, F_OUT), dtype=jnp.float32) * (2.0 / (K * F_OUT + 1)) ** 0.5
        return {'x': x, 'edge_index': edge_index, 'W': W, 'b': b, 'a_src': a_src, 'a_trg': a_trg}
    _L2_gnn_all = _L2_gnn_setup()
    _L2_gnn_in = {k: v for k, v in _L2_gnn_all.items() if k in ('W', 'b', 'a_src', 'a_trg')}
    del _L2_gnn_all

    def _L2_mix_setup():
        import jax, jax.numpy as jnp
        import numpy as np
        NUM_HEADS = 8
        key = jax.random.key(seed)
        ks = jax.random.split(key, 5)
        B, N, C = (8, 512, 256)
        x = jax.random.normal(ks[0], (B, N, C), dtype=jnp.float32)
        Wq = jax.random.normal(ks[1], (C, C), dtype=jnp.float32) * 0.02
        Wkv = jax.random.normal(ks[2], (2 * C, C), dtype=jnp.float32) * 0.02
        Wproj = jax.random.normal(ks[3], (C, C), dtype=jnp.float32) * 0.02
        bproj = jnp.zeros((C,), dtype=jnp.float32)
        return {'x': x, 'Wq': Wq, 'Wkv': Wkv, 'Wproj': Wproj, 'bproj': bproj}
    _L2_mix_all = _L2_mix_setup()
    _L2_mix_in = {k: v for k, v in _L2_mix_all.items() if k in ('Wq', 'Wkv', 'Wproj', 'bproj')}
    del _L2_mix_all

    def _L2_ffn_setup():
        import jax, jax.numpy as jnp
        import numpy as np
        BN_EPS = 0.001

        def _bn(h, g, b, m, v):
            return g * (h - m) * jax.lax.rsqrt(v + BN_EPS) + b
        key = jax.random.key(seed)
        ks = jax.random.split(key, 8)
        B, F, Df = (256, 64, 256)
        E, H, D = (8, 256, 256)
        s1 = 1.0 / np.sqrt(Df)
        s2 = 1.0 / np.sqrt(H)
        return {'x': jax.random.normal(ks[0], (B, F, Df), jnp.float32), 'Wr': jax.random.normal(ks[1], (Df, E), jnp.float32) * s1, 'br': jnp.zeros((E,), jnp.float32), 'W1': jax.random.normal(ks[2], (E, Df, H), jnp.float32) * s1, 'b1': jnp.zeros((E, H), jnp.float32), 'g1': jnp.ones((E, H), jnp.float32), 'be1': jnp.zeros((E, H), jnp.float32), 'm1': jnp.zeros((E, H), jnp.float32), 'v1': jnp.ones((E, H), jnp.float32), 'W2': jax.random.normal(ks[3], (E, H, H), jnp.float32) * s2, 'b2': jnp.zeros((E, H), jnp.float32), 'g2': jnp.ones((E, H), jnp.float32), 'be2': jnp.zeros((E, H), jnp.float32), 'm2': jnp.zeros((E, H), jnp.float32), 'v2': jnp.ones((E, H), jnp.float32), 'Wo': jax.random.normal(ks[4], (E, H, D), jnp.float32) * s2, 'bo': jnp.zeros((E, D), jnp.float32)}
    _L2_ffn_all = _L2_ffn_setup()
    _L2_ffn_in = {k: v for k, v in _L2_ffn_all.items() if k in ('Wr', 'br', 'W1', 'b1', 'g1', 'be1', 'm1', 'v1', 'W2', 'b2', 'g2', 'be2', 'm2', 'v2', 'Wo', 'bo')}
    del _L2_ffn_all

    def _L3_gnn_setup():
        import jax, jax.numpy as jnp
        import numpy as np
        N_NODES = 3125
        N_EDGES = 100000
        D_IN = 256
        D_OUT = 256
        key = jax.random.key(seed)
        k1, k2, k3, k4, k5 = jax.random.split(key, 5)
        x = jax.random.normal(k1, (N_NODES, D_IN), dtype=jnp.float32)
        limit = float(np.sqrt(6.0 / (D_IN + D_OUT)))
        weight = jax.random.uniform(k2, (D_IN, D_OUT), dtype=jnp.float32, minval=-limit, maxval=limit)
        edge_val = jax.random.uniform(k3, (N_EDGES,), dtype=jnp.float32)
        edge_row = jax.random.randint(k4, (N_EDGES,), 0, N_NODES, dtype=jnp.int32)
        edge_col = jax.random.randint(k5, (N_EDGES,), 0, N_NODES, dtype=jnp.int32)
        return {'x': x, 'weight': weight, 'edge_val': edge_val, 'edge_row': edge_row, 'edge_col': edge_col}
    _L3_gnn_all = _L3_gnn_setup()
    _L3_gnn_in = {k: v for k, v in _L3_gnn_all.items() if k in ('weight',)}
    del _L3_gnn_all

    def _L3_mix_setup():
        import jax, jax.numpy as jnp
        import numpy as np
        NHEAD = 8
        ATT_EPS = 1e-06
        LN_EPS = 1e-05

        def _layernorm(x, g, b):
            mu = jnp.mean(x, axis=-1, keepdims=True)
            var = jnp.mean(jnp.square(x - mu), axis=-1, keepdims=True)
            return (x - mu) * jax.lax.rsqrt(var + LN_EPS) * g + b
        key = jax.random.key(seed)
        ks = jax.random.split(key, 7)
        N, L, C = (4, 512, 256)
        s = 1.0 / np.sqrt(C)
        return {'x': jax.random.normal(ks[0], (N, L, C), jnp.float32), 'Wq': jax.random.normal(ks[1], (C, C), jnp.float32) * s, 'Wk': jax.random.normal(ks[2], (C, C), jnp.float32) * s, 'Wv': jax.random.normal(ks[3], (C, C), jnp.float32) * s, 'Wm': jax.random.normal(ks[4], (C, C), jnp.float32) * s, 'W1': jax.random.normal(ks[5], (2 * C, 2 * C), jnp.float32) * (1.0 / np.sqrt(2 * C)), 'W2': jax.random.normal(ks[6], (2 * C, C), jnp.float32) * (1.0 / np.sqrt(2 * C)), 'g1': jnp.ones((C,), jnp.float32), 'b1': jnp.zeros((C,), jnp.float32), 'g2': jnp.ones((C,), jnp.float32), 'b2': jnp.zeros((C,), jnp.float32)}
    _L3_mix_all = _L3_mix_setup()
    _L3_mix_in = {k: v for k, v in _L3_mix_all.items() if k in ('Wq', 'Wk', 'Wv', 'Wm', 'W1', 'W2', 'g1', 'b1', 'g2', 'b2')}
    del _L3_mix_all

    def _L3_ffn_setup():
        import jax, jax.numpy as jnp
        import numpy as np
        NUM_EXPERTS = 8
        TOP_K = 2
        B, S, D = (8, 256, 256)

        def _moe(tokens, router_w, w1, b1, w2, b2):
            N = tokens.shape[0]
            E = router_w.shape[0]
            logits = tokens.astype(jnp.float32) @ router_w.astype(jnp.float32).T
            probs = jax.nn.softmax(logits, axis=-1)
            rw, re = jax.lax.top_k(probs, TOP_K)
            if TOP_K > 1:
                rw = rw / jnp.maximum(rw.sum(-1, keepdims=True), 1e-12)
            rw = rw.astype(tokens.dtype)
            combine = jnp.zeros((N, E), tokens.dtype).at[jnp.arange(N)[:, None], re].set(rw)
            out = tokens
            for e in range(E):
                h = jax.nn.gelu(tokens @ w1[e] + b1[e], approximate=False)
                y = h @ w2[e] + b2[e]
                out = out + combine[:, e:e + 1] * y
            return out
        key = jax.random.key(seed)
        ks = jax.random.split(key, 4)
        scale = 1.0 / np.sqrt(D).astype(np.float32)
        return {'input_embeddings': jax.random.normal(ks[0], (B, S, D), jnp.float32), 'router_w': jax.random.normal(ks[1], (NUM_EXPERTS, D), jnp.float32) * scale, 'w1': jax.random.normal(ks[2], (NUM_EXPERTS, D, D), jnp.float32) * scale, 'b1': jnp.zeros((NUM_EXPERTS, D), jnp.float32), 'w2': jax.random.normal(ks[3], (NUM_EXPERTS, D, D), jnp.float32) * scale, 'b2': jnp.zeros((NUM_EXPERTS, D), jnp.float32)}
    _L3_ffn_all = _L3_ffn_setup()
    _L3_ffn_in = {k: v for k, v in _L3_ffn_all.items() if k in ('router_w', 'w1', 'b1', 'w2', 'b2')}
    del _L3_ffn_all
    return {'x': x, 'src': src, 'dst': dst, 'edge_type_64': edge_type_64, 'edge_weight': edge_weight, 'L0_gnn_W': _L0_gnn_in['W'], 'L0_gnn_b': _L0_gnn_in['b'], 'L0_mix_Wq': _L0_mix_in['Wq'], 'L0_mix_bq': _L0_mix_in['bq'], 'L0_mix_Wk': _L0_mix_in['Wk'], 'L0_mix_bk': _L0_mix_in['bk'], 'L0_mix_Wv': _L0_mix_in['Wv'], 'L0_mix_bv': _L0_mix_in['bv'], 'L0_mix_Wo': _L0_mix_in['Wo'], 'L0_mix_bo': _L0_mix_in['bo'], 'L0_mix_W1': _L0_mix_in['W1'], 'L0_mix_b1': _L0_mix_in['b1'], 'L0_mix_W2': _L0_mix_in['W2'], 'L0_mix_b2': _L0_mix_in['b2'], 'L0_mix_ln1_g': _L0_mix_in['ln1_g'], 'L0_mix_ln1_b': _L0_mix_in['ln1_b'], 'L0_mix_ln2_g': _L0_mix_in['ln2_g'], 'L0_mix_ln2_b': _L0_mix_in['ln2_b'], 'L0_ffn_W1': _L0_ffn_in['W1'], 'L0_ffn_b1': _L0_ffn_in['b1'], 'L0_ffn_Wg': _L0_ffn_in['Wg'], 'L0_ffn_bg': _L0_ffn_in['bg'], 'L0_ffn_Wd': _L0_ffn_in['Wd'], 'L0_ffn_bd': _L0_ffn_in['bd'], 'L1_gnn_query_emb': _L1_gnn_in['query_emb'], 'L1_gnn_Wq': _L1_gnn_in['Wq'], 'L1_gnn_bq': _L1_gnn_in['bq'], 'L1_gnn_Wk': _L1_gnn_in['Wk'], 'L1_gnn_bk': _L1_gnn_in['bk'], 'L1_gnn_Wv': _L1_gnn_in['Wv'], 'L1_gnn_bv': _L1_gnn_in['bv'], 'L1_gnn_rel_w': _L1_gnn_in['rel_w'], 'L1_gnn_Wo': _L1_gnn_in['Wo'], 'L1_gnn_bo': _L1_gnn_in['bo'], 'L1_gnn_gamma': _L1_gnn_in['gamma'], 'L1_gnn_beta': _L1_gnn_in['beta'], 'L1_mix_t': _L1_mix_in['t'], 'L1_mix_w_qkv': _L1_mix_in['w_qkv'], 'L1_mix_mem_kv': _L1_mix_in['mem_kv'], 'L1_mix_w_out': _L1_mix_in['w_out'], 'L1_mix_b_out': _L1_mix_in['b_out'], 'L1_mix_g_out': _L1_mix_in['g_out'], 'L1_mix_g_pre': _L1_mix_in['g_pre'], 'L1_ffn_gamma': _L1_ffn_in['gamma'], 'L1_ffn_beta': _L1_ffn_in['beta'], 'L1_ffn_Wr': _L1_ffn_in['Wr'], 'L1_ffn_br': _L1_ffn_in['br'], 'L1_ffn_W1': _L1_ffn_in['W1'], 'L1_ffn_b1': _L1_ffn_in['b1'], 'L1_ffn_W2': _L1_ffn_in['W2'], 'L1_ffn_b2': _L1_ffn_in['b2'], 'L2_gnn_W': _L2_gnn_in['W'], 'L2_gnn_b': _L2_gnn_in['b'], 'L2_gnn_a_src': _L2_gnn_in['a_src'], 'L2_gnn_a_trg': _L2_gnn_in['a_trg'], 'L2_mix_Wq': _L2_mix_in['Wq'], 'L2_mix_Wkv': _L2_mix_in['Wkv'], 'L2_mix_Wproj': _L2_mix_in['Wproj'], 'L2_mix_bproj': _L2_mix_in['bproj'], 'L2_ffn_Wr': _L2_ffn_in['Wr'], 'L2_ffn_br': _L2_ffn_in['br'], 'L2_ffn_W1': _L2_ffn_in['W1'], 'L2_ffn_b1': _L2_ffn_in['b1'], 'L2_ffn_g1': _L2_ffn_in['g1'], 'L2_ffn_be1': _L2_ffn_in['be1'], 'L2_ffn_m1': _L2_ffn_in['m1'], 'L2_ffn_v1': _L2_ffn_in['v1'], 'L2_ffn_W2': _L2_ffn_in['W2'], 'L2_ffn_b2': _L2_ffn_in['b2'], 'L2_ffn_g2': _L2_ffn_in['g2'], 'L2_ffn_be2': _L2_ffn_in['be2'], 'L2_ffn_m2': _L2_ffn_in['m2'], 'L2_ffn_v2': _L2_ffn_in['v2'], 'L2_ffn_Wo': _L2_ffn_in['Wo'], 'L2_ffn_bo': _L2_ffn_in['bo'], 'L3_gnn_weight': _L3_gnn_in['weight'], 'L3_mix_Wq': _L3_mix_in['Wq'], 'L3_mix_Wk': _L3_mix_in['Wk'], 'L3_mix_Wv': _L3_mix_in['Wv'], 'L3_mix_Wm': _L3_mix_in['Wm'], 'L3_mix_W1': _L3_mix_in['W1'], 'L3_mix_W2': _L3_mix_in['W2'], 'L3_mix_g1': _L3_mix_in['g1'], 'L3_mix_b1': _L3_mix_in['b1'], 'L3_mix_g2': _L3_mix_in['g2'], 'L3_mix_b2': _L3_mix_in['b2'], 'L3_ffn_router_w': _L3_ffn_in['router_w'], 'L3_ffn_w1': _L3_ffn_in['w1'], 'L3_ffn_b1': _L3_ffn_in['b1'], 'L3_ffn_w2': _L3_ffn_in['w2'], 'L3_ffn_b2': _L3_ffn_in['b2']}

def reference(x, src, dst, edge_type_64, edge_weight, L0_gnn_W, L0_gnn_b, L0_mix_Wq, L0_mix_bq, L0_mix_Wk, L0_mix_bk, L0_mix_Wv, L0_mix_bv, L0_mix_Wo, L0_mix_bo, L0_mix_W1, L0_mix_b1, L0_mix_W2, L0_mix_b2, L0_mix_ln1_g, L0_mix_ln1_b, L0_mix_ln2_g, L0_mix_ln2_b, L0_ffn_W1, L0_ffn_b1, L0_ffn_Wg, L0_ffn_bg, L0_ffn_Wd, L0_ffn_bd, L1_gnn_query_emb, L1_gnn_Wq, L1_gnn_bq, L1_gnn_Wk, L1_gnn_bk, L1_gnn_Wv, L1_gnn_bv, L1_gnn_rel_w, L1_gnn_Wo, L1_gnn_bo, L1_gnn_gamma, L1_gnn_beta, L1_mix_t, L1_mix_w_qkv, L1_mix_mem_kv, L1_mix_w_out, L1_mix_b_out, L1_mix_g_out, L1_mix_g_pre, L1_ffn_gamma, L1_ffn_beta, L1_ffn_Wr, L1_ffn_br, L1_ffn_W1, L1_ffn_b1, L1_ffn_W2, L1_ffn_b2, L2_gnn_W, L2_gnn_b, L2_gnn_a_src, L2_gnn_a_trg, L2_mix_Wq, L2_mix_Wkv, L2_mix_Wproj, L2_mix_bproj, L2_ffn_Wr, L2_ffn_br, L2_ffn_W1, L2_ffn_b1, L2_ffn_g1, L2_ffn_be1, L2_ffn_m1, L2_ffn_v1, L2_ffn_W2, L2_ffn_b2, L2_ffn_g2, L2_ffn_be2, L2_ffn_m2, L2_ffn_v2, L2_ffn_Wo, L2_ffn_bo, L3_gnn_weight, L3_mix_Wq, L3_mix_Wk, L3_mix_Wv, L3_mix_Wm, L3_mix_W1, L3_mix_W2, L3_mix_g1, L3_mix_b1, L3_mix_g2, L3_mix_b2, L3_ffn_router_w, L3_ffn_w1, L3_ffn_b1, L3_ffn_w2, L3_ffn_b2):
    import jax
    import jax.numpy as jnp

    def _L0_gnn_ref(x, edge_row, edge_col, edge_val, W, b):
        import jax, jax.numpy as jnp
        import numpy as np
        N = 3125
        E = 100000
        N_IN = 256
        N_OUT = 256
        h = x @ W.T + b
        msg = edge_val[:, None] * h[edge_col]
        agg = jax.ops.segment_sum(msg, edge_row, num_segments=N)
        return jax.nn.elu(agg)

    def _L0_mix_ref(x, Wq, bq, Wk, bk, Wv, bv, Wo, bo, W1, b1, W2, b2, ln1_g, ln1_b, ln2_g, ln2_b):
        import jax, jax.numpy as jnp
        import numpy as np
        D_MODEL = 256
        NHEAD = 8
        D_HEAD = D_MODEL // NHEAD
        DIM_FF = 1024
        B, L = (4, 512)
        LN_EPS = 1e-05

        def _layernorm(x, g, b):
            mu = jnp.mean(x, axis=-1, keepdims=True)
            var = jnp.mean((x - mu) ** 2, axis=-1, keepdims=True)
            return (x - mu) * jax.lax.rsqrt(var + LN_EPS) * g + b

        def _phi(x):
            return jnp.where(x > 0, x + 1.0, jnp.exp(x))
        Bq, Lq, _ = x.shape
        q = (x @ Wq + bq).reshape(Bq, Lq, NHEAD, D_HEAD)
        k = (x @ Wk + bk).reshape(Bq, Lq, NHEAD, D_HEAD)
        v = (x @ Wv + bv).reshape(Bq, Lq, NHEAD, D_HEAD)
        q_phi = _phi(q)
        k_phi = _phi(k)
        kv = jnp.einsum('blhd,blhe->bhde', k_phi, v)
        k_sum = k_phi.sum(axis=1)
        z = 1.0 / (jnp.einsum('blhd,bhd->blh', q_phi, k_sum) + 1e-06)
        out = jnp.einsum('blhd,bhde,blh->blhe', q_phi, kv, z)
        out = out.reshape(Bq, Lq, D_MODEL) @ Wo + bo
        x = _layernorm(x + out, ln1_g, ln1_b)
        ff = jax.nn.relu(x @ W1 + b1) @ W2 + b2
        x = _layernorm(x + ff, ln2_g, ln2_b)
        return x

    def _L0_ffn_ref(x, W1, b1, Wg, bg, Wd, bd):
        import jax, jax.numpy as jnp
        import numpy as np
        C = 256
        HID = 1024
        E = 8
        TEMP = 1.0
        orig_shape = x.shape
        xf = x.reshape(-1, orig_shape[-1])
        H = jax.nn.gelu(xf @ W1 + b1, approximate=False)
        probs = jax.nn.softmax((H @ Wg + bg) / TEMP, axis=-1)
        assign = jnp.argmax(probs, axis=-1)
        out = jnp.zeros_like(xf)
        for e in range(Wd.shape[0]):
            y = H @ Wd[e] + bd[e]
            sel = (assign == e)[:, None]
            out = out + jnp.where(sel, probs[:, e:e + 1] * y, 0.0)
        return out.reshape(orig_shape)

    def _L1_gnn_ref(node_features, edge_index, edge_relations, query_emb, Wq, bq, Wk, bk, Wv, bv, rel_w, Wo, bo, gamma, beta):
        import jax, jax.numpy as jnp
        import numpy as np
        N_NODES = 50000
        N_EDGES = 15625
        IN_DIM = 256
        HID = 64
        HEADS = 4
        N_REL = 64
        N = node_features.shape[0]
        D = rel_w.shape[1]
        H = Wq.shape[1] // D
        enh = node_features + 0.1 * query_emb[None, :]
        Q = (enh @ Wq + bq).reshape(N, H, D)
        K = (enh @ Wk + bk).reshape(N, H, D)
        V = (enh @ Wv + bv).reshape(N, H, D)
        src, dst = (edge_index[0], edge_index[1])
        rel = rel_w[edge_relations]
        mod_k = K[src] + 0.2 * rel[:, None, :]
        scores = jnp.einsum('ehd,ehd->eh', Q[dst], mod_k) / D ** 0.5
        seg_max = jax.ops.segment_max(scores, dst, num_segments=N)
        ex = jnp.exp(scores - seg_max[dst])
        denom = jax.ops.segment_sum(ex, dst, num_segments=N)
        w = ex / denom[dst]
        agg = jax.ops.segment_sum(w[:, :, None] * V[src], dst, num_segments=N)
        deg = jax.ops.segment_sum(jnp.ones((src.shape[0],), jnp.float32), dst, num_segments=N)
        msgs = jnp.where(deg[:, None, None] > 0, agg, V)
        out = msgs.reshape(N, H * D) @ Wo + bo
        x = out + node_features
        mu = jnp.mean(x, axis=-1, keepdims=True)
        var = jnp.var(x, axis=-1, keepdims=True)
        return (x - mu) / jnp.sqrt(var + 1e-05) * gamma + beta

    def _L1_mix_ref(x, t, w_qkv, mem_kv, w_out, b_out, g_out, g_pre):
        import jax, jax.numpy as jnp
        import numpy as np
        DIM = 256
        HEADS = 4
        DIM_HEAD = 32
        NUM_MEM = 4
        HIDDEN = HEADS * DIM_HEAD
        SCALE = DIM_HEAD ** (-0.5)

        def rmsnorm(x, g):
            n = jnp.linalg.norm(x, axis=-1, keepdims=True)
            return x / jnp.maximum(n, 1e-12) * g * x.shape[-1] ** 0.5
        b, n, c = x.shape
        xn = rmsnorm(x, g_pre)
        qkv = xn @ w_qkv
        q, k, v = jnp.split(qkv, 3, axis=-1)

        def to_heads(z):
            return z.reshape(b, n, HEADS, DIM_HEAD).transpose(0, 2, 3, 1)
        q, k, v = map(to_heads, (q, k, v))
        mk = jnp.broadcast_to(mem_kv[0], (b, HEADS, DIM_HEAD, NUM_MEM))
        mv = jnp.broadcast_to(mem_kv[1], (b, HEADS, DIM_HEAD, NUM_MEM))
        k = jnp.concatenate([mk, k], axis=-1)
        v = jnp.concatenate([mv, v], axis=-1)
        q = jax.nn.softmax(q, axis=-2) * SCALE
        k = jax.nn.softmax(k, axis=-1)
        context = jnp.einsum('bhdn,bhen->bhde', k, v)
        out = jnp.einsum('bhde,bhdn->bhen', context, q)
        out = out.transpose(0, 3, 1, 2).reshape(b, n, HIDDEN)
        out = rmsnorm(out @ w_out + b_out, g_out)
        return out + x

    def _L1_ffn_ref(x, gamma, beta, Wr, br, W1, b1, W2, b2):
        import jax, jax.numpy as jnp
        import numpy as np
        E = 8
        K = 2
        D = 256
        H = 512
        DOUT = 256
        EPS = 1e-05
        mu = jnp.mean(x, axis=-1, keepdims=True)
        var = jnp.mean(jnp.square(x - mu), axis=-1, keepdims=True)
        xn = (x - mu) * jax.lax.rsqrt(var + EPS) * gamma + beta
        logits = jnp.einsum('bsd,de->bse', xn, Wr) + br
        top_vals, top_idx = jax.lax.top_k(logits, K)
        w = jax.nn.softmax(top_vals, axis=-1)
        w_full = jnp.einsum('bsk,bske->bse', w, jax.nn.one_hot(top_idx, E, dtype=w.dtype))
        y = jnp.zeros(x.shape[:-1] + (DOUT,), x.dtype)
        for e in range(E):
            h = jax.nn.gelu(jnp.einsum('bsd,dh->bsh', xn, W1[e]) + b1[e], approximate=False)
            y_e = jnp.einsum('bsh,hd->bsd', h, W2[e]) + b2[e]
            y = y + y_e * w_full[..., e, None]
        return y

    def _L2_gnn_ref(x, edge_index, W, b, a_src, a_trg):
        import jax, jax.numpy as jnp
        import numpy as np
        N = 50000
        E = 25000
        F_IN = 256
        K = 8
        F_OUT = 32
        NEG_SLOPE = 0.2
        n = x.shape[0]
        loops = jnp.arange(n, dtype=edge_index.dtype)
        src = jnp.concatenate([edge_index[0], loops])
        trg = jnp.concatenate([edge_index[1], loops])
        h_prime = (x @ W + b).reshape(n, K, F_OUT)
        h_src = jnp.sum(h_prime * a_src, axis=2)
        h_trg = jnp.sum(h_prime * a_trg, axis=2)
        e = h_src[src] + h_trg[trg]
        e = jax.nn.leaky_relu(e, negative_slope=NEG_SLOPE)
        e = e - jnp.max(e)
        exp_e = jnp.exp(e)
        denom = jax.ops.segment_sum(exp_e, trg, num_segments=n)
        alpha = exp_e / (denom[trg] + 1e-10)
        msg = h_prime[src] * alpha[:, :, None]
        out = jax.ops.segment_sum(msg, trg, num_segments=n)
        return out.reshape(n, K * F_OUT)

    def _L2_mix_ref(x, Wq, Wkv, Wproj, bproj):
        import jax, jax.numpy as jnp
        import numpy as np
        NUM_HEADS = 8
        B, N, C = x.shape
        h = NUM_HEADS
        d = C // h
        q = jnp.einsum('bnc,oc->bno', x, Wq).reshape(B, N, h, d).transpose(0, 2, 1, 3)
        kv = jnp.einsum('bnc,oc->bno', x, Wkv).reshape(B, N, 2, h, d)
        k = kv[:, :, 0].transpose(0, 2, 1, 3)
        v = kv[:, :, 1].transpose(0, 2, 1, 3)
        q = jax.nn.elu(q) + 1.0
        k = jax.nn.elu(k) + 1.0
        k_sum = k.sum(axis=2)
        D_inv = 1.0 / jnp.maximum(jnp.einsum('bhnd,bhd->bhn', q, k_sum), 1e-06)
        context = jnp.einsum('bhnd,bhne->bhde', k, v)
        attn = jnp.einsum('bhnd,bhde->bhne', q, context) * D_inv[..., None]
        out = attn.transpose(0, 2, 1, 3).reshape(B, N, C)
        out = jnp.einsum('bnc,oc->bno', out, Wproj) + bproj
        return out

    def _L2_ffn_ref(x, Wr, br, W1, b1, g1, be1, m1, v1, W2, b2, g2, be2, m2, v2, Wo, bo):
        import jax, jax.numpy as jnp
        import numpy as np
        BN_EPS = 0.001

        def _bn(h, g, b, m, v):
            return g * (h - m) * jax.lax.rsqrt(v + BN_EPS) + b
        feat = jnp.mean(x, axis=0)
        w = jax.nn.softmax(feat @ Wr + br, axis=-1)
        h = jnp.einsum('bfd,edh->bfeh', x, W1) + b1
        h = jax.nn.relu(_bn(h, g1, be1, m1, v1))
        h = jnp.einsum('bfeh,ehk->bfek', h, W2) + b2
        h = jax.nn.relu(_bn(h, g2, be2, m2, v2))
        y = jnp.einsum('bfeh,ehd->bfed', h, Wo) + bo
        return jnp.einsum('bfed,fe->bfd', y, w)

    def _L3_gnn_ref(x, weight, edge_val, edge_row, edge_col):
        import jax, jax.numpy as jnp
        import numpy as np
        N_NODES = 3125
        N_EDGES = 100000
        D_IN = 256
        D_OUT = 256
        support = x @ weight
        msgs = support[edge_col] * edge_val[:, None]
        out = jax.ops.segment_sum(msgs, edge_row, num_segments=N_NODES)
        return jax.nn.relu(out)

    def _L3_mix_ref(x, Wq, Wk, Wv, Wm, W1, W2, g1, b1, g2, b2):
        import jax, jax.numpy as jnp
        import numpy as np
        NHEAD = 8
        ATT_EPS = 1e-06
        LN_EPS = 1e-05

        def _layernorm(x, g, b):
            mu = jnp.mean(x, axis=-1, keepdims=True)
            var = jnp.mean(jnp.square(x - mu), axis=-1, keepdims=True)
            return (x - mu) * jax.lax.rsqrt(var + LN_EPS) * g + b
        N, L, C = x.shape
        H = NHEAD
        D = C // H
        q = (x @ Wq).reshape(N, L, H, D)
        k = (x @ Wk).reshape(N, L, H, D)
        v = (x @ Wv).reshape(N, L, H, D)
        Q = jax.nn.elu(q) + 1.0
        K = jax.nn.elu(k) + 1.0
        v = v / L
        KV = jnp.einsum('nshd,nshv->nhdv', K, v)
        Z = 1.0 / (jnp.einsum('nlhd,nhd->nlh', Q, K.sum(axis=1)) + ATT_EPS)
        msg = jnp.einsum('nlhd,nhdv,nlh->nlhv', Q, KV, Z) * L
        msg = msg.reshape(N, L, C) @ Wm
        msg = _layernorm(msg, g1, b1)
        h = jnp.concatenate([x, msg], axis=-1) @ W1
        h = jax.nn.relu(h) @ W2
        msg = _layernorm(h, g2, b2)
        return x + msg

    def _L3_ffn_ref(input_embeddings, router_w, w1, b1, w2, b2):
        import jax, jax.numpy as jnp
        import numpy as np
        NUM_EXPERTS = 8
        TOP_K = 2
        B, S, D = (8, 256, 256)

        def _moe(tokens, router_w, w1, b1, w2, b2):
            N = tokens.shape[0]
            E = router_w.shape[0]
            logits = tokens.astype(jnp.float32) @ router_w.astype(jnp.float32).T
            probs = jax.nn.softmax(logits, axis=-1)
            rw, re = jax.lax.top_k(probs, TOP_K)
            if TOP_K > 1:
                rw = rw / jnp.maximum(rw.sum(-1, keepdims=True), 1e-12)
            rw = rw.astype(tokens.dtype)
            combine = jnp.zeros((N, E), tokens.dtype).at[jnp.arange(N)[:, None], re].set(rw)
            out = tokens
            for e in range(E):
                h = jax.nn.gelu(tokens @ w1[e] + b1[e], approximate=False)
                y = h @ w2[e] + b2[e]
                out = out + combine[:, e:e + 1] * y
            return out
        b, s, d = input_embeddings.shape
        tokens = input_embeddings.reshape(b * s, d)
        return _moe(tokens, router_w, w1, b1, w2, b2).reshape(b, s, d)
    edge_index = jnp.stack([src, dst])
    xn = _layernorm(x, axis=-1)
    x = x + _L0_gnn_ref(xn, src, dst, edge_weight, L0_gnn_W, L0_gnn_b) + _L0_mix_ref(xn[None], L0_mix_Wq, L0_mix_bq, L0_mix_Wk, L0_mix_bk, L0_mix_Wv, L0_mix_bv, L0_mix_Wo, L0_mix_bo, L0_mix_W1, L0_mix_b1, L0_mix_W2, L0_mix_b2, L0_mix_ln1_g, L0_mix_ln1_b, L0_mix_ln2_g, L0_mix_ln2_b)[0]
    x = x + _L0_ffn_ref(_layernorm(x, axis=-1)[None], L0_ffn_W1, L0_ffn_b1, L0_ffn_Wg, L0_ffn_bg, L0_ffn_Wd, L0_ffn_bd)[0]
    xn = _layernorm(x, axis=-1)
    x = x + _L1_gnn_ref(xn, edge_index, edge_type_64, L1_gnn_query_emb, L1_gnn_Wq, L1_gnn_bq, L1_gnn_Wk, L1_gnn_bk, L1_gnn_Wv, L1_gnn_bv, L1_gnn_rel_w, L1_gnn_Wo, L1_gnn_bo, L1_gnn_gamma, L1_gnn_beta) + _L1_mix_ref(xn[None], L1_mix_t, L1_mix_w_qkv, L1_mix_mem_kv, L1_mix_w_out, L1_mix_b_out, L1_mix_g_out, L1_mix_g_pre)[0]
    x = x + _L1_ffn_ref(_layernorm(x, axis=-1)[None], L1_ffn_gamma, L1_ffn_beta, L1_ffn_Wr, L1_ffn_br, L1_ffn_W1, L1_ffn_b1, L1_ffn_W2, L1_ffn_b2)[0]
    xn = _layernorm(x, axis=-1)
    x = x + _L2_gnn_ref(xn, edge_index, L2_gnn_W, L2_gnn_b, L2_gnn_a_src, L2_gnn_a_trg) + _L2_mix_ref(xn[None], L2_mix_Wq, L2_mix_Wkv, L2_mix_Wproj, L2_mix_bproj)[0]
    x = x + _L2_ffn_ref(_layernorm(x, axis=-1)[None], L2_ffn_Wr, L2_ffn_br, L2_ffn_W1, L2_ffn_b1, L2_ffn_g1, L2_ffn_be1, L2_ffn_m1, L2_ffn_v1, L2_ffn_W2, L2_ffn_b2, L2_ffn_g2, L2_ffn_be2, L2_ffn_m2, L2_ffn_v2, L2_ffn_Wo, L2_ffn_bo)[0]
    xn = _layernorm(x, axis=-1)
    x = x + _L3_gnn_ref(xn, L3_gnn_weight, edge_weight, src, dst) + _L3_mix_ref(xn[None], L3_mix_Wq, L3_mix_Wk, L3_mix_Wv, L3_mix_Wm, L3_mix_W1, L3_mix_W2, L3_mix_g1, L3_mix_b1, L3_mix_g2, L3_mix_b2)[0]
    x = x + _L3_ffn_ref(_layernorm(x, axis=-1)[None], L3_ffn_router_w, L3_ffn_w1, L3_ffn_b1, L3_ffn_w2, L3_ffn_b2)[0]
    return x

_drawn_inputs = setup_inputs


def setup_inputs(seed=0):
    import zlib

    import numpy as np

    out = dict(_drawn_inputs(seed))
    spreads = {'L0_mix_bq': (0.0, 0.8),
     'L0_mix_bk': (0.0, 0.8),
     'L0_mix_bv': (0.0, 0.1),
     'L0_mix_bo': (0.0, 0.1),
     'L0_mix_b1': (0.0, 0.1),
     'L0_mix_b2': (0.0, 0.1),
     'L0_mix_ln1_g': (1.0, 0.2),
     'L0_mix_ln1_b': (0.0, 0.1),
     'L0_mix_ln2_g': (1.0, 0.2),
     'L0_mix_ln2_b': (0.0, 0.1),
     'L0_ffn_b1': (0.0, 0.8),
     'L0_ffn_bg': (0.0, 0.8),
     'L0_ffn_bd': (0.0, 0.8),
     'L1_gnn_bq': (0.0, 0.8),
     'L1_gnn_bk': (0.0, 2.0),
     'L1_gnn_bv': (0.0, 0.726),
     'L1_gnn_bo': (0.0, 0.457),
     'L1_gnn_gamma': (1.0, 0.2),
     'L1_gnn_beta': (0.0, 0.1),
     'L1_mix_b_out': (0.0, 0.1),
     'L1_mix_g_out': (1.0, 0.2),
     'L1_mix_g_pre': (1.0, 0.6),
     'L1_ffn_br': (0.0, 0.8),
     'L2_mix_bproj': (0.0, 0.8),
     'L2_ffn_br': (0.0, 0.8),
     'L2_ffn_b1': (0.0, 2.0),
     'L2_ffn_g1': (1.0, 0.6),
     'L2_ffn_be1': (0.0, 2.0),
     'L2_ffn_m1': (0.0, 2.0),
     'L2_ffn_v1': (1.0, 0.6),
     'L2_ffn_b2': (0.0, 2.0),
     'L2_ffn_g2': (1.0, 0.6),
     'L2_ffn_be2': (0.0, 2.0),
     'L2_ffn_m2': (0.0, 2.0),
     'L2_ffn_v2': (1.0, 0.6),
     'L2_ffn_bo': (0.0, 2.0),
     'L3_mix_g1': (1.0, 0.6),
     'L3_mix_b1': (0.0, 2.0),
     'L3_mix_g2': (1.0, 0.6),
     'L3_mix_b2': (0.0, 1.411),
     'L3_ffn_b1': (0.0, 2.0),
     'L3_ffn_b2': (0.0, 2.0)}
    factors = {'L0_mix_Wq': 8.0,
     'L0_mix_Wk': 8.0,
     'L0_mix_Wv': 4.602,
     'L0_ffn_W1': 6.061,
     'L0_ffn_Wg': 6.362,
     'L0_ffn_Wd': 7.116,
     'L1_gnn_query_emb': 8.0,
     'L1_gnn_Wq': 8.0,
     'L1_gnn_Wk': 8.0,
     'L1_gnn_Wv': 5.506,
     'L1_gnn_rel_w': 35.127,
     'L1_gnn_Wo': 4.23,
     'L1_mix_w_qkv': 5.848,
     'L1_mix_mem_kv': 8.0,
     'L1_mix_w_out': 7.038,
     'L1_ffn_gamma': 8.0,
     'L1_ffn_beta': 8.0,
     'L1_ffn_Wr': 5.177,
     'L1_ffn_W1': 4.639,
     'L1_ffn_b1': 36.261,
     'L1_ffn_W2': 4.418,
     'L1_ffn_b2': 51.601,
     'L2_gnn_a_trg': 200.0,
     'L2_mix_Wq': 200.0,
     'L2_mix_Wkv': 4.534,
     'L2_mix_Wproj': 4.788,
     'L3_mix_Wq': 200.0,
     'L3_mix_Wk': 200.0,
     'L2_gnn_b': 26.536,
     'L2_gnn_a_src': 64.0,
     'L2_gnn_W': 8.0}
    for name, (base, spread) in spreads.items():
        noise = np.random.default_rng([zlib.crc32(name.encode()), seed]).standard_normal(out[name].shape)
        drawn = base * np.exp(spread * noise) if base else spread * noise
        out[name] = jnp.asarray(drawn.astype(out[name].dtype))
    for name, factor in factors.items():
        out[name] = (out[name] * factor).astype(out[name].dtype)
    return out
```

```python
from contextlib import ExitStack

import concourse.bass as bass
from concourse import mybir

F32 = mybir.dt.float32
I32 = mybir.dt.int32
ALU = mybir.AluOpType
ACT = mybir.ActivationFunctionType
AX = mybir.AxisListType

N = 3125
D = 256
P = 125
NT = N // P
NE = 53125
ET = NE // P
DC = D // 128
BODY = 5
NODE_LOOPS = NT // BODY
EDGE_LOOPS = ET // BODY
RUNS = [(0, 3), (3, 2)]
RUNMAX = 3 * P
TABLES = 5
PARTS = 3
LN_EPS = 1e-5
BANK = 512


class Done:

    def __init__(self, sem, per_body):
        self.sem, self.per_body = sem, per_body

    def open(self, eng):
        eng.sem_inc(self.sem, self.per_body)

    def at(self, step, index):
        return (step + 1) * self.per_body + (index + 1)


class Chain:

    def __init__(self, eng, sem, per_body=0, step=None, base=0):
        self.eng, self.sem, self.per_body, self.step, self.base, self.n = eng, sem, per_body, step, base, 0

    def __call__(self, ins):
        ins.then_inc(self.sem, 1)
        self.n += 1

    def settle(self):
        value = self.base + self.n
        if self.step is not None:
            value = self.step * self.per_body + value
        self.eng.wait_ge(self.sem, value)

    def link(self, ins):
        self(ins)
        self.settle()


class Phase:

    def __init__(self, nc, name):
        self.nc, self.name, self.stack = nc, name, ExitStack()

    def __enter__(self):
        self.stack.__enter__()
        self.sems = []
        self.stack.callback(self.release)
        self.spent = self.sem("spent")
        return self

    def release(self):
        self.nc.clear_and_free_semaphores(self.sems)
        self.nc.all_engine_barrier()

    def __exit__(self, *a):
        return self.stack.__exit__(*a)

    def sb(self, name, shape, dtype=F32):
        return self.stack.enter_context(self.nc.sbuf_tensor(f"{self.name}_{name}", shape, dtype))

    def ps(self, name):
        return self.stack.enter_context(self.nc.psum_tensor(f"{self.name}_{name}", [128, BANK], F32))

    def sem(self, name):
        self.sems.append(self.nc.alloc_semaphore(name=f"{self.name}_{name}"))
        return self.sems[-1]

    def done(self, name, per_body):
        return Done(self.sem(name), per_body)

    def block(self):
        return self.stack.enter_context(self.nc.Block())

    def hold(self, eng, done, step, index):
        eng.wait_ge(done.sem, done.at(step, index))
        eng.sem_inc(self.spent, 1)

    def hold_dma(self, eng, sem, step):
        eng.wait_ge(sem, step * 16 + 16)
        eng.sem_inc(self.spent, 1)


def slot_owner(slots, per_body, index):
    if index >= slots:
        return index - slots
    return max(i for i in range(per_body) if i % slots == index % slots) - per_body


def bcast_mid(ap, shape):
    return ap.unsqueeze(1).to_broadcast(shape)


def bcast_last(ap, shape):
    return ap.unsqueeze(len(shape) - 1).to_broadcast(shape)


def columns(tile, count=1):
    return bass.ds(tile * P, count * P)


def feature_rows(w):
    return w.rearrange("(c p) n -> p c n", p=128)


def feature_column(v):
    return v


class Core:

    def __init__(self, nc, a, stack):
        self.nc, self.a = nc, a

        def sb(name, shape, dtype=F32):
            return stack.enter_context(nc.sbuf_tensor(name, shape, dtype))

        self.x = sb("x", [P, NT, D])
        self.xn = sb("xn", [P, NT, D])
        self.xnT = sb("xnT", [128, DC, N])
        self.ident = sb("ident", [128, 128])
        self.heads = sb("heads", [128, 128])
        self.iota8 = sb("iota8", [P, 8])
        self.zero = sb("zero", [P, 264])
        self.src = sb("src", [P, ET], I32)
        self.dst = sb("dst", [P, ET], I32)
        self.srcf = sb("srcf", [P, ET])
        self.dstf = sb("dstf", [P, ET])
        self.src_once = sb("src_once", [P, ET], I32)
        self.dst_once = sb("dst_once", [P, ET], I32)
        self.weight = sb("weight", [P, ET])

    def table(self, name, rows, width):
        return self.nc.dram_tensor(name, (rows, width), F32, kind="Internal").ap()


def nodes(ap):
    return ap.rearrange("(p t) d -> p t d", t=NT)


def load_all(core):
    nc, a = core.nc, core.a
    with Phase(nc, "load") as ph:
        loaded, zeroed, converted = ph.sem("loaded"), ph.sem("zeroed"), ph.sem("converted")
        block = ph.block()

        @block.sync
        def _(sp):
            sp.dma_start(core.x[:], nodes(a["x"])).then_inc(loaded, 16)
            for buf, name in ((core.src, "src"), (core.dst, "dst"), (core.weight, "edge_weight"), (core.ident, "c_ident"),
                              (core.heads, "c_heads"), (core.iota8, "c_iota8")):
                sp.dma_start(buf[:], a[name]).then_inc(loaded, 16)
            sp.wait_ge(loaded, 16 * 7)

        @block.vector
        def _(v):
            nc.vector.memset(core.zero[:], 0.0).then_inc(zeroed, 1)
            v.wait_ge(loaded, 16 * 7)
            nc.vector.tensor_copy(core.srcf[:], core.src[:]).then_inc(converted, 1)
            nc.vector.tensor_copy(core.dstf[:], core.dst[:]).then_inc(converted, 1)


class Marks:

    LINKS = BODY + 4

    def __init__(self, core, ph, keyf, once):
        self.core, self.ph, self.keyf, self.once = core, ph, keyf, once
        self.earlier, self.spare = ph.sb("earlier", [P, P]), ph.sb("spare", [P, 1])
        self.before = ph.sb("before", [P, BODY, P])
        self.count, self.shift = ph.sb("count", [P, BODY]), ph.sb("shift", [P, BODY])
        self.const, self.marked = ph.sem("mark_const"), ph.done("marked", 1)

    def load(self, sp):
        sp.dma_start(self.earlier[:], self.core.a["c_earlier"]).then_inc(self.const, 16)
        sp.dma_start(self.spare[:], self.core.a["c_spare"]).then_inc(self.const, 16)
        sp.wait_ge(self.const, 32)

    def compare(self, chain, keys, o, k):
        chain(self.core.nc.vector.scalar_tensor_tensor(self.before[:, k, :], keys, self.keyf[:, bass.ds(o * BODY + k, 1)], self.earlier[:],
                                                       ALU.is_equal, ALU.mult))

    def finish(self, v, chain, o):
        nc = self.core.nc
        mine = bass.ds(o * BODY, BODY)

        def link(ins):
            chain.link(ins)
            v.sem_inc(self.ph.spent, 1)

        chain.settle()
        v.sem_inc(self.ph.spent, 1)
        link(nc.vector.tensor_reduce(self.count[:], self.before[:], AX.X, ALU.add))
        chain(nc.vector.tensor_scalar(self.count[:], self.count[:], 0.0, None, ALU.is_gt))
        link(nc.vector.tensor_scalar(self.shift[:], self.keyf[:, mine], self.spare[:, 0:1], -1.0, ALU.subtract, ALU.mult))
        link(nc.vector.tensor_tensor(self.shift[:], self.shift[:], self.count[:], ALU.mult))
        nc.vector.tensor_tensor(self.once[:, mine], self.keyf[:, mine], self.shift[:], ALU.add).then_inc(self.marked.sem, 1)


def whole_norm(v, nc, chain, buf, centred, square, stat, gamma=None, beta=None, act=None):
    mean, var, rstd, half = (stat[:, i, :] for i in range(4))
    shape = [P, NT, D]
    chain.link(nc.vector.tensor_reduce(mean, buf[:], AX.X, ALU.add))
    chain.link(nc.vector.tensor_scalar(mean, mean, 1.0 / D, None, ALU.mult))
    chain.link(nc.vector.tensor_tensor(centred[:], buf[:], bcast_last(mean, shape), ALU.subtract))
    chain.link(nc.vector.tensor_tensor(square[:], centred[:], centred[:], ALU.mult))
    chain.link(nc.vector.tensor_reduce(var, square[:], AX.X, ALU.add))
    chain.link(nc.vector.tensor_scalar(var, var, 1.0 / D, LN_EPS, ALU.mult, ALU.add))
    chain.link(nc.vector.reciprocal(half, var))
    act(half, rstd)
    chain.link(nc.vector.tensor_tensor(half, rstd, rstd, ALU.mult))
    chain.link(nc.vector.tensor_tensor(half, half, var, ALU.mult))
    chain.link(nc.vector.tensor_scalar(half, half, -0.5, 1.5, ALU.mult, ALU.add))
    chain.link(nc.vector.tensor_tensor(rstd, rstd, half, ALU.mult))
    chain.link(nc.vector.tensor_tensor(centred[:], centred[:], bcast_last(rstd, shape), ALU.mult))
    if gamma is not None:
        chain.link(nc.vector.tensor_tensor(centred[:], centred[:], bcast_mid(gamma[:], shape), ALU.mult))
        chain.link(nc.vector.tensor_tensor(centred[:], centred[:], bcast_mid(beta[:], shape), ALU.add))


def layer_norm(core, name, buf, out, outT=None, token_affine=None, feature_affine=None, add_to_x=False, add_xn=False):
    nc, a = core.nc, core.a
    with Phase(nc, name) as ph:
        square = ph.sb("square", [P, NT, D])
        stat = ph.sb("stat", [P, 4, NT])
        tile = ph.sb("tile", [P, BODY, D])
        gamma = beta = gcol = bcol = None
        loads = []
        if token_affine:
            gamma, beta = ph.sb("gamma", [P, D]), ph.sb("beta", [P, D])
            loads = [(gamma, a[token_affine[0]].partition_broadcast(P)), (beta, a[token_affine[1]].partition_broadcast(P))]
        if feature_affine:
            gcol, bcol = ph.sb("gcol", [128, DC]), ph.sb("bcol", [128, DC])
            loads = [(gcol, a[feature_affine[0]]), (bcol, a[feature_affine[1]])]
        loaded, chain_sem = ph.sem("loaded"), ph.sem("chain")
        inverse_ready, root_ready, normed = ph.sem("inverse_ready"), ph.sem("root_ready"), ph.sem("normed")
        staged, turned, stored = ph.done("staged", BODY), ph.done("turned", BODY), ph.done("stored", BODY)
        banks = [ph.ps(f"bank{k}") for k in range(BODY)] if outT is not None else []
        block = ph.block()

        @block.sync
        def _(sp):
            for to, what in loads:
                sp.dma_start(to[:], what).then_inc(loaded, 16)
            if loads:
                sp.wait_ge(loaded, 16 * len(loads))

        @block.vector
        def _(v):
            chain = Chain(v, chain_sem)

            def root(inverse, rstd):
                nc.vector.tensor_copy(rstd, inverse).then_inc(inverse_ready, 1)
                v.wait_ge(root_ready, 1)

            if loads:
                v.wait_ge(loaded, 16 * len(loads))
            whole_norm(v, nc, chain, buf, out, square, stat, gamma, beta, root)
            if add_xn:
                chain.link(nc.vector.tensor_tensor(out[:], out[:], core.xn[:], ALU.add))
            if add_to_x:
                chain.link(nc.vector.tensor_tensor(core.x[:], core.x[:], out[:], ALU.add))
            nc.vector.tensor_copy(stat[:, 3, :], stat[:, 0, :]).then_inc(normed, 1)

        @block.scalar
        def _(act):
            act.wait_ge(inverse_ready, 1)
            nc.scalar.activation(stat[:, 2, :], stat[:, 3, :], ACT.Sqrt).then_inc(root_ready, 1)
            if outT is None:
                return
            stored.open(act)
            if loads:
                act.wait_ge(loaded, 16 * len(loads))
            with act.Fori(0, NODE_LOOPS) as o:
                for k in range(BODY):
                    ph.hold(act, turned, o, k)
                    there = outT[:, :, columns(o * BODY + k)]
                    if feature_affine:
                        for c in range(DC):
                            ins = nc.scalar.activation(there[:, c, :], banks[k][:, c * P:(c + 1) * P], ACT.Identity,
                                                       scale=gcol[:, c:c + 1], bias=bcol[:, c:c + 1])
                    else:
                        ins = nc.scalar.activation(there, banks[k][:, 0:DC * P].rearrange("p (c n) -> p c n", c=DC), ACT.Copy)
                    ins.then_inc(stored.sem, 1)

        if outT is None:
            return

        @block.gpsimd
        def _(pool):
            staged.open(pool)
            pool.wait_ge(normed, 1)
            with pool.Fori(0, NODE_LOOPS) as o:
                for k in range(BODY):
                    ph.hold(pool, turned, o, k - BODY)
                    nc.gpsimd.tensor_copy(tile[:, k:k + 1, :], out[:, bass.ds(o * BODY + k, 1), :]).then_inc(staged.sem, 1)

        @block.tensor
        def _(pe):
            turned.open(pe)
            with pe.Fori(0, NODE_LOOPS) as o:
                for k in range(BODY):
                    ph.hold(pe, staged, o, k)
                    ph.hold(pe, stored, o, k - BODY)
                    for c in range(DC):
                        ins = nc.tensor.transpose(banks[k][:, c * P:(c + 1) * P], tile[:, k, c * 128:(c + 1) * 128], core.ident[0:P, 0:P])
                    ins.then_inc(turned.sem, 1)


def project(core, name, inT, weights, dest, width, bias=None, table=None, feature_scale=None, row_scale=None):
    nc, a = core.nc, core.a
    with Phase(nc, name) as ph:
        w = ph.sb("w", [128, DC, width])
        tile = ph.sb("tile", [128, BODY, DC, P])
        b = ph.sb("b", [P, width]) if bias else None
        fs = ph.sb("fs", [128, DC]) if feature_scale else None
        loaded, saved, scaled = ph.sem("loaded"), ph.sem("saved"), ph.sem("scaled")
        staged, product, kept = ph.done("staged", BODY), ph.done("product", BODY), ph.done("kept", BODY)
        banks = [ph.ps(f"bank{k}") for k in range(BODY)]
        nload = len(weights) + (len(bias) if bias else 0) + (1 if feature_scale else 0)
        block = ph.block()

        @block.sync
        def _(sp):
            at = 0
            for wname, n in weights:
                sp.dma_start(w[:, :, at:at + n], feature_rows(a[wname])).then_inc(loaded, 16)
                at += n
            at = 0
            for bname, n in bias or []:
                sp.dma_start(b[:, at:at + n], a[bname].partition_broadcast(P)).then_inc(loaded, 16)
                at += n
            if feature_scale:
                sp.dma_start(fs[:], a[feature_scale]).then_inc(loaded, 16)
            sp.wait_ge(loaded, 16 * nload)
            if table is not None:
                sp.wait_ge(kept.sem, kept.at(NODE_LOOPS - 1, BODY - 1))
                sp.dma_start(nodes(table), dest[:]).then_inc(saved, 16)
                sp.wait_ge(saved, 16)

        @block.gpsimd
        def _(pool):
            staged.open(pool)
            with pool.Fori(0, NODE_LOOPS) as o:
                for k in range(BODY):
                    ph.hold(pool, product, o, k - BODY)
                    nc.gpsimd.tensor_copy(tile[:, k, :, :], inT[:, :, columns(o * BODY + k)]).then_inc(staged.sem, 1)

        @block.tensor
        def _(pe):
            product.open(pe)
            pe.wait_ge(loaded, 16 * nload)
            if feature_scale:
                pe.wait_ge(scaled, DC)
            with pe.Fori(0, NODE_LOOPS) as o:
                for k in range(BODY):
                    ph.hold(pe, staged, o, k)
                    ph.hold(pe, kept, o, k - BODY)
                    for c in range(DC):
                        ins = nc.tensor.matmul(banks[k][0:P, 0:width], tile[:, k, c, :], w[:, c, :], start=c == 0, stop=c == DC - 1)
                    ins.then_inc(product.sem, 1)

        if row_scale is not None:
            @block.vector
            def _(v):
                kept.open(v)
                v.wait_ge(loaded, 16 * nload)
                for c in range(DC):
                    nc.vector.tensor_scalar(w[:, c, :], w[:, c, :], fs[:, c:c + 1], None, ALU.mult).then_inc(scaled, 1)
                with v.Fori(0, NODE_LOOPS) as o:
                    for k in range(BODY):
                        ph.hold(v, product, o, k)
                        nc.vector.tensor_scalar(dest[:, bass.ds(o * BODY + k, 1), :], banks[k][0:P, 0:width].unsqueeze(1),
                                                row_scale[:, bass.ds(o * BODY + k, 1)], None, ALU.mult).then_inc(kept.sem, 1)
        elif bias:
            @block.vector
            def _(v):
                kept.open(v)
                v.wait_ge(loaded, 16 * nload)
                with v.Fori(0, NODE_LOOPS) as o:
                    for k in range(BODY):
                        ph.hold(v, product, o, k)
                        nc.vector.tensor_tensor(dest[:, bass.ds(o * BODY + k, 1), :], banks[k][0:P, 0:width].unsqueeze(1),
                                                b[:].unsqueeze(1), ALU.add).then_inc(kept.sem, 1)
        else:
            @block.scalar
            def _(act):
                kept.open(act)
                with act.Fori(0, NODE_LOOPS) as o:
                    for k in range(BODY):
                        ph.hold(act, product, o, k)
                        nc.scalar.activation(dest[:, bass.ds(o * BODY + k, 1), :], banks[k][0:P, 0:width].unsqueeze(1),
                                             ACT.Copy).then_inc(kept.sem, 1)


def clear_tables(core, name, tables):
    nc = core.nc
    with Phase(nc, name) as ph:
        cleared = ph.sem("cleared")
        block = ph.block()

        @block.sync
        def _(sp):
            for t in tables:
                width = t.shape[1]
                sp.dma_start(t.rearrange("(p t) d -> p t d", p=P),
                             core.zero[:, 0:width].unsqueeze(1).to_broadcast([P, NT + 1, width])).then_inc(cleared, 16)
            sp.wait_ge(cleared, 16 * len(tables))


def spread(core, name, table, gather_index, key_rows, keyf, once, tables, weight=None, alpha=None, heads=0, mark=False):
    nc, a = core.nc, core.a
    width = D + heads
    with Phase(nc, name) as ph:
        gather_at = ph.sb("gather_at", [P, BODY], I32)
        scatter_at = ph.sb("scatter_at", [P, BODY], I32)
        rows = ph.sb("rows", [P, BODY, D])
        keys = ph.sb("keys", [P, BODY, P], I32)
        same = ph.sb("same", [P, BODY, P])
        message = ph.sb("message", [P, BODY, width]) if heads else rows
        total = ph.sb("total", [P, BODY, width])
        gathered = [ph.sem(f"gathered{k}") for k in range(BODY)]
        keys_in = [ph.sem(f"keys_in{k}") for k in range(BODY)]
        scattered = [ph.sem(f"scattered{k}") for k in range(BODY)]
        gather_set, scatter_set = ph.done("gather_set", BODY), ph.done("scatter_set", BODY)
        compared, scaled = ph.done("compared", BODY), ph.done("scaled", BODY)
        summed, total_set = ph.done("summed", BODY), ph.done("total_set", BODY)
        banks = [ph.ps(f"bank{k}") for k in range(BODY)]
        marks = Marks(core, ph, keyf, once) if mark else None
        chain_sem = ph.sem("chain")
        gathers = gather_index is not None
        last = EDGE_LOOPS - 1
        table_of = [k % TABLES for k in range(BODY)]
        block = ph.block()

        @block.sync
        def _(sp):
            if mark:
                marks.load(sp)
            with sp.Fori(0, EDGE_LOOPS) as o:
                for k in range(BODY):
                    ph.hold(sp, compared, o, k - BODY)
                    sp.dma_start(keys[:, k, :], key_rows[bass.ds((o * BODY + k) * P, P)].partition_broadcast(P)).then_inc(keys_in[k], 16)
                    if not gathers:
                        ph.hold(sp, scaled if heads else summed, o, k - BODY)
                        sp.dma_start(rows[:, k, :], table[bass.ds((o * BODY + k) * P, P), :]).then_inc(gathered[k], 16)

        @block.gpsimd
        def _(pool):
            def gather(k):
                nc.gpsimd.indirect_dma_start(rows[:, k, :], None, table, bass.IndirectOffsetOnAxis(ap=gather_at[:, k:k + 1], axis=0)).then_inc(gathered[k], 16)

            def scatter(o, k):
                ph.hold(pool, scatter_set, o, k)
                ph.hold(pool, total_set, o, k)
                before = max((j for j in range(k) if table_of[j] == table_of[k]), default=None)
                if before is not None:
                    ph.hold_dma(pool, scattered[before], o)
                elif not (isinstance(o, int) and o == 0):
                    ph.hold_dma(pool, scattered[max(j for j in range(BODY) if table_of[j] == table_of[k])], o - 1)
                nc.gpsimd.indirect_dma_start(tables[table_of[k]], bass.IndirectOffsetOnAxis(ap=scatter_at[:, k:k + 1], axis=0),
                                             total[:, k, :], None, compute_op=ALU.add).then_inc(scattered[k], 16)

            def next_gather(o, k):
                ph.hold(pool, gather_set, o + 1, k)
                ph.hold(pool, scaled if heads else summed, o, k)
                gather(k)

            if gathers:
                for k in range(BODY):
                    ph.hold(pool, gather_set, 0, k)
                    gather(k)
            for k in range(BODY):
                scatter(0, k)
                if gathers:
                    next_gather(0, k)
            with pool.Fori(1, last) as o:
                for k in range(BODY):
                    scatter(o, k)
                    if gathers:
                        next_gather(o, k)
            for k in range(BODY):
                scatter(last, k)
            for k in range(BODY):
                pool.wait_ge(scattered[k], 16 * EDGE_LOOPS)

        @block.vector
        def _(v):
            compared.open(v)
            if heads:
                scaled.open(v)
            if mark:
                marks.marked.open(v)
                v.wait_ge(marks.const, 32)
            with v.Fori(0, EDGE_LOOPS) as o:
                chain = Chain(v, chain_sem, Marks.LINKS, o)
                for k in range(BODY):
                    one = bass.ds(o * BODY + k, 1)
                    ph.hold_dma(v, keys_in[k], o)
                    if mark:
                        marks.compare(chain, keys[:, k, :], o, k)
                    ph.hold(v, summed, o, k - BODY)
                    if heads:
                        nc.vector.tensor_scalar(same[:, k, :], keys[:, k, :], keyf[:, one], None, ALU.is_equal).then_inc(compared.sem, 1)
                        ph.hold_dma(v, gathered[k], o)
                        nc.vector.tensor_copy(message[:, k:k + 1, D:width], alpha[:, one, :])
                        nc.vector.tensor_tensor(message[:, k, 0:D].rearrange("p (h d) -> p h d", h=heads), rows[:, k, :].rearrange("p (h d) -> p h d", h=heads),
                                                alpha[:, one, :].rearrange("p o h -> p (o h)").unsqueeze(2).to_broadcast([P, heads, D // heads]), ALU.mult).then_inc(scaled.sem, 1)
                    else:
                        nc.vector.tensor_scalar(same[:, k, :], keys[:, k, :], keyf[:, one], weight[:, one], ALU.is_equal, ALU.mult).then_inc(compared.sem, 1)
                if mark:
                    marks.finish(v, chain, o)
                    assert chain.n == Marks.LINKS

        @block.tensor
        def _(pe):
            summed.open(pe)
            with pe.Fori(0, EDGE_LOOPS) as o:
                for k in range(BODY):
                    ph.hold(pe, compared, o, k)
                    if heads:
                        ph.hold(pe, scaled, o, k)
                    else:
                        ph.hold_dma(pe, gathered[k], o)
                    ph.hold(pe, total_set, o, k - BODY)
                    nc.tensor.matmul(banks[k][0:P, 0:width], same[:, k, :], message[:, k, :], start=True, stop=True).then_inc(summed.sem, 1)

        @block.scalar
        def _(act):
            gather_set.open(act)
            scatter_set.open(act)
            total_set.open(act)

            def set_gather(o, k):
                nc.scalar.activation(gather_at[:, k:k + 1], gather_index[:, bass.ds(o * BODY + k, 1)], ACT.Copy).then_inc(gather_set.sem, 1)

            def finish(o, k):
                if not (isinstance(o, int) and o == 0):
                    ph.hold_dma(act, scattered[k], o - 1)
                if mark and k == 0:
                    ph.hold(act, marks.marked, o, 0)
                nc.scalar.activation(scatter_at[:, k:k + 1], once[:, bass.ds(o * BODY + k, 1)], ACT.Copy).then_inc(scatter_set.sem, 1)
                ph.hold(act, summed, o, k)
                nc.scalar.activation(total[:, k, :], banks[k][0:P, 0:width], ACT.Copy).then_inc(total_set.sem, 1)

            if gathers:
                for k in range(BODY):
                    set_gather(0, k)
            for k in range(BODY):
                finish(0, k)
                if gathers:
                    set_gather(1, k)
            with act.Fori(1, last) as o:
                for k in range(BODY):
                    finish(o, k)
                    if gathers:
                        set_gather(o + 1, k)
            for k in range(BODY):
                finish(last, k)


class TableSum:

    def __init__(self, ph, tables, width):
        self.tables = tables
        self.parts = [ph.sb(f"part{i}", [P, NT, width]) for i in range(PARTS)]
        self.part_in = [ph.sem(f"part_in{i}") for i in range(PARTS)]
        self.added = ph.sem("added")
        self.total = self.parts[0]

    def slot(self, i):
        return 0 if i == 0 else 1 + (i - 1) % (PARTS - 1)

    def load(self, sp):
        for i, t in enumerate(self.tables):
            if i >= PARTS:
                sp.wait_ge(self.added, i - (PARTS - 1))
            sp.dma_start(self.parts[self.slot(i)][:], nodes(t[0:N, :])).then_inc(self.part_in[self.slot(i)], 16)

    def add(self, v, nc):
        v.wait_ge(self.part_in[0], 16)
        for i in range(1, len(self.tables)):
            v.wait_ge(self.part_in[self.slot(i)], 16 * (1 + (i - 1) // (PARTS - 1)))
            nc.vector.tensor_tensor(self.total[:], self.total[:], self.parts[self.slot(i)][:], ALU.add).then_inc(self.added, 1)
            v.wait_ge(self.added, i)


def finish_plain(core, name, tables, elu):
    nc = core.nc
    with Phase(nc, name) as ph:
        table_sum = TableSum(ph, tables, D)
        parts = table_sum.parts
        low_ready, grown, chain_sem = ph.sem("low_ready"), ph.sem("grown"), ph.sem("chain")
        block = ph.block()

        @block.sync
        def _(sp):
            table_sum.load(sp)

        @block.vector
        def _(v):
            chain = Chain(v, chain_sem)
            table_sum.add(v, nc)
            if elu:
                nc.vector.tensor_scalar(parts[1][:], parts[0][:], 0.0, None, ALU.min).then_inc(low_ready, 1)
                chain.link(nc.vector.scalar_tensor_tensor(core.x[:], parts[0][:], 0.0, core.x[:], ALU.max, ALU.add))
                v.wait_ge(grown, 1)
                chain.link(nc.vector.scalar_tensor_tensor(core.x[:], parts[1][:], -1.0, core.x[:], ALU.add, ALU.add))
            else:
                chain.link(nc.vector.scalar_tensor_tensor(core.x[:], parts[0][:], 0.0, core.x[:], ALU.max, ALU.add))

        if elu:
            @block.scalar
            def _(act):
                act.wait_ge(low_ready, 1)
                nc.scalar.activation(parts[1][:], parts[1][:], ACT.Exp).then_inc(grown, 1)


def gnn0(core):
    h = core.table("h0", N, D)
    tables = [core.table(f"sum0_{i}", N + P, D) for i in range(TABLES)]
    clear_tables(core, "clear0", tables)
    with Phase(core.nc, "g0") as ph:
        dest = ph.sb("h", [P, NT, D])
        project(core, "proj0", core.xnT, [("L0_gnn_W", D)], dest, D, bias=[("L0_gnn_b", D)], table=h)
    spread(core, "spread0", h, core.dst, core.a["src_rows"], core.srcf, core.src_once, tables, weight=core.weight, mark=True)
    finish_plain(core, "fin0", tables, elu=True)


def linear_attention(core, name, wq, wkv, wo, target, bias=None, clamp=None, plus=None, length=1.0, add=True):
    nc, a = core.nc, core.a
    KV = 2 * D
    with Phase(nc, name) as outer:
        context = outer.sb("context", [128, DC, 128])
        keysum = outer.sb("keysum", [128, DC, 128])
        with Phase(nc, name + "_kv") as ph:
            w = ph.sb("w", [128, DC, KV])
            b = ph.sb("b", [P, KV]) if bias else None
            tile = ph.sb("tile", [128, BODY, DC, P])
            kv = ph.sb("kv", [P, BODY, KV + 1])
            low = ph.sb("low", [P, BODY, D])
            grown = ph.sb("grown", [P, BODY, D])
            keymap = ph.sb("keymap", [P, BODY, D])
            loaded, ones, closed = ph.sem("loaded"), ph.sem("ones"), ph.sem("closed")
            staged, product, kept = ph.done("staged", BODY), ph.done("product", BODY), ph.done("kept", BODY)
            low_set, grown_set, mapped, added = ph.done("low_set", BODY), ph.done("grown_set", BODY), ph.done("mapped", BODY), ph.done("added", BODY)
            banks = [ph.ps(f"bank{k}") for k in range(BODY)]
            sums = [ph.ps(f"sums{c}") for c in range(DC)]
            nload = len(wkv) + (2 if bias else 0)
            block = ph.block()

            @block.sync
            def _(sp):
                for i, (wname, cols) in enumerate(wkv):
                    n = KV // len(wkv)
                    sp.dma_start(w[:, :, i * n:(i + 1) * n], feature_rows(a[wname] if cols is None else a[wname][:, cols])).then_inc(loaded, 16)
                if bias:
                    for i in range(2):
                        sp.dma_start(b[:, i * D:(i + 1) * D], a[bias[1 + i]].partition_broadcast(P)).then_inc(loaded, 16)
                sp.wait_ge(loaded, 16 * nload)

            @block.gpsimd
            def _(pool):
                staged.open(pool)
                nc.gpsimd.memset(kv[:, :, KV:KV + 1], 1.0).then_inc(ones, 1)
                with pool.Fori(0, NODE_LOOPS) as o:
                    for k in range(BODY):
                        ph.hold(pool, product, o, k - BODY)
                        nc.gpsimd.tensor_copy(tile[:, k, :, :], core.xnT[:, :, columns(o * BODY + k)]).then_inc(staged.sem, 1)

            @block.tensor
            def _(pe):
                product.open(pe)
                added.open(pe)
                pe.wait_ge(loaded, 16 * nload)
                for c in range(DC):
                    nc.tensor.matmul(sums[c][:, 0:D + 1], core.zero[:, 0:128], core.zero[:, 0:D + 1], start=True, stop=False, skip_group_check=True)
                pe.wait_ge(ones, 1)
                with pe.Fori(0, NODE_LOOPS) as o:
                    for k in range(BODY):
                        ph.hold(pe, staged, o, k)
                        ph.hold(pe, kept, o, k - BODY)
                        for c in range(DC):
                            ins = nc.tensor.matmul(banks[k][0:P, :], tile[:, k, c, :], w[:, c, :], start=c == 0, stop=c == DC - 1)
                        ins.then_inc(product.sem, 1)
                    for k in range(BODY):
                        ph.hold(pe, mapped, o, k)
                        for c in range(DC):
                            ins = nc.tensor.matmul(sums[c][:, 0:D + 1], keymap[:, k, c * 128:(c + 1) * 128], kv[:, k, D:KV + 1],
                                                   start=False, stop=False, skip_group_check=True)
                        ins.then_inc(added.sem, 1)
                for c in range(DC):
                    ins = nc.tensor.matmul(sums[c][:, 0:D + 1], core.zero[:, 0:128], core.zero[:, 0:D + 1], start=False, stop=True, skip_group_check=True)
                ins.then_inc(closed, 1)

            @block.vector
            def _(v):
                kept.open(v)
                low_set.open(v)
                mapped.open(v)
                v.wait_ge(loaded, 16 * nload)
                with v.Fori(0, NODE_LOOPS) as o:
                    for k in range(BODY):
                        ph.hold(v, product, o, k)
                        ph.hold(v, added, o, k - BODY)
                        if bias:
                            nc.vector.tensor_tensor(kv[:, k, 0:KV], banks[k][0:P, :], b[:], ALU.add).then_inc(kept.sem, 1)
                        else:
                            nc.vector.tensor_copy(kv[:, k, 0:KV], banks[k][0:P, :]).then_inc(kept.sem, 1)
                        ph.hold(v, kept, o, k)
                        nc.vector.tensor_scalar(low[:, k, :], kv[:, k, 0:D], 0.0, None, ALU.min).then_inc(low_set.sem, 1)
                    for k in range(BODY):
                        ph.hold(v, grown_set, o, k)
                        nc.vector.scalar_tensor_tensor(keymap[:, k, :], kv[:, k, 0:D], 0.0, grown[:, k, :], ALU.max, ALU.add).then_inc(mapped.sem, 1)
                v.wait_ge(closed, 1)
                for c in range(DC):
                    nc.vector.scalar_tensor_tensor(context[:, c, :], sums[c][:, c * 128:(c + 1) * 128], 1.0 / length, core.heads[:], ALU.mult, ALU.mult)
                    nc.vector.tensor_scalar(keysum[:, c, :], core.heads[:], sums[c][:, D:D + 1], None, ALU.mult)

            @block.scalar
            def _(act):
                grown_set.open(act)
                with act.Fori(0, NODE_LOOPS) as o:
                    for k in range(BODY):
                        ph.hold(act, low_set, o, k)
                        ph.hold(act, mapped, o, k - BODY)
                        nc.scalar.activation(grown[:, k, :], low[:, k, :], ACT.Exp).then_inc(grown_set.sem, 1)

        with Phase(nc, name + "_read") as ph:
            w = ph.sb("w", [128, DC, D])
            wout = ph.sb("wout", [128, DC, D])
            bq = ph.sb("bq", [128, DC])
            low = ph.sb("low", [128, 2, DC, RUNMAX])
            pos = ph.sb("pos", [128, 2, DC, RUNMAX])
            grown = ph.sb("grown", [128, 2, DC, RUNMAX])
            query = ph.sb("query", [128, 2, DC, RUNMAX])
            inverse = ph.sb("inverse", [128, 2, RUNMAX])
            outT = ph.sb("outT", [128, 2, DC, RUNMAX])
            loaded, chain_sem = ph.sem("loaded"), ph.sem("chain")
            projected, low_set, grown_set, mapped = ph.done("projected", 4), ph.done("low_set", 4), ph.done("grown_set", 4), ph.done("mapped", 4)
            read, divided, result, kept = ph.done("read", 4), ph.done("divided", 4), ph.done("result", BODY), ph.done("kept", BODY)
            qbank = [ph.ps(f"q{i}") for i in range(4)]
            numbank, denbank = ph.ps("num"), ph.ps("den")
            obank = [ph.ps(f"o{i}") for i in range(2)]
            nload = 2 + (1 if bias else 0)
            block = ph.block()

            @block.sync
            def _(sp):
                sp.dma_start(w[:], feature_rows(a[wq])).then_inc(loaded, 16)
                sp.dma_start(wout[:], feature_rows(a[wo])).then_inc(loaded, 16)
                if bias:
                    sp.dma_start(bq[:], a[bias[0]]).then_inc(loaded, 16)
                sp.wait_ge(loaded, 16 * nload)

            @block.tensor
            def _(pe):
                projected.open(pe)
                read.open(pe)
                result.open(pe)
                pe.wait_ge(loaded, 16 * nload)
                with pe.Fori(0, NODE_LOOPS) as o:
                    for s, (first, m) in enumerate(RUNS):
                        for mo in range(DC):
                            i = s * DC + mo
                            ph.hold(pe, mapped, o, i - 4)
                            for c in range(DC):
                                ins = nc.tensor.matmul(qbank[i][:, 0:m * P], w[:, c, mo * 128:(mo + 1) * 128],
                                                       core.xnT[:, c, columns(o * BODY + first, m)], start=c == 0, stop=c == DC - 1)
                            ins.then_inc(projected.sem, 1)
                    for s, (first, m) in enumerate(RUNS):
                        for c in range(DC):
                            i = s * DC + c
                            ph.hold(pe, mapped, o, i)
                            ph.hold(pe, divided, o, i - 1)
                            nc.tensor.matmul(numbank[:, 0:m * P], context[:, c, :], query[:, s, c, 0:m * P], start=True, stop=True)
                            nc.tensor.matmul(denbank[:, 0:m * P], keysum[:, c, :], query[:, s, c, 0:m * P], start=True, stop=True).then_inc(read.sem, 1)
                    for s, (first, m) in enumerate(RUNS):
                        ph.hold(pe, divided, o, s * DC + DC - 1)
                        for j in range(m):
                            i = first + j
                            ph.hold(pe, kept, o, i - 2)
                            for c in range(DC):
                                ins = nc.tensor.matmul(obank[i % 2][0:P, 0:D], outT[:, s, c, j * P:(j + 1) * P], wout[:, c, :], start=c == 0, stop=c == DC - 1)
                            if i == BODY - 1:
                                pass
                            ins.then_inc(result.sem, 1)

            @block.vector
            def _(v):
                low_set.open(v)
                mapped.open(v)
                divided.open(v)
                kept.open(v)
                per_body = 2 * 4 + 4
                v.wait_ge(loaded, 16 * nload)
                with v.Fori(0, NODE_LOOPS) as o:
                    chain = Chain(v, chain_sem, per_body, o)
                    for s, (first, m) in enumerate(RUNS):
                        for mo in range(DC):
                            i, n = s * DC + mo, m * P
                            ph.hold(v, projected, o, i)
                            bcol = bq[:, mo:mo + 1] if bias else 0.0
                            chain(nc.vector.tensor_scalar(pos[:, s, mo, 0:n], qbank[i][:, 0:n], bcol, 0.0, ALU.add, ALU.max))
                            nc.vector.tensor_scalar(low[:, s, mo, 0:n], qbank[i][:, 0:n], bcol, 0.0, ALU.add, ALU.min).then_inc(low_set.sem, 1)
                    for s, (first, m) in enumerate(RUNS):
                        for mo in range(DC):
                            i, n = s * DC + mo, m * P
                            ph.hold(v, grown_set, o, i)
                            ph.hold(v, read, o, i - 4)
                            nc.vector.tensor_tensor(query[:, s, mo, 0:n], pos[:, s, mo, 0:n], grown[:, s, mo, 0:n], ALU.add).then_inc(mapped.sem, 1)
                    for s, (first, m) in enumerate(RUNS):
                        for c in range(DC):
                            i, n = s * DC + c, m * P
                            ph.hold(v, read, o, i)
                            if clamp is not None:
                                chain(nc.vector.tensor_scalar(inverse[:, s, 0:n], denbank[:, 0:n], clamp, None, ALU.max))
                            else:
                                chain(nc.vector.tensor_scalar(inverse[:, s, 0:n], denbank[:, 0:n], plus, None, ALU.add))
                            chain.settle()
                            v.sem_inc(ph.spent, 1)
                            chain(nc.vector.reciprocal(inverse[:, s, 0:n], inverse[:, s, 0:n]))
                            chain.settle()
                            v.sem_inc(ph.spent, 1)
                            if c == 0:
                                ph.hold(v, result, o, first + m - 1 - BODY)
                            nc.vector.scalar_tensor_tensor(outT[:, s, c, 0:n], numbank[:, 0:n], length, inverse[:, s, 0:n], ALU.mult, ALU.mult).then_inc(divided.sem, 1)
                    for s, (first, m) in enumerate(RUNS):
                        for j in range(m):
                            i = first + j
                            row = target[:, bass.ds(o * BODY + i, 1), :]
                            ph.hold(v, result, o, i)
                            if add:
                                nc.vector.tensor_tensor(row, row, obank[i % 2][0:P, 0:D].unsqueeze(1), ALU.add).then_inc(kept.sem, 1)
                            else:
                                nc.vector.tensor_scalar(row, obank[i % 2][0:P, 0:D].unsqueeze(1), 0.0, None, ALU.add).then_inc(kept.sem, 1)
                    assert chain.n == per_body

            @block.scalar
            def _(act):
                grown_set.open(act)
                with act.Fori(0, NODE_LOOPS) as o:
                    for s, (first, m) in enumerate(RUNS):
                        for mo in range(DC):
                            i, n = s * DC + mo, m * P
                            ph.hold(act, low_set, o, i)
                            ph.hold(act, mapped, o, i - 4)
                            nc.scalar.activation(grown[:, s, mo, 0:n], low[:, s, mo, 0:n], ACT.Exp).then_inc(grown_set.sem, 1)


def start_rows(core, name, target, source, bias):
    nc, a = core.nc, core.a
    with Phase(nc, name) as ph:
        b = ph.sb("b", [P, D])
        loaded = ph.sem("loaded")
        block = ph.block()

        @block.sync
        def _(sp):
            sp.dma_start(b[:], a[bias].partition_broadcast(P)).then_inc(loaded, 16)
            sp.wait_ge(loaded, 16)

        @block.vector
        def _(v):
            v.wait_ge(loaded, 16)
            nc.vector.tensor_tensor(target[:], (target if source is None else source)[:], bcast_mid(b[:], [P, NT, D]), ALU.add)


def routing(kind):
    first = 5
    return {"soft": 3 + 3, "argmax": 3 + 3 + first + 1, "top2prob": 3 + 3 + 2 * first + 1 + 1 + 5, "top2logit": 3 + 2 * first + 1 + 1 + 4}[kind]


def ffn(core, name, sources, hidden, w1, b1, func, w2, target, experts=1, shared=False, gate=None, kind=None, b2=None, norm=None):
    nc, a = core.nc, core.a
    KC, HC = DC * len(sources), hidden // 128
    groups = 1 if shared else experts
    depth = 2 if norm else 1
    entries = [(s, g) for s in range(2) for g in range(groups)]
    order = []
    for step in range(len(entries) + depth):
        if step < len(entries):
            order.append(("h", 0, step))
        if depth == 2 and 0 <= step - 1 < len(entries):
            order.append(("h", 1, step - 1))
        if 0 <= step - depth < len(entries):
            order.append(("y", None, step - depth))
    hitems, yitems = [], []
    for what, layer, i in order:
        s, g = entries[i]
        if what == "h":
            hitems += [(layer, i, mo) for mo in range(HC)]
        else:
            yitems += [(i, j, e) for e in (range(experts) if shared else [g]) for j in range(RUNS[s][1])]
            if gate and b2 and g == 0:
                yitems += [(i, j, None) for j in range(RUNS[s][1])]
    hindex = {it: q for q, it in enumerate(hitems)}
    yindex = {it: q for q, it in enumerate(yitems)}
    HR, YR = 4, 3
    HB, YB = len(hitems), len(yitems)
    def last_reader(layer, i):
        if layer + 1 < depth:
            return "h", hindex[(layer + 1, i, HC - 1)]
        return "y", max(q for q, it in enumerate(yitems) if it[0] == i and it[2] is not None)
    def last_update(q):
        i, j, _ = yitems[q]
        s = entries[i][0]
        return max((r for r in range(q) if entries[yitems[r][0]][0] == s and yitems[r][1] == j), default=None)

    with Phase(nc, name) as ph:
        W1 = ph.sb("W1", [128, groups, KC, hidden])
        W1b = ph.sb("W1b", [128, groups, HC, hidden]) if norm else None
        W2 = ph.sb("W2", [128, experts, HC, D])
        hid = [ph.sb(f"hid{layer}", [128, 2, HC, RUNMAX]) for layer in range(depth)]
        b1c = ph.sb("b1c", [128, groups, HC])
        loads = []
        for g in range(groups):
            loads.append((W1[:, g], (a[w1] if groups == 1 else a[w1][g]).rearrange("(c p) h -> p c h", p=128)))
        if norm:
            for g in range(groups):
                loads.append((W1b[:, g], a[norm["w"]][g].rearrange("(c p) h -> p c h", p=128)))
            bn = {n: ph.sb("bn_" + n, [128, groups, HC]) for layer in norm["columns"] for n in layer}
            for layer in norm["columns"]:
                for n in layer:
                    loads.append((bn[n][:], a[n]))
            scale = [ph.sb(f"scale{i}", [128, groups, HC]) for i in range(2)]
            shift = [ph.sb(f"shift{i}", [128, groups, HC]) for i in range(2)]
            root = [ph.sb(f"root{i}", [128, groups, HC]) for i in range(2)]
        elif b1:
            loads.append((b1c[:, 0] if groups == 1 else b1c[:], a[b1]))
        for e in range(experts):
            loads.append((W2[:, e], (a[w2] if experts == 1 else a[w2][e]).rearrange("(c p) d -> p c d", p=128)))
        if gate:
            wg = ph.sb("wg", [128, HC if shared else DC, 8])
            bg = ph.sb("bg", [P, 8])
            loads.append((wg[:], feature_rows(a[gate[0]])))
            if gate[1]:
                loads.append((bg[:], a[gate[1]].partition_broadcast(P)))
            if b2:
                b2r = ph.sb("b2r", [8, D])
                loads.append((b2r[:], a[b2]))
            logitT = ph.sb("logitT", [8, 2, RUNMAX])
            comb = ph.sb("comb", [P, 2, 3, 8])
            combT = ph.sb("combT", [8, 2, RUNMAX])
            work = ph.sb("work", [P, 2, 8, 3, 8])
            col = ph.sb("col", [P, 2, 4, 3])
            gbank = ph.ps("gate")
        loaded, chain_sem = ph.sem("loaded"), ph.sem("chain")
        hid_made, hid_kept = ph.done("hid_made", HB), ph.done("hid_kept", HB)
        out_made, out_kept = ph.done("out_made", YB), ph.done("out_kept", YB)
        scored, score_kept, scores_turned = ph.done("scored", 2), ph.done("score_kept", 2), ph.done("scores_turned", 2)
        centred, grown, routed = ph.done("centred", 2), ph.done("grown", 2), ph.done("routed", 2)
        comb_turned, comb_kept = ph.done("comb_turned", 2), ph.done("comb_kept", 2)
        inverse_ready, root_ready, folded = ph.sem("inverse_ready"), ph.sem("root_ready"), ph.sem("folded")
        hbank = [ph.ps(f"h{i}") for i in range(HR)]
        ybank = [ph.ps(f"y{i}") for i in range(YR)]
        nload = 16 * len(loads)
        block = ph.block()

        @block.sync
        def _(sp):
            for to, what in loads:
                sp.dma_start(to, what).then_inc(loaded, 16)
            sp.wait_ge(loaded, nload)

        @block.tensor
        def _(pe):
            hid_made.open(pe)
            out_made.open(pe)
            for d in (scored, scores_turned, comb_turned):
                d.open(pe)
            pe.wait_ge(loaded, nload)
            with pe.Fori(0, NODE_LOOPS) as o:
                def score(s):
                    first, m = RUNS[s]
                    ph.hold(pe, comb_kept if b2 else routed, o, s - 1)
                    for c in range(DC):
                        ins = nc.tensor.matmul(gbank[0:8, 0:m * P], wg[:, c, :], sources[0][:, c, columns(o * BODY + first, m)], start=c == 0, stop=c == DC - 1)
                    ins.then_inc(scored.sem, 1)

                def turn_scores(s):
                    ph.hold(pe, score_kept, o, s)
                    for j in range(RUNS[s][1]):
                        ins = nc.tensor.transpose(gbank[0:P, 400 + 8 * j:408 + 8 * j], logitT[:, s, j * P:(j + 1) * P], core.ident[0:8, 0:8])
                    ins.then_inc(scores_turned.sem, 1)

                def score_hidden(s, i):
                    ph.hold(pe, comb_kept if b2 else routed, o, s - 1)
                    ph.hold(pe, hid_kept, o, hindex[(0, i, HC - 1)])
                    for j in range(RUNS[s][1]):
                        for c in range(HC):
                            ins = nc.tensor.matmul(gbank[0:P, 400 + 8 * j:408 + 8 * j], hid[0][:, i % 2, c, j * P:(j + 1) * P], wg[:, c, :], start=c == 0, stop=c == HC - 1)
                    ins.then_inc(scores_turned.sem, 1)

                def turn_comb(s):
                    ph.hold(pe, routed, o, s)
                    for j in range(RUNS[s][1]):
                        ins = nc.tensor.transpose(gbank[0:8, j * P:(j + 1) * P], comb[:, s, j, :], core.ident[0:P, 0:P])
                    ins.then_inc(comb_turned.sem, 1)

                for what, layer, i in order:
                    s, g = entries[i]
                    first, m = RUNS[s]
                    n = m * P
                    if what == "h":
                        if layer == 0 and g == 0 and gate and not shared:
                            score(s)
                        for mo in range(HC):
                            q = hindex[(layer, i, mo)]
                            ph.hold(pe, hid_kept, o, slot_owner(HR, HB, q))
                            if layer == 0:
                                pieces = [(W1[:, g, c, mo * 128:(mo + 1) * 128], sources[c // DC][:, c % DC, columns(o * BODY + first, m)]) for c in range(KC)]
                            else:
                                ph.hold(pe, hid_kept, o, hindex[(0, i, HC - 1)])
                                pieces = [(W1b[:, g, c, mo * 128:(mo + 1) * 128], hid[0][:, i % 2, c, 0:n]) for c in range(HC)]
                            for c, (lhsT, rhs) in enumerate(pieces):
                                ins = nc.tensor.matmul(hbank[q % HR][:, 0:n], lhsT, rhs, start=c == 0, stop=c == len(pieces) - 1)
                            ins.then_inc(hid_made.sem, 1)
                        if layer == 0 and g == 0 and gate and not shared:
                            turn_scores(s)
                    else:
                        if shared and gate:
                            score_hidden(s, i)
                        mine = [q for q, it in enumerate(yitems) if it[0] == i]
                        turned = False
                        for q in mine:
                            _, j, e = yitems[q]
                            if e is None and not turned:
                                turn_comb(s)
                                ph.hold(pe, comb_kept, o, s)
                                turned = True
                            ph.hold(pe, out_kept, o, slot_owner(YR, YB, q))
                            if e is None:
                                ins = nc.tensor.matmul(ybank[q % YR][0:P, 0:D], combT[:, s, j * P:(j + 1) * P], b2r[:], start=True, stop=True)
                            else:
                                ph.hold(pe, hid_kept, o, hindex[(depth - 1, i, HC - 1)])
                                for c in range(HC):
                                    ins = nc.tensor.matmul(ybank[q % YR][0:P, 0:D], hid[-1][:, i % 2, c, j * P:(j + 1) * P], W2[:, e, c, :], start=c == 0, stop=c == HC - 1)
                            ins.then_inc(out_made.sem, 1)

        @block.scalar
        def _(act):
            hid_kept.open(act)
            for d in (score_kept, grown, comb_kept):
                d.open(act)
            act.wait_ge(loaded, nload)
            if norm:
                act.wait_ge(inverse_ready, 1)
                for i in range(2):
                    nc.scalar.activation(root[i][:], shift[i][:], ACT.Sqrt).then_inc(root_ready, 1)
                act.wait_ge(folded, 1)
            with act.Fori(0, NODE_LOOPS) as o:
                def grow(s):
                    ph.hold(act, centred, o, s)
                    m = RUNS[s][1]
                    nc.scalar.activation(work[:, s, 1, 0:m, :], work[:, s, 0, 0:m, :], ACT.Exp).then_inc(grown.sem, 1)

                for what, layer, i in order:
                    s, g = entries[i]
                    first, m = RUNS[s]
                    n = m * P
                    if what == "h":
                        if layer == 0 and g == 0 and gate and not shared:
                            ph.hold(act, scored, o, s)
                            ph.hold(act, scores_turned, o, s - 2)
                            nc.scalar.activation(logitT[:, s, 0:n], gbank[0:8, 0:n], ACT.Copy).then_inc(score_kept.sem, 1)
                        for mo in range(HC):
                            q = hindex[(layer, i, mo)]
                            ph.hold(act, hid_made, o, q)
                            if mo == 0:
                                back = i - 2
                                reader, r = last_reader(layer, back % len(entries))
                                if back < 0:
                                    r -= HB if reader == "h" else YB
                                ph.hold(act, hid_made if reader == "h" else out_made, o, r)
                            if norm:
                                nc.scalar.activation(hid[layer][:, i % 2, mo, 0:n], hbank[q % HR][:, 0:n], func,
                                                     scale=scale[layer][:, g, mo:mo + 1], bias=shift[layer][:, g, mo:mo + 1]).then_inc(hid_kept.sem, 1)
                            elif b1:
                                nc.scalar.activation(hid[layer][:, i % 2, mo, 0:n], hbank[q % HR][:, 0:n], func,
                                                     bias=b1c[:, g, mo:mo + 1]).then_inc(hid_kept.sem, 1)
                            else:
                                nc.scalar.activation(hid[layer][:, i % 2, mo, 0:n], hbank[q % HR][:, 0:n], func).then_inc(hid_kept.sem, 1)
                        if layer == 0 and g == 0 and gate and not shared:
                            grow(s)
                    elif gate:
                        if shared:
                            grow(s)
                        if b2 and g == 0:
                            ph.hold(act, comb_turned, o, s)
                            bias_items = [q for q, it in enumerate(yitems) if it[2] is None and entries[it[0]][0] == s]
                            ph.hold(act, out_made, o, bias_items[-1] - YB)
                            nc.scalar.activation(combT[:, s, 0:n], gbank[0:8, 0:n], ACT.Copy).then_inc(comb_kept.sem, 1)

        @block.vector
        def _(v):
            out_kept.open(v)
            for d in (centred, routed):
                d.open(v)
            v.wait_ge(loaded, nload)
            base = 0
            if norm:
                chain = Chain(v, chain_sem)
                for i, (b, gname, be, mean, var) in enumerate(norm["columns"]):
                    chain.link(nc.vector.tensor_scalar(bn[var][:], bn[var][:], norm["eps"], None, ALU.add))
                    chain.link(nc.vector.reciprocal(shift[i][:], bn[var][:]))
                nc.vector.tensor_copy(root[0][:, 0:1, 0:1], shift[0][:, 0:1, 0:1]).then_inc(inverse_ready, 1)
                v.wait_ge(root_ready, 2)
                for i, (b, gname, be, mean, var) in enumerate(norm["columns"]):
                    chain.link(nc.vector.tensor_tensor(scale[i][:], root[i][:], root[i][:], ALU.mult))
                    chain.link(nc.vector.tensor_tensor(scale[i][:], scale[i][:], bn[var][:], ALU.mult))
                    chain.link(nc.vector.tensor_scalar(scale[i][:], scale[i][:], -0.5, 1.5, ALU.mult, ALU.add))
                    chain.link(nc.vector.tensor_tensor(scale[i][:], scale[i][:], root[i][:], ALU.mult))
                    chain.link(nc.vector.tensor_tensor(scale[i][:], scale[i][:], bn[gname][:], ALU.mult))
                    chain.link(nc.vector.tensor_tensor(shift[i][:], bn[b][:], bn[mean][:], ALU.subtract))
                    chain.link(nc.vector.tensor_tensor(shift[i][:], shift[i][:], scale[i][:], ALU.mult))
                    chain.link(nc.vector.tensor_tensor(shift[i][:], shift[i][:], bn[be][:], ALU.add))
                nc.vector.tensor_copy(root[0][:, 0:1, 0:1], shift[0][:, 0:1, 0:1]).then_inc(folded, 1)
                base = chain.n
            per_body = 2 * routing(kind) if gate else 0
            with v.Fori(0, NODE_LOOPS) as o:
                chain = Chain(v, chain_sem, per_body, o, base)

                def link(ins):
                    chain.link(ins)
                    v.sem_inc(ph.spent, 1)

                def route(s):
                    m = RUNS[s][1]
                    full = [P, m, 8]
                    z, ex, eq, val, pick, rest, pick2, both = (work[:, s, i, 0:m, :] for i in range(8))
                    top, den, low, _ = (col[:, s, i, 0:m] for i in range(4))
                    wide = lambda c: bcast_last(c, full)
                    logits = gbank[0:P, 400:400 + 8 * m].rearrange("p (j e) -> p j e", e=8)

                    def first_of(scores, picked):
                        link(nc.vector.tensor_reduce(top, scores, AX.X, ALU.max))
                        link(nc.vector.tensor_tensor(eq, scores, wide(top), ALU.is_equal))
                        link(nc.vector.scalar_tensor_tensor(val, eq, -8.0, bcast_mid(core.iota8[:], full), ALU.mult, ALU.add))
                        link(nc.vector.tensor_reduce(low, val, AX.X, ALU.min))
                        link(nc.vector.tensor_tensor(picked, val, wide(low), ALU.is_equal))

                    ph.hold(v, scores_turned, o, s)
                    if gate[1]:
                        link(nc.vector.tensor_tensor(rest, logits, bcast_mid(bg[:], full), ALU.add))
                    else:
                        link(nc.vector.tensor_scalar(rest, logits, 0.0, None, ALU.add))
                    link(nc.vector.tensor_reduce(top, rest, AX.X, ALU.max))
                    chain(nc.vector.tensor_tensor(z, rest, wide(top), ALU.subtract))
                    chain.settle()
                    v.sem_inc(centred.sem, 1)
                    ph.hold(v, grown, o, s)
                    if kind == "top2logit":
                        first_of(rest, pick)
                        link(nc.vector.scalar_tensor_tensor(rest, pick, -3e38, rest, ALU.mult, ALU.add))
                        first_of(rest, pick2)
                        link(nc.vector.tensor_tensor(both, pick, pick2, ALU.add))
                        link(nc.vector.tensor_tensor(both, both, ex, ALU.mult))
                        link(nc.vector.tensor_reduce(den, both, AX.X, ALU.add))
                        link(nc.vector.reciprocal(den, den))
                        answer, by = both, den
                    else:
                        link(nc.vector.tensor_reduce(den, ex, AX.X, ALU.add))
                        link(nc.vector.reciprocal(den, den))
                        link(nc.vector.tensor_tensor(ex, ex, wide(den), ALU.mult))
                        if kind == "argmax":
                            first_of(ex, pick)
                        elif kind == "top2prob":
                            first_of(ex, pick)
                            link(nc.vector.scalar_tensor_tensor(rest, pick, -2.0, ex, ALU.mult, ALU.add))
                            first_of(rest, pick2)
                            link(nc.vector.tensor_tensor(both, pick, pick2, ALU.add))
                            link(nc.vector.tensor_tensor(both, both, ex, ALU.mult))
                            link(nc.vector.tensor_reduce(den, both, AX.X, ALU.add))
                            link(nc.vector.tensor_scalar(den, den, 1e-12, None, ALU.max))
                            link(nc.vector.reciprocal(den, den))
                    if b2:
                        ph.hold(v, comb_turned, o, s - 2)
                    out = comb[:, s, 0:m, :]
                    if kind == "soft":
                        return link(nc.vector.tensor_copy(out, ex)) if False else v.sem_inc(ph.spent, 1)
                    if kind == "argmax":
                        link(nc.vector.tensor_tensor(out, ex, pick, ALU.mult))
                    else:
                        link(nc.vector.tensor_tensor(out, both, wide(den), ALU.mult))

                for what, layer, i in order:
                    s, g = entries[i]
                    first, m = RUNS[s]
                    if gate and ((shared and what == "y") or (not shared and what == "h" and layer == 0 and g == 0)):
                        route(s)
                        if kind == "soft":
                            nc.vector.tensor_copy(comb[:, s, 0:m, :], work[:, s, 1, 0:m, :]).then_inc(routed.sem, 1)
                            ph.hold(v, routed, o, s)
                        else:
                            v.sem_inc(routed.sem, 1)
                    if what == "y":
                        for q in [q for q, it in enumerate(yitems) if it[0] == i]:
                            _, j, e = yitems[q]
                            row = target[:, bass.ds(o * BODY + first + j, 1), :]
                            made = ybank[q % YR][0:P, 0:D].unsqueeze(1)
                            ph.hold(v, out_made, o, q)
                            if last_update(q) is not None:
                                ph.hold(v, out_kept, o, last_update(q))
                            if e is None or not gate:
                                nc.vector.tensor_tensor(row, made, row, ALU.add).then_inc(out_kept.sem, 1)
                            else:
                                nc.vector.scalar_tensor_tensor(row, made, comb[:, s, j, e:e + 1], row, ALU.mult, ALU.add).then_inc(out_kept.sem, 1)
                if gate:
                    assert chain.n == per_body, (chain.n, per_body)


def mix0(core):
    with Phase(core.nc, "m0") as ph:
        mid = ph.sb("mid", [P, NT, D])
        midT = ph.sb("midT", [128, DC, N])
        start_rows(core, "m0_start", mid, core.xn, "L0_mix_bo")
        linear_attention(core, "m0_att", "L0_mix_Wq", [("L0_mix_Wk", None), ("L0_mix_Wv", None)], "L0_mix_Wo", mid,
                         bias=("L0_mix_bq", "L0_mix_bk", "L0_mix_bv"), plus=1e-6)
        layer_norm(core, "m0_ln1", mid, mid, midT, token_affine=("L0_mix_ln1_g", "L0_mix_ln1_b"))
        start_rows(core, "m0_bias", mid, None, "L0_mix_b2")
        ffn(core, "m0_ff", [midT], 1024, "L0_mix_W1", "L0_mix_b1", ACT.Relu, "L0_mix_W2", mid)
        layer_norm(core, "m0_ln2", mid, mid, token_affine=("L0_mix_ln2_g", "L0_mix_ln2_b"), add_to_x=True)


def ffn0(core):
    layer_norm(core, "ln0b", core.x, core.xn, core.xnT)
    ffn(core, "f0", [core.xnT], 1024, "L0_ffn_W1", "L0_ffn_b1", ACT.Gelu, "L0_ffn_Wd", core.x, experts=8, shared=True,
        gate=("L0_ffn_Wg", "L0_ffn_bg"), kind="argmax", b2="L0_ffn_bd")


def ffn1(core):
    layer_norm(core, "ln1b", core.x, core.xn, core.xnT, feature_affine=("L1_ffn_gamma", "L1_ffn_beta"))
    ffn(core, "f1", [core.xnT], 512, "L1_ffn_W1", "L1_ffn_b1", ACT.Gelu, "L1_ffn_W2", core.x, experts=8,
        gate=("L1_ffn_Wr", "L1_ffn_br"), kind="top2logit", b2="L1_ffn_b2")


def mix2(core):
    start_rows(core, "m2_start", core.x, None, "L2_mix_bproj")
    linear_attention(core, "m2_att", "L2_mix_Wq", [("L2_mix_Wkv", None)], "L2_mix_Wproj", core.x, clamp=1e-6)


def ffn2(core):
    layer_norm(core, "ln2b", core.x, core.xn, core.xnT)
    ffn(core, "f2", [core.xnT], 256, "L2_ffn_W1", None, ACT.Relu, "L2_ffn_Wo", core.x, experts=8,
        gate=("L2_ffn_Wr", "L2_ffn_br"), kind="soft", b2="L2_ffn_bo",
        norm={"w": "L2_ffn_W2", "eps": 1e-3, "columns": [[f"L2_ffn_{n}{i}" for n in ("b", "g", "be", "m", "v")] for i in (1, 2)]})


def gnn3(core):
    support = core.table("support3", N, D)
    tables = [core.table(f"sum3_{i}", N + P, D) for i in range(TABLES)]
    clear_tables(core, "clear3", tables)
    with Phase(core.nc, "g3") as ph:
        dest = ph.sb("s", [P, NT, D])
        project(core, "proj3", core.xnT, [("L3_gnn_weight", D)], dest, D, table=support)
    spread(core, "spread3", support, core.dst, core.a["src_rows"], core.srcf, core.src_once, tables, weight=core.weight)
    finish_plain(core, "fin3", tables, elu=False)


def mix3(core):
    with Phase(core.nc, "m3") as ph:
        mid = ph.sb("mid", [P, NT, D])
        midT = ph.sb("midT", [128, DC, N])
        linear_attention(core, "m3_att", "L3_mix_Wq", [("L3_mix_Wk", None), ("L3_mix_Wv", None)], "L3_mix_Wm", mid,
                         plus=1e-6, length=float(N), add=False)
        layer_norm(core, "m3_ln1", mid, mid, midT, token_affine=("L3_mix_g1", "L3_mix_b1"))
        clear_rows(core, "m3_clear", mid)
        ffn(core, "m3_ff", [core.xnT, midT], 512, "L3_mix_W1", None, ACT.Relu, "L3_mix_W2", mid)
        layer_norm(core, "m3_ln2", mid, mid, token_affine=("L3_mix_g2", "L3_mix_b2"), add_to_x=True, add_xn=True)


def clear_rows(core, name, target):
    with Phase(core.nc, name) as ph:
        block = ph.block()

        @block.vector
        def _(v):
            core.nc.vector.memset(target[:], 0.0)


def ffn3(core):
    layer_norm(core, "ln3b", core.x, core.xn, core.xnT, add_to_x=True)
    ffn(core, "f3", [core.xnT], 256, "L3_ffn_w1", "L3_ffn_b1", ACT.Gelu, "L3_ffn_w2", core.x, experts=8,
        gate=("L3_ffn_router_w", None), kind="top2prob", b2="L3_ffn_b2")


def transpose_rows(core, name, buf, outT):
    nc = core.nc
    with Phase(nc, name) as ph:
        tile = ph.sb("tile", [P, BODY, D])
        staged, turned, stored = ph.done("staged", BODY), ph.done("turned", BODY), ph.done("stored", BODY)
        banks = [ph.ps(f"bank{k}") for k in range(BODY)]
        block = ph.block()

        @block.gpsimd
        def _(pool):
            staged.open(pool)
            with pool.Fori(0, NODE_LOOPS) as o:
                for k in range(BODY):
                    ph.hold(pool, turned, o, k - BODY)
                    nc.gpsimd.tensor_copy(tile[:, k:k + 1, :], buf[:, bass.ds(o * BODY + k, 1), :]).then_inc(staged.sem, 1)

        @block.tensor
        def _(pe):
            turned.open(pe)
            with pe.Fori(0, NODE_LOOPS) as o:
                for k in range(BODY):
                    ph.hold(pe, staged, o, k)
                    ph.hold(pe, stored, o, k - BODY)
                    for c in range(DC):
                        ins = nc.tensor.transpose(banks[k][:, c * P:(c + 1) * P], tile[:, k, c * 128:(c + 1) * 128], core.ident[0:P, 0:P])
                    ins.then_inc(turned.sem, 1)

        @block.scalar
        def _(act):
            stored.open(act)
            with act.Fori(0, NODE_LOOPS) as o:
                for k in range(BODY):
                    ph.hold(act, turned, o, k)
                    nc.scalar.activation(outT[:, :, columns(o * BODY + k)], banks[k][:, 0:DC * P].rearrange("p (c n) -> p c n", c=DC), ACT.Copy).then_inc(stored.sem, 1)


def edge_scores(core, name, left, left_index, right, right_index, left_width, width, score, stash, kept_columns, types=None, mark=None):
    nc, a = core.nc, core.a
    with Phase(nc, name) as ph:
        left_at, right_at = ph.sb("left_at", [P, BODY], I32), ph.sb("right_at", [P, BODY], I32)
        lrow, rrow = ph.sb("lrow", [P, BODY, left_width]), ph.sb("rrow", [P, BODY, width])
        left_in, right_in = [ph.sem(f"left_in{k}") for k in range(BODY)], [ph.sem(f"right_in{k}") for k in range(BODY)]
        stashed = [ph.sem(f"stashed{k}") for k in range(BODY)]
        index_set, used = ph.done("index_set", BODY), ph.done("used", BODY)
        chain_sem, const, scaled = ph.sem("chain"), ph.sem("const"), ph.sem("scaled")
        if types:
            tw = a[types[1]].shape[1]
            trow = ph.sb("trow", [64, BODY, P], I32)
            which = ph.sb("which", [64, BODY, P])
            number = ph.sb("number", [64, 1])
            rel = ph.sb("rel", [64, tw])
            types_in = [ph.sem(f"types_in{k}") for k in range(BODY)]
            compared, picked = ph.done("compared", BODY), ph.done("picked", BODY)
            banks = [ph.ps(f"bank{k}") for k in range(BODY)]
        if mark:
            keys = ph.sb("keys", [P, BODY, P], I32)
            keys_in = ph.sem("keys_in")
            marks = Marks(core, ph, mark[1], mark[2])
        block = ph.block()

        if types:
            @block.sync
            def _(sp):
                sp.dma_start(number[:], a["c_types"]).then_inc(const, 16)
                sp.dma_start(rel[:], a[types[1]]).then_inc(const, 16)
                if mark:
                    marks.load(sp)
                with sp.Fori(0, EDGE_LOOPS) as o:
                    for k in range(BODY):
                        ph.hold(sp, compared, o, k - BODY)
                        sp.dma_start(trow[:, k, :], a[types[0]][bass.ds((o * BODY + k) * P, P)].partition_broadcast(64)).then_inc(types_in[k], 16)
                    if mark:
                        ph.hold(sp, marks.marked, o, -1)
                        sp.dma_start(keys[:], mark[0][bass.ds(o * BODY * P, BODY * P)].partition_broadcast(P)
                                     .rearrange("p (k e) -> p k e", k=BODY)).then_inc(keys_in, 16)

            @block.tensor
            def _(pe):
                picked.open(pe)
                pe.wait_ge(scaled, 1)
                with pe.Fori(0, EDGE_LOOPS) as o:
                    for k in range(BODY):
                        ph.hold(pe, compared, o, k)
                        ph.hold(pe, used, o, k - BODY)
                        nc.tensor.matmul(banks[k][0:P, 0:tw], which[:, k, :], rel[:], start=True, stop=True).then_inc(picked.sem, 1)

        @block.scalar
        def _(act):
            index_set.open(act)

            def set_index(o, k):
                ph.hold(act, used, o, k - BODY)
                if not (isinstance(o, int) and o == 0):
                    ph.hold_dma(act, stashed[k], o - 1)
                one = bass.ds(o * BODY + k, 1)
                nc.scalar.activation(left_at[:, k:k + 1], left_index[:, one], ACT.Copy)
                nc.scalar.activation(right_at[:, k:k + 1], right_index[:, one], ACT.Copy).then_inc(index_set.sem, 1)

            def keep(o, k):
                ph.hold_dma(act, left_in[k], o)
                act.dma_start(stash[bass.ds((o * BODY + k) * P, P), :], lrow[:, k, kept_columns]).then_inc(stashed[k], 16)

            for k in range(BODY):
                set_index(0, k)
            for k in range(BODY):
                keep(0, k)
            with act.Fori(1, EDGE_LOOPS) as o:
                for k in range(BODY):
                    set_index(o, k)
                for k in range(BODY):
                    keep(o, k)
            for k in range(BODY):
                act.wait_ge(stashed[k], 16 * EDGE_LOOPS)

        @block.gpsimd
        def _(pool):
            with pool.Fori(0, EDGE_LOOPS) as o:
                for k in range(BODY):
                    ph.hold(pool, index_set, o, k)
                    nc.gpsimd.indirect_dma_start(lrow[:, k, :], None, left, bass.IndirectOffsetOnAxis(ap=left_at[:, k:k + 1], axis=0)).then_inc(left_in[k], 16)
                    nc.gpsimd.indirect_dma_start(rrow[:, k, :], None, right, bass.IndirectOffsetOnAxis(ap=right_at[:, k:k + 1], axis=0)).then_inc(right_in[k], 16)

        @block.vector
        def _(v):
            used.open(v)
            if types:
                compared.open(v)
                v.wait_ge(const, 32)
                nc.vector.tensor_scalar(rel[:], rel[:], types[2], None, ALU.mult).then_inc(scaled, 1)
            if mark:
                marks.marked.open(v)
                v.wait_ge(marks.const, 32)
            with v.Fori(0, EDGE_LOOPS) as o:
                if types:
                    for k in range(BODY):
                        ph.hold_dma(v, types_in[k], o)
                        ph.hold(v, picked, o, k - BODY)
                        nc.vector.tensor_scalar(which[:, k, :], trow[:, k, :], number[:, 0:1], None, ALU.is_equal).then_inc(compared.sem, 1)
                steps = (2 * BODY if types else 0) + (Marks.LINKS if mark else 0)
                chain = Chain(v, chain_sem, steps, o)
                for k in range(BODY):
                    ph.hold_dma(v, left_in[k], o)
                    ph.hold_dma(v, right_in[k], o)
                    if types:
                        ph.hold(v, picked, o, k)
                    score(ph, v, chain, lrow[:, k, :], rrow[:, k, :], banks[k][0:P, 0:tw] if types else None, o * BODY + k).then_inc(used.sem, 1)
                if mark:
                    ph.hold_dma(v, keys_in, o)
                    for k in range(BODY):
                        marks.compare(chain, keys[:, k, :], o, k)
                    marks.finish(v, chain, o)
                assert chain.n == steps
            v.wait_ge(used.sem, used.at(EDGE_LOOPS - 1, BODY - 1))
            if mark:
                v.wait_ge(marks.marked.sem, marks.marked.at(EDGE_LOOPS - 1, 0))


def spread_row(v_engine, nc, out, column):
    return nc.vector.tensor_scalar(out, column[0], column[1], None, ALU.mult)


def segment_softmax(core, name, scores, factor, alpha, heads):
    nc, a = core.nc, core.a
    LOW = -1e38
    with Phase(nc, name) as ph:
        starts = ph.sb("starts", [P, ET])
        forward = ph.sb("forward", [P, heads, ET])
        backward = ph.sb("backward", [P, heads, ET])
        mask = ph.sb("mask", [P, 2, ET])
        near = ph.sb("near", [P, ET])
        ends = ph.sb("ends", [P, 2 + 2 * heads])
        diag = ph.sb("diag", [P, 2 + 2 * heads, P])
        rows = ph.sb("rows", [P, 2 + 2 * heads, P])
        ones = ph.sb("ones", [P, P])
        equal = ph.sb("equal", [P, 2, 2, P])
        cand = ph.sb("cand", [P, heads, 2, P])
        best = ph.sb("best", [P, 2, heads])
        chain_sem, diag_set, spread_done, shifted = ph.sem("chain"), ph.sem("diag_set"), ph.sem("spread_done"), ph.sem("shifted")
        nv = 2 + 2 * heads
        per = 4
        banks = [ph.ps(f"bank{i}") for i in range((nv + per - 1) // per)]
        key = core.dstf
        block = ph.block()

        @block.vector
        def _(v):
            chain = Chain(v, chain_sem)
            link = chain.link
            chain(nc.vector.memset(ones[:], 1.0))
            chain(nc.vector.memset(starts[:, 0:1], 0.0))
            link(nc.vector.tensor_tensor(starts[:, 1:ET], key[:, 1:ET], key[:, 0:ET - 1], ALU.not_equal))
            link(nc.vector.tensor_scalar(starts[:], starts[:], LOW, None, ALU.mult))
            for h in range(heads):
                chain(nc.vector.tensor_tensor_scan(forward[:, h, :], starts[:], scores[:, h, :], 2 * LOW, ALU.add, ALU.max))
            chain.settle()
            for h in range(heads):
                chain(nc.vector.tensor_copy(backward[:, h, ET - 1:ET], scores[:, h, ET - 1:ET]))
                link(nc.vector.tensor_tensor_scan(backward[:, h, ET - 2::-1], starts[:, ET - 1:0:-1], scores[:, h, ET - 2::-1],
                                                  scores[:, h, ET - 1:ET], ALU.add, ALU.max))
            chain(nc.vector.tensor_copy(ends[:, 0:1], key[:, 0:1]))
            chain(nc.vector.tensor_copy(ends[:, 1:2], key[:, ET - 1:ET]))
            chain(nc.vector.tensor_copy(ends[:, 2:2 + heads], backward[:, :, 0:1].rearrange("p h o -> p (h o)")))
            link(nc.vector.tensor_copy(ends[:, 2 + heads:nv], forward[:, :, ET - 1:ET].rearrange("p h o -> p (h o)")))
            link(nc.vector.tensor_tensor(forward[:], forward[:], backward[:], ALU.max))
            for i in range(nv):
                ins = nc.vector.tensor_scalar(diag[:, i, :], core.ident[0:P, 0:P], ends[:, i:i + 1], None, ALU.mult)
                if i < nv - 1:
                    chain(ins)
            chain.settle()
            ins.then_inc(diag_set, 1)
            v.wait_ge(spread_done, 1)
            for i in range(nv):
                chain(nc.vector.tensor_copy(rows[:, i, :], banks[i // per][0:P, (i % per) * P:(i % per + 1) * P]))
            chain.settle()
            for side in range(2):
                link(nc.vector.tensor_scalar(equal[:, side], rows[:, 0:2, :], ends[:, side:side + 1], None, ALU.is_equal))
                link(nc.vector.tensor_scalar(equal[:, side], equal[:, side], 1.0, -LOW, ALU.subtract, ALU.mult))
                for h in range(heads):
                    chain(nc.vector.tensor_tensor(cand[:, h, 0, :], rows[:, 2 + h, :], equal[:, side, 0, :], ALU.add))
                    chain(nc.vector.tensor_tensor(cand[:, h, 1, :], rows[:, 2 + heads + h, :], equal[:, side, 1, :], ALU.add))
                chain.settle()
                link(nc.vector.tensor_reduce(best[:, side, :], cand[:], AX.XY, ALU.max))
                link(nc.vector.tensor_scalar(mask[:, side, :], key[:], ends[:, side:side + 1], None, ALU.is_equal))
                link(nc.vector.tensor_scalar(mask[:, side, :], mask[:, side, :], 1.0, -LOW, ALU.subtract, ALU.mult))
                for h in range(heads):
                    link(nc.vector.scalar_tensor_tensor(forward[:, h, :], mask[:, side, :], best[:, side, h:h + 1], forward[:, h, :], ALU.add, ALU.max))
            nc.vector.tensor_tensor(forward[:], scores[:], forward[:], ALU.subtract).then_inc(shifted, 1)

        @block.tensor
        def _(pe):
            pe.wait_ge(diag_set, 1)
            for b in range(len(banks)):
                n = min(per, nv - per * b)
                ins = nc.tensor.matmul(banks[b][0:P, 0:n * P], ones[:], diag[:, per * b:per * b + n, :], start=True, stop=True)
            ins.then_inc(spread_done, 1)

        @block.scalar
        def _(act):
            act.wait_ge(shifted, 1)
            nc.scalar.activation(alpha[:].rearrange("p e h -> p h e"), forward[:], ACT.Exp, scale=factor)


def gnn1(core):
    nc, a = core.nc, core.a
    heads, dim = 4, 64
    q, kv, val = core.table("q1", N, D), core.table("kv1", N, 2 * D), core.table("val1", ET * P, D)
    tables = [core.table(f"sum1_{i}", N + P, D + heads) for i in range(TABLES)]
    clear_tables(core, "clear1", tables)
    with Phase(nc, "g1a") as outer:
        enhT = outer.sb("enhT", [128, DC, N])
        dest = outer.sb("dest", [P, NT, 2 * D])
        with Phase(nc, "g1_enh") as ph:
            emb = ph.sb("emb", [128, DC])
            loaded, chain_sem = ph.sem("loaded"), ph.sem("chain")
            block = ph.block()

            @block.sync
            def _(sp):
                sp.dma_start(emb[:], a["L1_gnn_query_emb"]).then_inc(loaded, 16)
                sp.wait_ge(loaded, 16)

            @block.vector
            def _(v):
                chain = Chain(v, chain_sem)
                v.wait_ge(loaded, 16)
                chain.link(nc.vector.tensor_scalar(emb[:], emb[:], 0.1, None, ALU.mult))
                for c in range(DC):
                    chain(nc.vector.tensor_scalar(enhT[:, c, :], core.xnT[:, c, :], emb[:, c:c + 1], None, ALU.add))
        project(core, "g1_kv", enhT, [("L1_gnn_Wk", D), ("L1_gnn_Wv", D)], dest, 2 * D, bias=[("L1_gnn_bk", D), ("L1_gnn_bv", D)], table=kv)
        project(core, "g1_q", enhT, [("L1_gnn_Wq", D)], dest[:, :, 0:D], D, bias=[("L1_gnn_bq", D)], table=q)
    with Phase(nc, "g1b") as outer:
        alpha = outer.sb("alpha", [P, ET, heads])
        scores = outer.sb("scores", [P, heads, ET])

        def score(ph, v, chain, krow, qrow, rel, edge):
            krow = krow[:, 0:D]
            kh = krow.rearrange("p (h d) -> p h d", h=heads)
            chain(nc.vector.tensor_tensor(kh, kh, bcast_mid(rel, [P, heads, dim]), ALU.add))
            chain.settle()
            v.sem_inc(ph.spent, 1)
            chain(nc.vector.tensor_tensor(krow, krow, qrow, ALU.mult))
            chain.settle()
            v.sem_inc(ph.spent, 1)
            return nc.vector.tensor_reduce(scores[:, :, bass.ds(edge, 1)].rearrange("p h o -> p (h o)"), kh, AX.X, ALU.add)

        edge_scores(core, "g1_sc", kv, core.src, q, core.dst, 2 * D, D, score, val, slice(D, 2 * D), types=("type_rows", "L1_gnn_rel_w", 0.2),
                    mark=(a["dst_rows"], core.dstf, core.dst_once))
        segment_softmax(core, "g1_sm", scores, dim ** -0.5, alpha, heads)
        spread(core, "g1_sp", val, None, a["dst_rows"], core.dstf, core.dst_once, tables, alpha=alpha, heads=heads)
    with Phase(nc, "g1c") as outer:
        mid = outer.sb("mid", [P, NT, D])
        with Phase(nc, "g1_fin") as ph:
            table_sum = TableSum(ph, tables, D + heads)
            parts = table_sum.parts
            some = ph.sb("some", [P, NT, heads])
            den = ph.sb("den", [P, NT, heads])
            back, chain_sem = ph.sem("back"), ph.sem("chain")
            block = ph.block()

            @block.sync
            def _(sp):
                table_sum.load(sp)
                sp.dma_start(mid[:], nodes(kv[:, D:2 * D])).then_inc(back, 16)
                sp.wait_ge(back, 16)

            @block.vector
            def _(v):
                chain = Chain(v, chain_sem)
                link = chain.link
                table_sum.add(v, nc)
                total = parts[0][:, :, D:D + heads]
                wide = [P, NT, heads, dim]
                hd = lambda ap: ap.rearrange("p t (h d) -> p t h d", h=heads)
                link(nc.vector.tensor_scalar(some[:], total, 0.0, None, ALU.is_le))
                link(nc.vector.tensor_tensor(den[:], total, some[:], ALU.add))
                link(nc.vector.reciprocal(den[:], den[:]))
                link(nc.vector.tensor_tensor(hd(parts[0][:, :, 0:D]), hd(parts[0][:, :, 0:D]), bcast_last(den[:], wide), ALU.mult))
                v.wait_ge(back, 16)
                link(nc.vector.tensor_tensor(hd(mid[:]), hd(mid[:]), bcast_last(some[:], wide), ALU.mult))
                link(nc.vector.tensor_tensor(mid[:], mid[:], parts[0][:, :, 0:D], ALU.add))

        midT = outer.sb("midT", [128, DC, N])
        transpose_rows(core, "g1_turn", mid, midT)
        project(core, "g1_out", midT, [("L1_gnn_Wo", D)], mid, D, bias=[("L1_gnn_bo", D)])
        add_rows(core, "g1_res", mid, core.xn)
        layer_norm(core, "g1_ln", mid, mid, token_affine=("L1_gnn_gamma", "L1_gnn_beta"), add_to_x=True)


def add_rows(core, name, target, source):
    with Phase(core.nc, name) as ph:
        block = ph.block()

        @block.vector
        def _(v):
            core.nc.vector.tensor_tensor(target[:], target[:], source[:], ALU.add)


def row_lengths(core, name, buf, inverse):
    nc = core.nc
    with Phase(nc, name) as ph:
        square = ph.sb("square", [P, NT, D])
        total, root, part = ph.sb("total", [P, NT]), ph.sb("root", [P, NT]), ph.sb("part", [P, NT])
        summed, rooted, chain_sem = ph.sem("summed"), ph.sem("rooted"), ph.sem("chain")
        block = ph.block()

        @block.vector
        def _(v):
            link = Chain(v, chain_sem).link
            link(nc.vector.tensor_tensor(square[:], buf[:], buf[:], ALU.mult))
            nc.vector.tensor_reduce(total[:], square[:], AX.X, ALU.add).then_inc(summed, 1)
            v.wait_ge(summed, 1)
            v.wait_ge(rooted, 1)
            link(nc.vector.tensor_scalar(root[:], root[:], 1e-12, None, ALU.max))
            link(nc.vector.reciprocal(part[:], root[:]))
            link(nc.vector.tensor_tensor(part[:], part[:], total[:], ALU.mult))
            link(nc.vector.tensor_tensor(root[:], root[:], part[:], ALU.add))
            link(nc.vector.tensor_scalar(root[:], root[:], 0.5, 1e-12, ALU.mult, ALU.max))
            link(nc.vector.reciprocal(inverse[:], root[:]))
            link(nc.vector.tensor_scalar(inverse[:], inverse[:], float(D) ** 0.5, None, ALU.mult))

        @block.scalar
        def _(act):
            act.wait_ge(summed, 1)
            nc.scalar.activation(root[:], total[:], ACT.Sqrt).then_inc(rooted, 1)


def mix1(core):
    nc, a = core.nc, core.a
    heads, dim, mem = 4, 32, 4
    H = heads * dim
    with Phase(nc, "m1") as outer:
        qkv = outer.sb("qkv", [P, NT, 3 * H])
        context = outer.sb("context", [128, H])
        inverse = outer.sb("inverse", [P, NT])
        mid = outer.sb("mid", [P, NT, D])
        row_lengths(core, "m1_len", core.xn, inverse)
        project(core, "m1_qkv", core.xnT, [("L1_mix_w_qkv", 3 * H)], qkv, 3 * H, feature_scale="L1_mix_g_pre", row_scale=inverse)

        with Phase(nc, "m1_sm") as ph:
            top, den = ph.sb("top", [P, NT, heads]), ph.sb("den", [P, NT, heads])
            kbest = ph.sb("kbest", [P, H])
            kcol = ph.sb("kcol", [128, 1])
            diag, ones = ph.sb("diag", [128, H]), ph.sb("ones", [128, P])
            krow = ph.sb("krow", [P, H])
            memkv = ph.sb("memkv", [mem, 2 * H])
            tile = ph.sb("tile", [P, BODY, 2 * H + 1])
            memk, memv = ph.sb("memk", [mem, H]), ph.sb("memv", [mem, H + 1])
            inv = ph.sb("inv", [128, 1])
            loaded, chain_sem = ph.sem("loaded"), ph.sem("chain")
            qshift, qgrown, kmax_set, kturned, diag_set, spread_done = (ph.sem(n) for n in ("qshift", "qgrown", "kmax_set", "kturned", "diag_set", "spread_done"))
            kshift, kgrown, closed, ones_set = (ph.sem(n) for n in ("kshift", "kgrown", "closed", "ones_set"))
            staged, added = ph.done("staged", BODY), ph.done("added", BODY)
            tbank, rbank, cbank = ph.ps("turn"), ph.ps("row"), ph.ps("ctx")
            block = ph.block()
            qs = qkv[:, :, 0:H].rearrange("p t (h d) -> p t h d", h=heads)
            ks = qkv[:, :, H:2 * H]
            wide = [P, NT, heads, dim]

            @block.sync
            def _(sp):
                sp.dma_start(memkv[:].rearrange("m (k c) -> m k c", k=2), a["L1_mix_mem_kv"]).then_inc(loaded, 16)
                sp.wait_ge(loaded, 16)

            @block.vector
            def _(v):
                chain = Chain(v, chain_sem)
                link = chain.link
                link(nc.vector.memset(ones[:], 1.0))
                nc.vector.tensor_reduce(kbest[:], ks.rearrange("p t c -> p c t"), AX.X, ALU.max).then_inc(kmax_set, 1)
                link(nc.vector.tensor_reduce(top[:], qs, AX.X, ALU.max))
                nc.vector.tensor_tensor(qs, qs, bcast_last(top[:], wide), ALU.subtract).then_inc(qshift, 1)
                v.wait_ge(kturned, 1)
                link(nc.vector.tensor_reduce(kcol[:], tbank[:, 0:P + mem], AX.X, ALU.max))
                nc.vector.tensor_scalar(diag[:], core.ident[:], kcol[:, 0:1], None, ALU.mult).then_inc(diag_set, 1)
                v.wait_ge(spread_done, 1)
                link(nc.vector.tensor_copy(krow[:], rbank[0:P, 0:H]))
                link(nc.vector.tensor_tensor(memk[:], memkv[:, 0:H], krow[0:mem, :], ALU.subtract))
                link(nc.vector.tensor_copy(memv[:, 0:H], memkv[:, H:2 * H]))
                link(nc.vector.memset(memv[:, H:H + 1], 1.0))
                nc.vector.tensor_tensor(ks, ks, bcast_mid(krow[:], [P, NT, H]), ALU.subtract).then_inc(kshift, 1)
                v.wait_ge(qgrown, 1)
                link(nc.vector.tensor_reduce(den[:], qs, AX.X, ALU.add))
                link(nc.vector.reciprocal(den[:], den[:]))
                link(nc.vector.tensor_scalar(den[:], den[:], dim ** -0.5, None, ALU.mult))
                link(nc.vector.tensor_tensor(qs, qs, bcast_last(den[:], wide), ALU.mult))
                v.wait_ge(closed, 1)
                link(nc.vector.reciprocal(inv[:], cbank[:, H:H + 1]))
                link(nc.vector.scalar_tensor_tensor(context[:], cbank[:, 0:H], inv[:, 0:1], core.heads[:], ALU.mult, ALU.mult))

            @block.scalar
            def _(act):
                act.wait_ge(qshift, 1)
                nc.scalar.activation(qs, qs, ACT.Exp).then_inc(qgrown, 1)
                act.wait_ge(kshift, 1)
                nc.scalar.activation(memk[:], memk[:], ACT.Exp).then_inc(kgrown, 1)
                nc.scalar.activation(ks, ks, ACT.Exp).then_inc(kgrown, 1)

            @block.gpsimd
            def _(pool):
                staged.open(pool)
                nc.gpsimd.memset(tile[:, :, 2 * H:2 * H + 1], 1.0).then_inc(ones_set, 1)
                pool.wait_ge(kgrown, 2)
                with pool.Fori(0, NODE_LOOPS) as o:
                    for k in range(BODY):
                        ph.hold(pool, added, o, k - BODY)
                        nc.gpsimd.tensor_copy(tile[:, k:k + 1, 0:2 * H], qkv[:, bass.ds(o * BODY + k, 1), H:3 * H]).then_inc(staged.sem, 1)

            @block.tensor
            def _(pe):
                added.open(pe)
                pe.wait_ge(kmax_set, 1)
                pe.wait_ge(loaded, 16)
                nc.tensor.transpose(tbank[:, 0:P], kbest[:], core.ident[0:P, 0:P])
                nc.tensor.transpose(tbank[:, P:P + mem], memkv[:, 0:H], core.ident[0:mem, 0:mem]).then_inc(kturned, 1)
                pe.wait_ge(diag_set, 1)
                nc.tensor.matmul(rbank[0:P, 0:H], ones[:], diag[:], start=True, stop=True).then_inc(spread_done, 1)
                pe.wait_ge(kgrown, 2)
                pe.wait_ge(ones_set, 1)
                nc.tensor.matmul(cbank[:, 0:H + 1], memk[:], memv[:], start=True, stop=False, skip_group_check=True)
                with pe.Fori(0, NODE_LOOPS) as o:
                    for k in range(BODY):
                        ph.hold(pe, staged, o, k)
                        nc.tensor.matmul(cbank[:, 0:H + 1], tile[:, k, 0:H], tile[:, k, H:2 * H + 1], start=False, stop=False, skip_group_check=True).then_inc(added.sem, 1)
                nc.tensor.matmul(cbank[:, 0:H + 1], core.zero[0:P, 0:128], core.zero[0:P, 0:H + 1], start=False, stop=True, skip_group_check=True).then_inc(closed, 1)

        with Phase(nc, "m1_read") as ph:
            wout = ph.sb("wout", [128, D])
            b = ph.sb("b", [P, D])
            tile = ph.sb("tile", [P, BODY, H])
            qT, outT = ph.sb("qT", [128, BODY, P]), ph.sb("outT", [128, BODY, P])
            loaded = ph.sem("loaded")
            staged, turned, qkept, read, okept, result, kept = (ph.done(n, BODY) for n in ("staged", "turned", "qkept", "read", "okept", "result", "kept"))
            banks = [ph.ps(f"bank{k}") for k in range(BODY)]
            block = ph.block()

            @block.sync
            def _(sp):
                sp.dma_start(wout[:], a["L1_mix_w_out"]).then_inc(loaded, 16)
                sp.dma_start(b[:], a["L1_mix_b_out"].partition_broadcast(P)).then_inc(loaded, 16)
                sp.wait_ge(loaded, 32)

            @block.gpsimd
            def _(pool):
                staged.open(pool)
                with pool.Fori(0, NODE_LOOPS) as o:
                    for k in range(BODY):
                        ph.hold(pool, turned, o, k - BODY)
                        nc.gpsimd.tensor_copy(tile[:, k:k + 1, :], qkv[:, bass.ds(o * BODY + k, 1), 0:H]).then_inc(staged.sem, 1)

            @block.tensor
            def _(pe):
                for d in (turned, read, result):
                    d.open(pe)
                pe.wait_ge(loaded, 32)
                with pe.Fori(0, NODE_LOOPS) as o:
                    for k in range(BODY):
                        ph.hold(pe, staged, o, k)
                        ph.hold(pe, kept, o, k - BODY)
                        nc.tensor.transpose(banks[k][:, 0:P], tile[:, k, :], core.ident[0:P, 0:P]).then_inc(turned.sem, 1)
                    for k in range(BODY):
                        ph.hold(pe, qkept, o, k)
                        nc.tensor.matmul(banks[k][:, 128:128 + P], context[:], qT[:, k, :], start=True, stop=True).then_inc(read.sem, 1)
                    for k in range(BODY):
                        ph.hold(pe, okept, o, k)
                        nc.tensor.matmul(banks[k][0:P, 256:512], outT[:, k, :], wout[:], start=True, stop=True).then_inc(result.sem, 1)

            @block.scalar
            def _(act):
                qkept.open(act)
                okept.open(act)
                with act.Fori(0, NODE_LOOPS) as o:
                    for k in range(BODY):
                        ph.hold(act, turned, o, k)
                        ph.hold(act, read, o, k - BODY)
                        nc.scalar.activation(qT[:, k, :], banks[k][:, 0:P], ACT.Copy).then_inc(qkept.sem, 1)
                    for k in range(BODY):
                        ph.hold(act, read, o, k)
                        ph.hold(act, result, o, k - BODY)
                        nc.scalar.activation(outT[:, k, :], banks[k][:, 128:128 + P], ACT.Copy).then_inc(okept.sem, 1)

            @block.vector
            def _(v):
                kept.open(v)
                v.wait_ge(loaded, 32)
                with v.Fori(0, NODE_LOOPS) as o:
                    for k in range(BODY):
                        ph.hold(v, result, o, k)
                        nc.vector.tensor_tensor(mid[:, bass.ds(o * BODY + k, 1), :], banks[k][0:P, 256:512].unsqueeze(1), b[:].unsqueeze(1), ALU.add).then_inc(kept.sem, 1)

        row_lengths(core, "m1_len2", mid, inverse)
        with Phase(nc, "m1_end") as ph:
            g = ph.sb("g", [P, D])
            loaded, chain_sem = ph.sem("loaded"), ph.sem("chain")
            block = ph.block()

            @block.sync
            def _(sp):
                sp.dma_start(g[:], a["L1_mix_g_out"].partition_broadcast(P)).then_inc(loaded, 16)
                sp.wait_ge(loaded, 16)

            @block.vector
            def _(v):
                link = Chain(v, chain_sem).link
                link(nc.vector.tensor_tensor(mid[:], mid[:], bcast_last(inverse[:], [P, NT, D]), ALU.mult))
                v.wait_ge(loaded, 16)
                link(nc.vector.tensor_tensor(mid[:], mid[:], bcast_mid(g[:], [P, NT, D]), ALU.mult))
                link(nc.vector.tensor_tensor(mid[:], mid[:], core.xn[:], ALU.add))
                link(nc.vector.tensor_tensor(core.x[:], core.x[:], mid[:], ALU.add))


def gnn2(core):
    nc, a = core.nc, core.a
    heads, dim = 8, 32
    full = D + 2 * heads
    table, logits, kept = core.table("h2", N, full), core.table("logits2", N, 2 * heads), core.table("kept2", ET * P, D)
    tables = [core.table(f"sum2_{i}", N + P, D + heads) for i in range(TABLES)]
    clear_tables(core, "clear2", tables)
    wide = [P, NT, heads, dim]
    with Phase(nc, "g2") as outer:
        alpha = outer.sb("alpha", [P, ET, heads])
        own = outer.sb("own", [P, NT, heads])
        with Phase(nc, "g2a") as inner:
            dest = inner.sb("dest", [P, NT, D])
            project(core, "g2_h", core.xnT, [("L2_gnn_W", D)], dest, D, bias=[("L2_gnn_b", D)], table=table[:, 0:D])
            with Phase(nc, "g2_logit") as ph:
                prod = ph.sb("prod", [P, NT, D])
                av = ph.sb("av", [P, 2, D])
                both = ph.sb("both", [P, NT, 2 * heads])
                loaded, made, saved, chain_sem = ph.sem("loaded"), ph.sem("made"), ph.sem("saved"), ph.sem("chain")
                block = ph.block()

                @block.sync
                def _(sp):
                    for i, n in enumerate(("src", "trg")):
                        sp.dma_start(av[:, i, :], a["L2_gnn_a_" + n].partition_broadcast(P)).then_inc(loaded, 16)
                    sp.wait_ge(loaded, 32)
                    sp.wait_ge(made, 1)
                    sp.dma_start(nodes(logits), both[:]).then_inc(saved, 16)
                    sp.dma_start(nodes(table[:, D:full]), both[:]).then_inc(saved, 16)
                    sp.wait_ge(saved, 32)

                @block.vector
                def _(v):
                    link = Chain(v, chain_sem).link
                    v.wait_ge(loaded, 32)
                    for i in range(2):
                        link(nc.vector.tensor_tensor(prod[:], dest[:], bcast_mid(av[:, i, :], [P, NT, D]), ALU.mult))
                        link(nc.vector.tensor_reduce(both[:, :, i * heads:(i + 1) * heads], prod[:].rearrange("p t (h d) -> p t h d", h=heads), AX.X, ALU.add))
                    nc.vector.tensor_tensor(own[:], both[:, :, 0:heads], both[:, :, heads:2 * heads], ALU.add).then_inc(made, 1)

        def score(ph, v, chain, srow, drow, _, edge):
            return nc.vector.tensor_tensor(alpha[:, bass.ds(edge, 1), :], srow[:, D:D + heads].unsqueeze(1), drow[:, heads:2 * heads].unsqueeze(1), ALU.add)

        edge_scores(core, "g2_sc", table, core.src, logits, core.dst, full, 2 * heads, score, kept, slice(0, D))
        with Phase(nc, "g2_exp") as ph:
            best = ph.sb("best", [P, 2])
            diag, ones = ph.sb("diag", [P, 2, P]), ph.sb("ones", [P, P])
            top = ph.sb("top", [P, 1])
            chain_sem, diag_set, spread_done, shifted = ph.sem("chain"), ph.sem("diag_set"), ph.sem("spread_done"), ph.sem("shifted")
            bank = ph.ps("bank")
            block = ph.block()

            @block.vector
            def _(v):
                link = Chain(v, chain_sem).link
                link(nc.vector.memset(ones[:], 1.0))
                for ap, i in ((alpha, 0), (own, 1)):
                    link(nc.vector.scalar_tensor_tensor(ap[:], ap[:], 0.2, ap[:], ALU.mult, ALU.max))
                    link(nc.vector.tensor_reduce(best[:, i:i + 1], ap[:], AX.XY, ALU.max))
                link(nc.vector.tensor_scalar(diag[:, 0, :], core.ident[0:P, 0:P], best[:, 0:1], None, ALU.mult))
                nc.vector.tensor_scalar(diag[:, 1, :], core.ident[0:P, 0:P], best[:, 1:2], None, ALU.mult).then_inc(diag_set, 1)
                v.wait_ge(spread_done, 1)
                link(nc.vector.tensor_reduce(top[:], bank[0:P, 0:2 * P], AX.X, ALU.max))
                link(nc.vector.tensor_scalar(own[:], own[:], top[:, 0:1], None, ALU.subtract))
                nc.vector.tensor_scalar(alpha[:], alpha[:], top[:, 0:1], None, ALU.subtract).then_inc(shifted, 1)

            @block.tensor
            def _(pe):
                pe.wait_ge(diag_set, 1)
                nc.tensor.matmul(bank[0:P, 0:2 * P], ones[:], diag[:], start=True, stop=True).then_inc(spread_done, 1)

            @block.scalar
            def _(act):
                act.wait_ge(shifted, 1)
                nc.scalar.activation(alpha[:], alpha[:], ACT.Exp)
                nc.scalar.activation(own[:], own[:], ACT.Exp)

        spread(core, "g2_sp", kept, None, a["dst_rows"], core.dstf, core.dst_once, tables, alpha=alpha, heads=heads)
        own_kept = own
        with Phase(nc, "g2_fin") as ph:
            table_sum = TableSum(ph, tables, D + heads)
            parts = table_sum.parts
            den = ph.sb("den", [P, NT, heads])
            back, chain_sem = ph.sem("back"), ph.sem("chain")
            block = ph.block()
            hprime = parts[1][:, :, 0:D]

            @block.sync
            def _(sp):
                table_sum.load(sp)
                sp.wait_ge(table_sum.added, TABLES - 1)
                sp.dma_start(hprime, nodes(table[:, 0:D])).then_inc(back, 16)
                sp.wait_ge(back, 16)

            @block.vector
            def _(v):
                link = Chain(v, chain_sem).link
                hd = lambda ap: ap.rearrange("p t (h d) -> p t h d", h=heads)
                table_sum.add(v, nc)
                link(nc.vector.tensor_tensor(den[:], parts[0][:, :, D:D + heads], own[:], ALU.add))
                link(nc.vector.tensor_scalar(den[:], den[:], 1e-10, None, ALU.add))
                link(nc.vector.reciprocal(den[:], den[:]))
                v.wait_ge(back, 16)
                link(nc.vector.tensor_tensor(hd(hprime), hd(hprime), bcast_last(own[:], wide), ALU.mult))
                link(nc.vector.tensor_tensor(parts[0][:, :, 0:D], parts[0][:, :, 0:D], hprime, ALU.add))
                link(nc.vector.tensor_tensor(hd(parts[0][:, :, 0:D]), hd(parts[0][:, :, 0:D]), bcast_last(den[:], wide), ALU.mult))
                link(nc.vector.tensor_tensor(core.x[:], core.x[:], parts[0][:, :, 0:D], ALU.add))


def norm_of(layer):
    return lambda core: layer_norm(core, f"ln{layer}", core.x, core.xn, core.xnT)


COLUMNS = ["L0_mix_bq", "L0_mix_b1", "L0_ffn_b1", "L1_ffn_gamma", "L1_ffn_beta", "L1_gnn_query_emb", "L1_mix_g_pre"]
EXPERT_COLUMNS = ["L1_ffn_b1", "L3_ffn_b1"] + [f"L2_ffn_{n}{i}" for i in (1, 2) for n in ("b", "g", "be", "m", "v")]
PHASES = [
    ("load", load_all),
    ("ln0", norm_of(0)), ("gnn0", gnn0), ("mix0", mix0), ("ffn0", ffn0),
    ("ln1", norm_of(1)), ("gnn1", gnn1), ("mix1", mix1), ("ffn1", ffn1),
    ("ln2", norm_of(2)), ("gnn2", gnn2), ("mix2", mix2), ("ffn2", ffn2),
    ("ln3", norm_of(3)), ("gnn3", gnn3), ("mix3", mix3), ("ffn3", ffn3),
]


def program(nc, a, out, stop=None):
    with ExitStack() as stack:
        core = Core(nc, a, stack)
        for name, phase in PHASES:
            phase(core)
            if name == stop:
                break
        with Phase(nc, "store") as ph:
            stored = ph.sem("stored")
            block = ph.block()

            @block.sync
            def _(sp):
                sp.dma_start(nodes(out), core.x[:]).then_inc(stored, 16)
                sp.wait_ge(stored, 16)


def kernel(**inputs):
    import numpy as np
    import concourse.bacc as bacc
    from concourse.bass_utils import run_bass_kernel_spmd as run

    def column(v):
        return v.reshape(-1, 128).T

    arrays = {name: np.asarray(v) for name, v in inputs.items()}
    arrays["src_rows"] = arrays["src"].reshape(P, ET).T.reshape(-1)
    arrays["dst_rows"] = arrays["dst"].reshape(P, ET).T.reshape(-1)
    arrays["type_rows"] = arrays["edge_type_64"].reshape(P, ET).T.reshape(-1)
    for name in ("src", "dst", "edge_weight"):
        arrays[name] = arrays[name].reshape(P, ET)
    for name in ("L0_gnn_W", "L2_mix_Wq", "L2_mix_Wkv", "L2_mix_Wproj", "L3_ffn_router_w"):
        arrays[name] = arrays[name].T
    arrays["L1_mix_mem_kv"] = arrays["L1_mix_mem_kv"].reshape(2, 128, 4).transpose(2, 0, 1)
    for name in ("L2_gnn_a_src", "L2_gnn_a_trg"):
        arrays[name] = arrays[name].reshape(D)
    for name in COLUMNS:
        arrays[name] = column(arrays[name])
    for name in EXPERT_COLUMNS:
        v = arrays[name]
        arrays[name] = v.reshape(v.shape[0], -1, 128).transpose(2, 0, 1)
    arrays["c_ident"] = np.eye(128, dtype=np.float32)
    arrays["c_heads"] = np.kron(np.eye(4), np.ones((32, 32))).astype(np.float32)
    arrays["c_iota8"] = np.tile(np.arange(8, dtype=np.float32), (P, 1))
    arrays["c_earlier"] = np.tril(np.ones((P, P), np.float32), -1)
    arrays["c_spare"] = (N + np.arange(P, dtype=np.float32))[:, None]
    arrays["c_types"] = np.arange(64, dtype=np.float32)[:, None]

    nc = bacc.Bacc("TRN2", target_bir_lowering=False, num_devices=1)
    given, a = {}, {}
    for name, v in arrays.items():
        if name == "L1_mix_t":
            continue
        v = np.ascontiguousarray(v)
        given["in_" + name] = v
        a[name] = nc.dram_tensor("in_" + name, v.shape, mybir.dt.from_np(v.dtype), kind="ExternalInput").ap()
    out = nc.dram_tensor("out", (N, D), F32, kind="ExternalOutput").ap()
    program(nc, a, out)
    result = run(nc, [given], core_ids=[0])
    return result.results[0]["out"]
```

```python
from contextlib import ExitStack

import concourse.bass as bass
from concourse import mybir

F32 = mybir.dt.float32
I32 = mybir.dt.int32
ALU = mybir.AluOpType
ACT = mybir.ActivationFunctionType
AX = mybir.AxisListType

N = 3125
D = 256
P = 125
NT = N // P
NE = 53125
ET = NE // P
DC = D // 128
BODY = 5
NODE_LOOPS = NT // BODY
EBODY = 17
EDGE_LOOPS = ET // EBODY
EBANKS = 5
RUNS = [(0, 3), (3, 2)]
RUNMAX = 3 * P
TABLES = [3, 6, 6, 3]
PARTS = 3
LN_EPS = 1e-5
BANK = 512


class Done:

    def __init__(self, sem, per_body):
        self.sem, self.per_body = sem, per_body

    def open(self, eng):
        eng.sem_inc(self.sem, self.per_body)

    def at(self, step, index):
        return (step + 1) * self.per_body + (index + 1)


class Chain:

    def __init__(self, eng, sem, per_body=0, step=None, base=0):
        self.eng, self.sem, self.per_body, self.step, self.base, self.n = eng, sem, per_body, step, base, 0

    def __call__(self, ins):
        ins.then_inc(self.sem, 1)
        self.n += 1

    def settle(self, count=None):
        value = self.base + (self.n if count is None else count)
        if self.step is not None:
            value = self.step * self.per_body + value
        self.eng.wait_ge(self.sem, value)

    def link(self, ins):
        self(ins)
        self.settle()


class Phase:

    def __init__(self, nc, name):
        self.nc, self.name, self.stack = nc, name, ExitStack()

    def __enter__(self):
        self.stack.__enter__()
        self.sems = []
        self.stack.callback(self.release)
        self.spent = self.sem("spent")
        return self

    def release(self):
        self.nc.clear_and_free_semaphores(self.sems)
        self.nc.all_engine_barrier()

    def __exit__(self, *a):
        return self.stack.__exit__(*a)

    def sb(self, name, shape, dtype=F32):
        return self.stack.enter_context(self.nc.sbuf_tensor(f"{self.name}_{name}", shape, dtype))

    def ps(self, name):
        return self.stack.enter_context(self.nc.psum_tensor(f"{self.name}_{name}", [128, BANK], F32))

    def sem(self, name):
        self.sems.append(self.nc.alloc_semaphore(name=f"{self.name}_{name}"))
        return self.sems[-1]

    def done(self, name, per_body):
        return Done(self.sem(name), per_body)

    def block(self):
        return self.stack.enter_context(self.nc.Block())

    def hold(self, eng, done, step, index):
        eng.wait_ge(done.sem, done.at(step, index))
        eng.sem_inc(self.spent, 1)

    def hold_dma(self, eng, sem, step, count=1):
        eng.wait_ge(sem, step * 16 * count + 16 * count)
        eng.sem_inc(self.spent, 1)


def slot_owner(slots, per_body, index):
    if index >= slots:
        return index - slots
    return max(i for i in range(per_body) if i % slots == index % slots) - per_body


def bcast_mid(ap, shape):
    return ap.unsqueeze(1).to_broadcast(shape)


def bcast_last(ap, shape):
    return ap.unsqueeze(len(shape) - 1).to_broadcast(shape)


def columns(tile, count=1):
    return bass.ds(tile * P, count * P)


def feature_rows(w):
    return w.rearrange("(c p) n -> p c n", p=128)


def feature_column(v):
    return v


class Core:

    def __init__(self, nc, a, stack):
        self.nc, self.a = nc, a

        def sb(name, shape, dtype=F32):
            return stack.enter_context(nc.sbuf_tensor(name, shape, dtype))

        self.x = sb("x", [P, NT, D])
        self.xn = sb("xn", [P, NT, D])
        self.xnT = sb("xnT", [128, DC, N])
        self.ident = sb("ident", [128, 128])
        self.heads = sb("heads", [128, 128])
        self.iota8 = sb("iota8", [P, 8])
        self.zero = sb("zero", [P, 264])
        self.src = sb("src", [P, ET], I32)
        self.dst = sb("dst", [P, ET], I32)
        self.srcf = sb("srcf", [P, ET])
        self.dstf = sb("dstf", [P, ET])
        self.src_once = sb("src_once", [P, ET], I32)
        self.dst_once = sb("dst_once", [P, ET], I32)
        self.weight = sb("weight", [P, ET])
        self.sums = [[self.table(f"sum{layer}_{i}", N + P, D + heads) for i in range(TABLES[layer])] for layer, heads in enumerate((0, 4, 8, 0))]

    def table(self, name, rows, width):
        return self.nc.dram_tensor(name, (rows, width), F32, kind="Internal").ap()


def nodes(ap):
    return ap.rearrange("(p t) d -> p t d", t=NT)


def load_all(core):
    nc, a = core.nc, core.a
    with Phase(nc, "load") as ph:
        loaded, zeroed, converted = ph.sem("loaded"), ph.sem("zeroed"), ph.sem("converted")
        block = ph.block()

        @block.sync
        def _(sp):
            sp.dma_start(core.x[:], nodes(a["x"])).then_inc(loaded, 16)
            for buf, name in ((core.src, "src"), (core.dst, "dst"), (core.weight, "edge_weight"), (core.ident, "c_ident"),
                              (core.heads, "c_heads"), (core.iota8, "c_iota8")):
                sp.dma_start(buf[:], a[name]).then_inc(loaded, 16)
            sp.wait_ge(loaded, 16 * 7)

        @block.vector
        def _(v):
            nc.vector.memset(core.zero[:], 0.0).then_inc(zeroed, 1)
            v.wait_ge(loaded, 16 * 7)
            nc.vector.tensor_copy(core.srcf[:], core.src[:]).then_inc(converted, 1)
            nc.vector.tensor_copy(core.dstf[:], core.dst[:]).then_inc(converted, 1)


class Marks:

    LINKS = EBODY + 4

    def __init__(self, core, ph, keyf, once):
        self.core, self.ph, self.keyf, self.once = core, ph, keyf, once
        self.earlier, self.spare = ph.sb("earlier", [P, P]), ph.sb("spare", [P, 1])
        self.before = ph.sb("before", [P, EBODY, P])
        self.count, self.shift = ph.sb("count", [P, EBODY]), ph.sb("shift", [P, EBODY])
        self.const, self.marked = ph.sem("mark_const"), ph.done("marked", 1)

    def load(self, sp):
        sp.dma_start(self.earlier[:], self.core.a["c_earlier"]).then_inc(self.const, 16)
        sp.dma_start(self.spare[:], self.core.a["c_spare"]).then_inc(self.const, 16)
        sp.wait_ge(self.const, 32)

    def compare(self, chain, keys, o, k):
        chain(self.core.nc.vector.scalar_tensor_tensor(self.before[:, k, :], keys, self.keyf[:, bass.ds(o * EBODY + k, 1)], self.earlier[:],
                                                       ALU.is_equal, ALU.mult))

    def finish(self, v, chain, o):
        nc = self.core.nc
        mine = bass.ds(o * EBODY, EBODY)

        def link(ins):
            chain.link(ins)
            v.sem_inc(self.ph.spent, 1)

        chain.settle()
        v.sem_inc(self.ph.spent, 1)
        link(nc.vector.tensor_reduce(self.count[:], self.before[:], AX.X, ALU.add))
        chain(nc.vector.tensor_scalar(self.count[:], self.count[:], 0.0, None, ALU.is_gt))
        link(nc.vector.tensor_scalar(self.shift[:], self.keyf[:, mine], self.spare[:, 0:1], -1.0, ALU.subtract, ALU.mult))
        link(nc.vector.tensor_tensor(self.shift[:], self.shift[:], self.count[:], ALU.mult))
        nc.vector.tensor_tensor(self.once[:, mine], self.keyf[:, mine], self.shift[:], ALU.add).then_inc(self.marked.sem, 1)


def clear(core, sp, tables, cleared):
    for t in tables:
        width = t.shape[1]
        sp.dma_start(t.rearrange("(p t) d -> p t d", p=P),
                     core.zero[:, 0:width].unsqueeze(1).to_broadcast([P, NT + 1, width])).then_inc(cleared, 16)
    if tables:
        sp.wait_ge(cleared, 16 * len(tables))


def layer_norm(core, name, buf, out, outT=None, rows=True, token_affine=None, feature_affine=None, add_to_x=False, add_xn=False, tables=()):
    nc, a = core.nc, core.a
    with Phase(nc, name) as ph:
        halves = ph.sb("halves", [P, NT, 6])
        stat = ph.sb("stat", [P, 5, NT])
        tile = ph.sb("tile", [P, BODY, D])
        mean, var, rstd, half, gap = (stat[:, i, :] for i in range(5))
        gamma = beta = gcol = bcol = None
        loads = []
        if token_affine:
            gamma, beta = ph.sb("gamma", [P, D]), ph.sb("beta", [P, D])
            loads = [(gamma, a[token_affine[0]].partition_broadcast(P)), (beta, a[token_affine[1]].partition_broadcast(P))]
        if feature_affine:
            gcol, bcol = ph.sb("gcol", [128, DC]), ph.sb("bcol", [128, DC])
            loads = [(gcol, a[feature_affine[0]]), (bcol, a[feature_affine[1]])]
        loaded, chain_sem, cleared = ph.sem("loaded"), ph.sem("chain"), ph.sem("cleared")
        inverse_ready, root_ready = ph.sem("inverse_ready"), ph.sem("root_ready")
        measured, normed = ph.done("measured", BODY), ph.done("normed", BODY)
        staged, turned, stored, taken = (ph.done(n, BODY) for n in ("staged", "turned", "stored", "taken"))
        banks = [ph.ps(f"bank{k}") for k in range(BODY)] if outT is not None else []
        block = ph.block()

        @block.sync
        def _(sp):
            for to, what in loads:
                sp.dma_start(to[:], what).then_inc(loaded, 16)
            if loads:
                sp.wait_ge(loaded, 16 * len(loads))
            clear(core, sp, tables, cleared)

        @block.vector
        def _(v):
            measured.open(v)
            with v.Fori(0, NODE_LOOPS) as o:
                for k in range(BODY):
                    one = bass.ds(o * BODY + k, 1)
                    nc.vector.bn_stats(halves[:, one, :].rearrange("p o s -> p (o s)"), buf[:, one, :].rearrange("p o d -> p (o d)")).then_inc(measured.sem, 1)
            v.wait_ge(measured.sem, measured.at(NODE_LOOPS - 1, BODY - 1))
            chain = Chain(v, chain_sem)
            link = chain.link
            mean_e, dev_e, mean_o, dev_o = (halves[:, :, i] for i in (1, 2, 4, 5))
            chain(nc.vector.tensor_tensor(mean, mean_e, mean_o, ALU.add))
            chain(nc.vector.tensor_tensor(gap, mean_e, mean_o, ALU.subtract))
            link(nc.vector.tensor_tensor(var, dev_e, dev_o, ALU.add))
            chain(nc.vector.tensor_scalar(mean, mean, 0.5, None, ALU.mult))
            chain(nc.vector.tensor_tensor(gap, gap, gap, ALU.mult))
            link(nc.vector.tensor_scalar(var, var, 1.0 / D, LN_EPS, ALU.mult, ALU.add))
            link(nc.vector.scalar_tensor_tensor(var, gap, 0.25, var, ALU.mult, ALU.add))
            nc.vector.reciprocal(half, var).then_inc(inverse_ready, 1)
            v.wait_ge(root_ready, 1)
            link(nc.vector.tensor_tensor(half, rstd, rstd, ALU.mult))
            link(nc.vector.tensor_tensor(half, half, var, ALU.mult))
            link(nc.vector.tensor_scalar(half, half, -0.5, 1.5, ALU.mult, ALU.add))
            link(nc.vector.tensor_tensor(rstd, rstd, half, ALU.mult))
            if loads:
                v.wait_ge(loaded, 16 * len(loads))
            if outT is None:
                normed.open(v)
                with v.Fori(0, NODE_LOOPS) as o:
                    for k in range(BODY):
                        one = bass.ds(o * BODY + k, 1)
                        nc.vector.tensor_scalar(out[:, one, :], buf[:, one, :], mean[:, one], rstd[:, one], ALU.subtract, ALU.mult).then_inc(normed.sem, 1)
                v.wait_ge(normed.sem, normed.at(NODE_LOOPS - 1, BODY - 1))
                shape = [P, NT, D]
                if token_affine:
                    link(nc.vector.tensor_tensor(out[:], out[:], bcast_mid(gamma[:], shape), ALU.mult))
                    link(nc.vector.tensor_tensor(out[:], out[:], bcast_mid(beta[:], shape), ALU.add))
                if add_xn:
                    link(nc.vector.tensor_tensor(out[:], out[:], core.xn[:], ALU.add))
                if add_to_x:
                    link(nc.vector.tensor_tensor(core.x[:], core.x[:], out[:], ALU.add))
                return
            staged.open(v)
            taken.open(v)
            base = chain.n
            per_body = 2 * BODY if token_affine else 0
            with v.Fori(0, NODE_LOOPS) as o:
                chain = Chain(v, chain_sem, per_body, o, base)
                for k in range(BODY):
                    one = bass.ds(o * BODY + k, 1)
                    ph.hold(v, turned, o, k - BODY)
                    if rows or add_to_x:
                        ph.hold(v, taken, o, k - BODY)
                    ins = nc.vector.tensor_scalar(tile[:, k:k + 1, :], buf[:, one, :], mean[:, one], rstd[:, one], ALU.subtract, ALU.mult)
                    if token_affine:
                        chain(ins)
                    else:
                        ins.then_inc(staged.sem, 1)
                if token_affine:
                    for k in range(BODY):
                        chain.settle(k + 1)
                        v.sem_inc(ph.spent, 1)
                        chain(nc.vector.tensor_tensor(tile[:, k, :], tile[:, k, :], gamma[:], ALU.mult))
                    for k in range(BODY):
                        chain.settle(BODY + k + 1)
                        v.sem_inc(ph.spent, 1)
                        nc.vector.tensor_tensor(tile[:, k, :], tile[:, k, :], beta[:], ALU.add).then_inc(staged.sem, 1)
                for k in range(BODY):
                    one = bass.ds(o * BODY + k, 1)
                    if rows or add_to_x:
                        ph.hold(v, staged, o, k)
                    if rows:
                        nc.vector.tensor_copy(out[:, one, :], tile[:, k:k + 1, :]).then_inc(taken.sem, 1)
                    if add_to_x:
                        nc.vector.tensor_tensor(core.x[:, one, :], core.x[:, one, :], tile[:, k:k + 1, :], ALU.add).then_inc(taken.sem, 1)
                assert chain.n == per_body

        @block.scalar
        def _(act):
            act.wait_ge(inverse_ready, 1)
            nc.scalar.activation(rstd, half, ACT.Sqrt).then_inc(root_ready, 1)
            if outT is None:
                return
            stored.open(act)
            if loads:
                act.wait_ge(loaded, 16 * len(loads))
            with act.Fori(0, NODE_LOOPS) as o:
                for k in range(BODY):
                    ph.hold(act, turned, o, k)
                    there = outT[:, :, columns(o * BODY + k)]
                    if feature_affine:
                        for c in range(DC):
                            ins = nc.scalar.activation(there[:, c, :], banks[k][:, c * P:(c + 1) * P], ACT.Identity,
                                                       scale=gcol[:, c:c + 1], bias=bcol[:, c:c + 1])
                    else:
                        ins = nc.scalar.activation(there, banks[k][:, 0:DC * P].rearrange("p (c n) -> p c n", c=DC), ACT.Copy)
                    ins.then_inc(stored.sem, 1)

        if outT is None:
            return

        @block.tensor
        def _(pe):
            turned.open(pe)
            with pe.Fori(0, NODE_LOOPS) as o:
                for k in range(BODY):
                    ph.hold(pe, staged, o, k)
                    ph.hold(pe, stored, o, k - BODY)
                    for c in range(DC):
                        ins = nc.tensor.transpose(banks[k][:, c * P:(c + 1) * P], tile[:, k, c * 128:(c + 1) * 128], core.ident[0:P, 0:P])
                    ins.then_inc(turned.sem, 1)


def project(core, name, inT, weights, dest, width, bias=None, table=None, feature_scale=None, row_scale=None):
    nc, a = core.nc, core.a
    with Phase(nc, name) as ph:
        w = ph.sb("w", [128, DC, width])
        tile = ph.sb("tile", [128, BODY, DC, P])
        b = ph.sb("b", [P, width]) if bias else None
        fs = ph.sb("fs", [128, DC]) if feature_scale else None
        loaded, saved, scaled = ph.sem("loaded"), ph.sem("saved"), ph.sem("scaled")
        staged, product, kept = ph.done("staged", BODY), ph.done("product", BODY), ph.done("kept", BODY)
        banks = [ph.ps(f"bank{k}") for k in range(BODY)]
        nload = len(weights) + (len(bias) if bias else 0) + (1 if feature_scale else 0)
        block = ph.block()

        @block.sync
        def _(sp):
            at = 0
            for wname, n in weights:
                sp.dma_start(w[:, :, at:at + n], feature_rows(a[wname])).then_inc(loaded, 16)
                at += n
            at = 0
            for bname, n in bias or []:
                sp.dma_start(b[:, at:at + n], a[bname].partition_broadcast(P)).then_inc(loaded, 16)
                at += n
            if feature_scale:
                sp.dma_start(fs[:], a[feature_scale]).then_inc(loaded, 16)
            sp.wait_ge(loaded, 16 * nload)
            if table is not None:
                sp.wait_ge(kept.sem, kept.at(NODE_LOOPS - 1, BODY - 1))
                sp.dma_start(nodes(table), dest[:]).then_inc(saved, 16)
                sp.wait_ge(saved, 16)

        @block.gpsimd
        def _(pool):
            staged.open(pool)
            with pool.Fori(0, NODE_LOOPS) as o:
                for k in range(BODY):
                    ph.hold(pool, product, o, k - BODY)
                    nc.gpsimd.tensor_copy(tile[:, k, :, :], inT[:, :, columns(o * BODY + k)]).then_inc(staged.sem, 1)

        @block.tensor
        def _(pe):
            product.open(pe)
            pe.wait_ge(loaded, 16 * nload)
            if feature_scale:
                pe.wait_ge(scaled, DC)
            with pe.Fori(0, NODE_LOOPS) as o:
                for k in range(BODY):
                    ph.hold(pe, staged, o, k)
                    ph.hold(pe, kept, o, k - BODY)
                    for c in range(DC):
                        ins = nc.tensor.matmul(banks[k][0:P, 0:width], tile[:, k, c, :], w[:, c, :], start=c == 0, stop=c == DC - 1)
                    ins.then_inc(product.sem, 1)

        if row_scale is not None:
            @block.vector
            def _(v):
                kept.open(v)
                v.wait_ge(loaded, 16 * nload)
                for c in range(DC):
                    nc.vector.tensor_scalar(w[:, c, :], w[:, c, :], fs[:, c:c + 1], None, ALU.mult).then_inc(scaled, 1)
                with v.Fori(0, NODE_LOOPS) as o:
                    for k in range(BODY):
                        ph.hold(v, product, o, k)
                        nc.vector.tensor_scalar(dest[:, bass.ds(o * BODY + k, 1), :], banks[k][0:P, 0:width].unsqueeze(1),
                                                row_scale[:, bass.ds(o * BODY + k, 1)], None, ALU.mult).then_inc(kept.sem, 1)
        elif bias:
            @block.vector
            def _(v):
                kept.open(v)
                v.wait_ge(loaded, 16 * nload)
                with v.Fori(0, NODE_LOOPS) as o:
                    for k in range(BODY):
                        ph.hold(v, product, o, k)
                        nc.vector.tensor_tensor(dest[:, bass.ds(o * BODY + k, 1), :], banks[k][0:P, 0:width].unsqueeze(1),
                                                b[:].unsqueeze(1), ALU.add).then_inc(kept.sem, 1)
        else:
            @block.scalar
            def _(act):
                kept.open(act)
                with act.Fori(0, NODE_LOOPS) as o:
                    for k in range(BODY):
                        ph.hold(act, product, o, k)
                        nc.scalar.activation(dest[:, bass.ds(o * BODY + k, 1), :], banks[k][0:P, 0:width].unsqueeze(1),
                                             ACT.Copy).then_inc(kept.sem, 1)


def spread(core, name, table, gather_index, key_rows, keyf, once, tables, weight=None, alpha=None, heads=0, mark=False):
    nc, a = core.nc, core.a
    width = D + heads
    with Phase(nc, name) as ph:
        gather_at = ph.sb("gather_at", [P, EBODY], I32)
        scatter_at = ph.sb("scatter_at", [P, EBODY], I32)
        rows = ph.sb("rows", [P, EBODY, D])
        keys = ph.sb("keys", [P, EBODY, P], I32)
        same = ph.sb("same", [P, EBODY, P])
        message = ph.sb("message", [P, EBODY, width]) if heads else rows
        total = ph.sb("total", [P, EBODY, width])
        gathered = [ph.sem(f"gathered{k}") for k in range(EBODY)]
        keys_in = ph.sem("keys_in")
        scattered = [ph.sem(f"scattered{k}") for k in range(EBODY)]
        gather_set, scatter_set = ph.done("gather_set", EBODY), ph.done("scatter_set", EBODY)
        compared, scaled = ph.done("compared", EBODY), ph.done("scaled", EBODY)
        summed, total_set = ph.done("summed", EBODY), ph.done("total_set", EBODY)
        banks = [ph.ps(f"bank{k}") for k in range(EBANKS)]
        marks = Marks(core, ph, keyf, once) if mark else None
        chain_sem = ph.sem("chain")
        gathers = gather_index is not None
        last = EDGE_LOOPS - 1
        table_of = [k % len(tables) for k in range(EBODY)]
        block = ph.block()

        @block.sync
        def _(sp):
            if mark:
                marks.load(sp)
            with sp.Fori(0, EDGE_LOOPS) as o:
                ph.hold(sp, compared, o, -1)
                sp.dma_start(keys[:], key_rows[bass.ds(o * EBODY * P, EBODY * P)].partition_broadcast(P)
                             .rearrange("p (k e) -> p k e", k=EBODY)).then_inc(keys_in, 16)
                if not gathers:
                    for k in range(EBODY):
                        ph.hold(sp, scaled if heads else summed, o, k - EBODY)
                        sp.dma_start(rows[:, k, :], table[bass.ds((o * EBODY + k) * P, P), :]).then_inc(gathered[k], 16)

        @block.gpsimd
        def _(pool):
            def gather(k):
                nc.gpsimd.indirect_dma_start(rows[:, k, :], None, table, bass.IndirectOffsetOnAxis(ap=gather_at[:, k:k + 1], axis=0)).then_inc(gathered[k], 16)

            def scatter(o, k):
                ph.hold(pool, scatter_set, o, k)
                ph.hold(pool, total_set, o, k)
                before = max((j for j in range(k) if table_of[j] == table_of[k]), default=None)
                if before is not None:
                    ph.hold_dma(pool, scattered[before], o)
                elif not (isinstance(o, int) and o == 0):
                    ph.hold_dma(pool, scattered[max(j for j in range(EBODY) if table_of[j] == table_of[k])], o - 1)
                nc.gpsimd.indirect_dma_start(tables[table_of[k]], bass.IndirectOffsetOnAxis(ap=scatter_at[:, k:k + 1], axis=0),
                                             total[:, k, :], None, compute_op=ALU.add).then_inc(scattered[k], 16)

            def next_gather(o, k):
                ph.hold(pool, gather_set, o + 1, k)
                ph.hold(pool, scaled if heads else summed, o, k)
                gather(k)

            if gathers:
                for k in range(EBODY):
                    ph.hold(pool, gather_set, 0, k)
                    gather(k)
            for k in range(EBODY):
                scatter(0, k)
                if gathers:
                    next_gather(0, k)
            with pool.Fori(1, last) as o:
                for k in range(EBODY):
                    scatter(o, k)
                    if gathers:
                        next_gather(o, k)
            for k in range(EBODY):
                scatter(last, k)
            for k in range(EBODY):
                pool.wait_ge(scattered[k], 16 * EDGE_LOOPS)

        @block.vector
        def _(v):
            compared.open(v)
            if heads:
                scaled.open(v)
            if mark:
                marks.marked.open(v)
                v.wait_ge(marks.const, 32)
            with v.Fori(0, EDGE_LOOPS) as o:
                chain = Chain(v, chain_sem, Marks.LINKS, o)
                ph.hold_dma(v, keys_in, o)
                for k in range(EBODY):
                    one = bass.ds(o * EBODY + k, 1)
                    if mark:
                        marks.compare(chain, keys[:, k, :], o, k)
                    ph.hold(v, summed, o, k - EBODY)
                    if heads:
                        nc.vector.tensor_scalar(same[:, k, :], keys[:, k, :], keyf[:, one], None, ALU.is_equal).then_inc(compared.sem, 1)
                        ph.hold_dma(v, gathered[k], o)
                        nc.vector.tensor_copy(message[:, k:k + 1, D:width], alpha[:, one, :])
                        nc.vector.tensor_tensor(message[:, k, 0:D].rearrange("p (h d) -> p h d", h=heads), rows[:, k, :].rearrange("p (h d) -> p h d", h=heads),
                                                alpha[:, one, :].rearrange("p o h -> p (o h)").unsqueeze(2).to_broadcast([P, heads, D // heads]), ALU.mult).then_inc(scaled.sem, 1)
                    else:
                        nc.vector.tensor_scalar(same[:, k, :], keys[:, k, :], keyf[:, one], weight[:, one], ALU.is_equal, ALU.mult).then_inc(compared.sem, 1)
                if mark:
                    marks.finish(v, chain, o)
                    assert chain.n == Marks.LINKS

        @block.tensor
        def _(pe):
            summed.open(pe)
            with pe.Fori(0, EDGE_LOOPS) as o:
                for k in range(EBODY):
                    ph.hold(pe, compared, o, k)
                    if heads:
                        ph.hold(pe, scaled, o, k)
                    else:
                        ph.hold_dma(pe, gathered[k], o)
                    ph.hold(pe, total_set, o, slot_owner(EBANKS, EBODY, k))
                    nc.tensor.matmul(banks[k % EBANKS][0:P, 0:width], same[:, k, :], message[:, k, :], start=True, stop=True).then_inc(summed.sem, 1)

        @block.scalar
        def _(act):
            gather_set.open(act)
            scatter_set.open(act)
            total_set.open(act)

            def set_gather(o, k):
                nc.scalar.activation(gather_at[:, k:k + 1], gather_index[:, bass.ds(o * EBODY + k, 1)], ACT.Copy).then_inc(gather_set.sem, 1)

            def finish(o, k):
                if not (isinstance(o, int) and o == 0):
                    ph.hold_dma(act, scattered[k], o - 1)
                if mark and k == 0:
                    ph.hold(act, marks.marked, o, 0)
                nc.scalar.activation(scatter_at[:, k:k + 1], once[:, bass.ds(o * EBODY + k, 1)], ACT.Copy).then_inc(scatter_set.sem, 1)
                ph.hold(act, summed, o, k)
                nc.scalar.activation(total[:, k, :], banks[k % EBANKS][0:P, 0:width], ACT.Copy).then_inc(total_set.sem, 1)

            if gathers:
                for k in range(EBODY):
                    set_gather(0, k)
            for k in range(EBODY):
                finish(0, k)
                if gathers:
                    set_gather(1, k)
            with act.Fori(1, last) as o:
                for k in range(EBODY):
                    finish(o, k)
                    if gathers:
                        set_gather(o + 1, k)
            for k in range(EBODY):
                finish(last, k)


class TableSum:

    def __init__(self, ph, tables, width):
        self.tables = tables
        self.parts = [ph.sb(f"part{i}", [P, NT, width]) for i in range(PARTS)]
        self.part_in = [ph.sem(f"part_in{i}") for i in range(PARTS)]
        self.added = ph.sem("added")
        self.total = self.parts[0]

    def slot(self, i):
        return 0 if i == 0 else 1 + (i - 1) % (PARTS - 1)

    def load(self, sp):
        for i, t in enumerate(self.tables):
            if i >= PARTS:
                sp.wait_ge(self.added, i - (PARTS - 1))
            sp.dma_start(self.parts[self.slot(i)][:], nodes(t[0:N, :])).then_inc(self.part_in[self.slot(i)], 16)

    def add(self, v, nc):
        v.wait_ge(self.part_in[0], 16)
        for i in range(1, len(self.tables)):
            v.wait_ge(self.part_in[self.slot(i)], 16 * (1 + (i - 1) // (PARTS - 1)))
            nc.vector.tensor_tensor(self.total[:], self.total[:], self.parts[self.slot(i)][:], ALU.add).then_inc(self.added, 1)
            v.wait_ge(self.added, i)


def finish_plain(core, name, tables, elu):
    nc = core.nc
    with Phase(nc, name) as ph:
        table_sum = TableSum(ph, tables, D)
        parts = table_sum.parts
        low_ready, grown, chain_sem = ph.sem("low_ready"), ph.sem("grown"), ph.sem("chain")
        block = ph.block()

        @block.sync
        def _(sp):
            table_sum.load(sp)

        @block.vector
        def _(v):
            chain = Chain(v, chain_sem)
            table_sum.add(v, nc)
            if elu:
                nc.vector.tensor_scalar(parts[1][:], parts[0][:], 0.0, None, ALU.min).then_inc(low_ready, 1)
                chain.link(nc.vector.scalar_tensor_tensor(core.x[:], parts[0][:], 0.0, core.x[:], ALU.max, ALU.add))
                v.wait_ge(grown, 1)
                chain.link(nc.vector.scalar_tensor_tensor(core.x[:], parts[1][:], -1.0, core.x[:], ALU.add, ALU.add))
            else:
                chain.link(nc.vector.scalar_tensor_tensor(core.x[:], parts[0][:], 0.0, core.x[:], ALU.max, ALU.add))

        if elu:
            @block.scalar
            def _(act):
                act.wait_ge(low_ready, 1)
                nc.scalar.activation(parts[1][:], parts[1][:], ACT.Exp).then_inc(grown, 1)


def gnn0(core):
    h = core.table("h0", N, D)
    tables = core.sums[0]
    with Phase(core.nc, "g0") as ph:
        dest = ph.sb("h", [P, NT, D])
        project(core, "proj0", core.xnT, [("L0_gnn_W", D)], dest, D, bias=[("L0_gnn_b", D)], table=h)
    spread(core, "spread0", h, core.dst, core.a["src_rows"], core.srcf, core.src_once, tables, weight=core.weight, mark=True)
    finish_plain(core, "fin0", tables, elu=True)


def linear_attention(core, name, wq, wkv, wo, target, bias=None, clamp=None, plus=None, length=1.0, add=True):
    nc, a = core.nc, core.a
    KV = 2 * D
    with Phase(nc, name) as outer:
        context = outer.sb("context", [128, DC, 128])
        keysum = outer.sb("keysum", [128, DC, 128])
        with Phase(nc, name + "_kv") as ph:
            w = ph.sb("w", [128, DC, KV])
            b = ph.sb("b", [P, KV]) if bias else None
            tile = ph.sb("tile", [128, BODY, DC, P])
            kv = ph.sb("kv", [P, BODY, KV + 1])
            low = ph.sb("low", [P, BODY, D])
            grown = ph.sb("grown", [P, BODY, D])
            keymap = ph.sb("keymap", [P, BODY, D])
            loaded, ones, closed = ph.sem("loaded"), ph.sem("ones"), ph.sem("closed")
            staged, product, kept = ph.done("staged", BODY), ph.done("product", BODY), ph.done("kept", BODY)
            low_set, grown_set, mapped, added = ph.done("low_set", BODY), ph.done("grown_set", BODY), ph.done("mapped", BODY), ph.done("added", BODY)
            banks = [ph.ps(f"bank{k}") for k in range(BODY)]
            sums = [ph.ps(f"sums{c}") for c in range(DC)]
            nload = len(wkv) + (2 if bias else 0)
            block = ph.block()

            @block.sync
            def _(sp):
                for i, (wname, cols) in enumerate(wkv):
                    n = KV // len(wkv)
                    sp.dma_start(w[:, :, i * n:(i + 1) * n], feature_rows(a[wname] if cols is None else a[wname][:, cols])).then_inc(loaded, 16)
                if bias:
                    for i in range(2):
                        sp.dma_start(b[:, i * D:(i + 1) * D], a[bias[1 + i]].partition_broadcast(P)).then_inc(loaded, 16)
                sp.wait_ge(loaded, 16 * nload)

            @block.gpsimd
            def _(pool):
                staged.open(pool)
                nc.gpsimd.memset(kv[:, :, KV:KV + 1], 1.0).then_inc(ones, 1)
                with pool.Fori(0, NODE_LOOPS) as o:
                    for k in range(BODY):
                        ph.hold(pool, product, o, k - BODY)
                        nc.gpsimd.tensor_copy(tile[:, k, :, :], core.xnT[:, :, columns(o * BODY + k)]).then_inc(staged.sem, 1)

            @block.tensor
            def _(pe):
                product.open(pe)
                added.open(pe)
                pe.wait_ge(loaded, 16 * nload)
                for c in range(DC):
                    nc.tensor.matmul(sums[c][:, 0:D + 1], core.zero[:, 0:128], core.zero[:, 0:D + 1], start=True, stop=False, skip_group_check=True)
                pe.wait_ge(ones, 1)
                with pe.Fori(0, NODE_LOOPS) as o:
                    for k in range(BODY):
                        ph.hold(pe, staged, o, k)
                        ph.hold(pe, kept, o, k - BODY)
                        for c in range(DC):
                            ins = nc.tensor.matmul(banks[k][0:P, :], tile[:, k, c, :], w[:, c, :], start=c == 0, stop=c == DC - 1)
                        ins.then_inc(product.sem, 1)
                    for k in range(BODY):
                        ph.hold(pe, mapped, o, k)
                        for c in range(DC):
                            ins = nc.tensor.matmul(sums[c][:, 0:D + 1], keymap[:, k, c * 128:(c + 1) * 128], kv[:, k, D:KV + 1],
                                                   start=False, stop=False, skip_group_check=True)
                        ins.then_inc(added.sem, 1)
                for c in range(DC):
                    ins = nc.tensor.matmul(sums[c][:, 0:D + 1], core.zero[:, 0:128], core.zero[:, 0:D + 1], start=False, stop=True, skip_group_check=True)
                ins.then_inc(closed, 1)

            @block.vector
            def _(v):
                kept.open(v)
                low_set.open(v)
                mapped.open(v)
                v.wait_ge(loaded, 16 * nload)
                with v.Fori(0, NODE_LOOPS) as o:
                    for k in range(BODY):
                        ph.hold(v, product, o, k)
                        ph.hold(v, added, o, k - BODY)
                        if bias:
                            nc.vector.tensor_tensor(kv[:, k, 0:KV], banks[k][0:P, :], b[:], ALU.add).then_inc(kept.sem, 1)
                        else:
                            nc.vector.tensor_copy(kv[:, k, 0:KV], banks[k][0:P, :]).then_inc(kept.sem, 1)
                        ph.hold(v, kept, o, k)
                        nc.vector.tensor_scalar(low[:, k, :], kv[:, k, 0:D], 0.0, None, ALU.min).then_inc(low_set.sem, 1)
                    for k in range(BODY):
                        ph.hold(v, grown_set, o, k)
                        nc.vector.scalar_tensor_tensor(keymap[:, k, :], kv[:, k, 0:D], 0.0, grown[:, k, :], ALU.max, ALU.add).then_inc(mapped.sem, 1)
                v.wait_ge(closed, 1)
                for c in range(DC):
                    nc.vector.scalar_tensor_tensor(context[:, c, :], sums[c][:, c * 128:(c + 1) * 128], 1.0 / length, core.heads[:], ALU.mult, ALU.mult)
                    nc.vector.tensor_scalar(keysum[:, c, :], core.heads[:], sums[c][:, D:D + 1], None, ALU.mult)

            @block.scalar
            def _(act):
                grown_set.open(act)
                with act.Fori(0, NODE_LOOPS) as o:
                    for k in range(BODY):
                        ph.hold(act, low_set, o, k)
                        ph.hold(act, mapped, o, k - BODY)
                        nc.scalar.activation(grown[:, k, :], low[:, k, :], ACT.Exp).then_inc(grown_set.sem, 1)

        with Phase(nc, name + "_read") as ph:
            w = ph.sb("w", [128, DC, D])
            wout = ph.sb("wout", [128, DC, D])
            bq = ph.sb("bq", [128, DC])
            low = ph.sb("low", [128, 2, DC, RUNMAX])
            pos = ph.sb("pos", [128, 2, DC, RUNMAX])
            grown = ph.sb("grown", [128, 2, DC, RUNMAX])
            query = ph.sb("query", [128, 2, DC, RUNMAX])
            inverse = ph.sb("inverse", [128, 2, RUNMAX])
            outT = ph.sb("outT", [128, 2, DC, RUNMAX])
            loaded, chain_sem = ph.sem("loaded"), ph.sem("chain")
            projected, low_set, grown_set, mapped = ph.done("projected", 4), ph.done("low_set", 4), ph.done("grown_set", 4), ph.done("mapped", 4)
            read, divided, result, kept = ph.done("read", 4), ph.done("divided", 4), ph.done("result", BODY), ph.done("kept", BODY)
            qbank = [ph.ps(f"q{i}") for i in range(4)]
            numbank, denbank = ph.ps("num"), ph.ps("den")
            obank = [ph.ps(f"o{i}") for i in range(2)]
            nload = 2 + (1 if bias else 0)
            block = ph.block()

            @block.sync
            def _(sp):
                sp.dma_start(w[:], feature_rows(a[wq])).then_inc(loaded, 16)
                sp.dma_start(wout[:], feature_rows(a[wo])).then_inc(loaded, 16)
                if bias:
                    sp.dma_start(bq[:], a[bias[0]]).then_inc(loaded, 16)
                sp.wait_ge(loaded, 16 * nload)

            @block.tensor
            def _(pe):
                projected.open(pe)
                read.open(pe)
                result.open(pe)
                pe.wait_ge(loaded, 16 * nload)
                with pe.Fori(0, NODE_LOOPS) as o:
                    for s, (first, m) in enumerate(RUNS):
                        for mo in range(DC):
                            i = s * DC + mo
                            ph.hold(pe, mapped, o, i - 4)
                            for c in range(DC):
                                ins = nc.tensor.matmul(qbank[i][:, 0:m * P], w[:, c, mo * 128:(mo + 1) * 128],
                                                       core.xnT[:, c, columns(o * BODY + first, m)], start=c == 0, stop=c == DC - 1)
                            ins.then_inc(projected.sem, 1)
                    for s, (first, m) in enumerate(RUNS):
                        for c in range(DC):
                            i = s * DC + c
                            ph.hold(pe, mapped, o, i)
                            ph.hold(pe, divided, o, i - 1)
                            nc.tensor.matmul(numbank[:, 0:m * P], context[:, c, :], query[:, s, c, 0:m * P], start=True, stop=True)
                            nc.tensor.matmul(denbank[:, 0:m * P], keysum[:, c, :], query[:, s, c, 0:m * P], start=True, stop=True).then_inc(read.sem, 1)
                    for s, (first, m) in enumerate(RUNS):
                        ph.hold(pe, divided, o, s * DC + DC - 1)
                        for j in range(m):
                            i = first + j
                            ph.hold(pe, kept, o, i - 2)
                            for c in range(DC):
                                ins = nc.tensor.matmul(obank[i % 2][0:P, 0:D], outT[:, s, c, j * P:(j + 1) * P], wout[:, c, :], start=c == 0, stop=c == DC - 1)
                            if i == BODY - 1:
                                pass
                            ins.then_inc(result.sem, 1)

            @block.vector
            def _(v):
                low_set.open(v)
                mapped.open(v)
                divided.open(v)
                kept.open(v)
                per_body = 2 * 4 + 4
                v.wait_ge(loaded, 16 * nload)
                with v.Fori(0, NODE_LOOPS) as o:
                    chain = Chain(v, chain_sem, per_body, o)
                    for s, (first, m) in enumerate(RUNS):
                        for mo in range(DC):
                            i, n = s * DC + mo, m * P
                            ph.hold(v, projected, o, i)
                            bcol = bq[:, mo:mo + 1] if bias else 0.0
                            chain(nc.vector.tensor_scalar(pos[:, s, mo, 0:n], qbank[i][:, 0:n], bcol, 0.0, ALU.add, ALU.max))
                            nc.vector.tensor_scalar(low[:, s, mo, 0:n], qbank[i][:, 0:n], bcol, 0.0, ALU.add, ALU.min).then_inc(low_set.sem, 1)
                    for s, (first, m) in enumerate(RUNS):
                        for mo in range(DC):
                            i, n = s * DC + mo, m * P
                            ph.hold(v, grown_set, o, i)
                            ph.hold(v, read, o, i - 4)
                            nc.vector.tensor_tensor(query[:, s, mo, 0:n], pos[:, s, mo, 0:n], grown[:, s, mo, 0:n], ALU.add).then_inc(mapped.sem, 1)
                    for s, (first, m) in enumerate(RUNS):
                        for c in range(DC):
                            i, n = s * DC + c, m * P
                            ph.hold(v, read, o, i)
                            if clamp is not None:
                                chain(nc.vector.tensor_scalar(inverse[:, s, 0:n], denbank[:, 0:n], clamp, None, ALU.max))
                            else:
                                chain(nc.vector.tensor_scalar(inverse[:, s, 0:n], denbank[:, 0:n], plus, None, ALU.add))
                            chain.settle()
                            v.sem_inc(ph.spent, 1)
                            chain(nc.vector.reciprocal(inverse[:, s, 0:n], inverse[:, s, 0:n]))
                            chain.settle()
                            v.sem_inc(ph.spent, 1)
                            if c == 0:
                                ph.hold(v, result, o, first + m - 1 - BODY)
                            nc.vector.scalar_tensor_tensor(outT[:, s, c, 0:n], numbank[:, 0:n], length, inverse[:, s, 0:n], ALU.mult, ALU.mult).then_inc(divided.sem, 1)
                    for s, (first, m) in enumerate(RUNS):
                        for j in range(m):
                            i = first + j
                            row = target[:, bass.ds(o * BODY + i, 1), :]
                            ph.hold(v, result, o, i)
                            if add:
                                nc.vector.tensor_tensor(row, row, obank[i % 2][0:P, 0:D].unsqueeze(1), ALU.add).then_inc(kept.sem, 1)
                            else:
                                nc.vector.tensor_scalar(row, obank[i % 2][0:P, 0:D].unsqueeze(1), 0.0, None, ALU.add).then_inc(kept.sem, 1)
                    assert chain.n == per_body

            @block.scalar
            def _(act):
                grown_set.open(act)
                with act.Fori(0, NODE_LOOPS) as o:
                    for s, (first, m) in enumerate(RUNS):
                        for mo in range(DC):
                            i, n = s * DC + mo, m * P
                            ph.hold(act, low_set, o, i)
                            ph.hold(act, mapped, o, i - 4)
                            nc.scalar.activation(grown[:, s, mo, 0:n], low[:, s, mo, 0:n], ACT.Exp).then_inc(grown_set.sem, 1)


def start_rows(core, name, target, source, bias):
    nc, a = core.nc, core.a
    with Phase(nc, name) as ph:
        b = ph.sb("b", [P, D])
        loaded = ph.sem("loaded")
        block = ph.block()

        @block.sync
        def _(sp):
            sp.dma_start(b[:], a[bias].partition_broadcast(P)).then_inc(loaded, 16)
            sp.wait_ge(loaded, 16)

        @block.vector
        def _(v):
            v.wait_ge(loaded, 16)
            nc.vector.tensor_tensor(target[:], (target if source is None else source)[:], bcast_mid(b[:], [P, NT, D]), ALU.add)


def routing(kind):
    first = 5
    return {"soft": 3 + 3, "argmax": 3 + 3 + first + 1, "top2prob": 3 + 3 + 2 * first + 1 + 1 + 5, "top2logit": 3 + 2 * first + 1 + 1 + 4}[kind]


def ffn(core, name, sources, hidden, w1, b1, func, w2, target, experts=1, shared=False, gate=None, kind=None, b2=None, norm=None, before=None, tables=()):
    nc, a = core.nc, core.a
    KC, HC = DC * len(sources), hidden // 128
    groups = 1 if shared else experts
    depth = 2 if norm else 1
    entries = [(s, g) for s in range(2) for g in range(groups)]
    order = []
    for step in range(len(entries) + depth):
        if step < len(entries):
            order.append(("h", 0, step))
        if depth == 2 and 0 <= step - 1 < len(entries):
            order.append(("h", 1, step - 1))
        if 0 <= step - depth < len(entries):
            order.append(("y", None, step - depth))
    hitems, yitems = [], []
    for what, layer, i in order:
        s, g = entries[i]
        if what == "h":
            hitems += [(layer, i, mo) for mo in range(HC)]
        else:
            yitems += [(i, j, e) for e in (range(experts) if shared else [g]) for j in range(RUNS[s][1])]
            if gate and b2 and g == 0:
                yitems += [(i, j, None) for j in range(RUNS[s][1])]
    hindex = {it: q for q, it in enumerate(hitems)}
    yindex = {it: q for q, it in enumerate(yitems)}
    HR, YR = 4, 3
    HB, YB = len(hitems), len(yitems)
    def last_reader(layer, i):
        if layer + 1 < depth:
            return "h", hindex[(layer + 1, i, HC - 1)]
        return "y", max(q for q, it in enumerate(yitems) if it[0] == i and it[2] is not None)
    def last_update(q):
        i, j, _ = yitems[q]
        s = entries[i][0]
        return max((r for r in range(q) if entries[yitems[r][0]][0] == s and yitems[r][1] == j), default=None)

    with Phase(nc, name) as ph:
        W1 = ph.sb("W1", [128, groups, KC, hidden])
        W1b = ph.sb("W1b", [128, groups, HC, hidden]) if norm else None
        W2 = ph.sb("W2", [128, experts, HC, D])
        hid = [ph.sb(f"hid{layer}", [128, 2, HC, RUNMAX]) for layer in range(depth)]
        b1c = ph.sb("b1c", [128, groups, HC])
        loads = []
        for g in range(groups):
            loads.append((W1[:, g], (a[w1] if groups == 1 else a[w1][g]).rearrange("(c p) h -> p c h", p=128)))
        if norm:
            for g in range(groups):
                loads.append((W1b[:, g], a[norm["w"]][g].rearrange("(c p) h -> p c h", p=128)))
            bn = {n: ph.sb("bn_" + n, [128, groups, HC]) for layer in norm["columns"] for n in layer}
            for layer in norm["columns"]:
                for n in layer:
                    loads.append((bn[n][:], a[n]))
            scale = [ph.sb(f"scale{i}", [128, groups, HC]) for i in range(2)]
            shift = [ph.sb(f"shift{i}", [128, groups, HC]) for i in range(2)]
            root = [ph.sb(f"root{i}", [128, groups, HC]) for i in range(2)]
        elif b1:
            loads.append((b1c[:, 0] if groups == 1 else b1c[:], a[b1]))
        for e in range(experts):
            loads.append((W2[:, e], (a[w2] if experts == 1 else a[w2][e]).rearrange("(c p) d -> p c d", p=128)))
        if gate:
            wg = ph.sb("wg", [128, HC if shared else DC, 8])
            bg = ph.sb("bg", [P, 8])
            loads.append((wg[:], feature_rows(a[gate[0]])))
            if gate[1]:
                loads.append((bg[:], a[gate[1]].partition_broadcast(P)))
            if b2:
                b2r = ph.sb("b2r", [8, D])
                loads.append((b2r[:], a[b2]))
            logitT = ph.sb("logitT", [8, 2, RUNMAX])
            comb = ph.sb("comb", [P, 2, 3, 8])
            combT = ph.sb("combT", [8, 2, RUNMAX])
            work = ph.sb("work", [P, 2, 8, 3, 8])
            col = ph.sb("col", [P, 2, 4, 3])
        loaded, chain_sem, cleared = ph.sem("loaded"), ph.sem("chain"), ph.sem("cleared")
        hid_made, hid_kept = ph.done("hid_made", HB), ph.done("hid_kept", HB)
        out_made, out_kept = ph.done("out_made", YB), ph.done("out_kept", YB)
        scored, score_kept, scores_turned = ph.done("scored", 2), ph.done("score_kept", 2), ph.done("scores_turned", 2)
        centred, grown, routed = ph.done("centred", 2), ph.done("grown", 2), ph.done("routed", 2)
        comb_turned, comb_kept = ph.done("comb_turned", 2), ph.done("comb_kept", 2)
        inverse_ready, root_ready, folded = ph.sem("inverse_ready"), ph.sem("root_ready"), ph.sem("folded")
        nload = 16 * len(loads)
        with nc.Block() as prefetch:
            @prefetch.sync
            def _(sp):
                for to, what in loads:
                    sp.dma_start(to, what).then_inc(loaded, 16)

        if before:
            before()
        hbank = [ph.ps(f"h{i}") for i in range(HR)]
        ybank = [ph.ps(f"y{i}") for i in range(YR)]
        gbank = ph.ps("gate") if gate else None
        block = ph.block()

        @block.sync
        def _(sp):
            clear(core, sp, tables, cleared)
            sp.wait_ge(loaded, nload)

        @block.tensor
        def _(pe):
            hid_made.open(pe)
            out_made.open(pe)
            for d in (scored, scores_turned, comb_turned):
                d.open(pe)
            pe.wait_ge(loaded, nload)
            with pe.Fori(0, NODE_LOOPS) as o:
                def score(s):
                    first, m = RUNS[s]
                    ph.hold(pe, comb_kept if b2 else routed, o, s - 1)
                    for c in range(DC):
                        ins = nc.tensor.matmul(gbank[0:8, 0:m * P], wg[:, c, :], sources[0][:, c, columns(o * BODY + first, m)], start=c == 0, stop=c == DC - 1)
                    ins.then_inc(scored.sem, 1)

                def turn_scores(s):
                    ph.hold(pe, score_kept, o, s)
                    for j in range(RUNS[s][1]):
                        ins = nc.tensor.transpose(gbank[0:P, 400 + 8 * j:408 + 8 * j], logitT[:, s, j * P:(j + 1) * P], core.ident[0:8, 0:8])
                    ins.then_inc(scores_turned.sem, 1)

                def score_hidden(s, i):
                    ph.hold(pe, comb_kept if b2 else routed, o, s - 1)
                    ph.hold(pe, hid_kept, o, hindex[(0, i, HC - 1)])
                    for j in range(RUNS[s][1]):
                        for c in range(HC):
                            ins = nc.tensor.matmul(gbank[0:P, 400 + 8 * j:408 + 8 * j], hid[0][:, i % 2, c, j * P:(j + 1) * P], wg[:, c, :], start=c == 0, stop=c == HC - 1)
                    ins.then_inc(scores_turned.sem, 1)

                def turn_comb(s):
                    ph.hold(pe, routed, o, s)
                    for j in range(RUNS[s][1]):
                        ins = nc.tensor.transpose(gbank[0:8, j * P:(j + 1) * P], comb[:, s, j, :], core.ident[0:P, 0:P])
                    ins.then_inc(comb_turned.sem, 1)

                for what, layer, i in order:
                    s, g = entries[i]
                    first, m = RUNS[s]
                    n = m * P
                    if what == "h":
                        if layer == 0 and g == 0 and gate and not shared:
                            score(s)
                        for mo in range(HC):
                            q = hindex[(layer, i, mo)]
                            ph.hold(pe, hid_kept, o, slot_owner(HR, HB, q))
                            if layer == 0:
                                pieces = [(W1[:, g, c, mo * 128:(mo + 1) * 128], sources[c // DC][:, c % DC, columns(o * BODY + first, m)]) for c in range(KC)]
                            else:
                                ph.hold(pe, hid_kept, o, hindex[(0, i, HC - 1)])
                                pieces = [(W1b[:, g, c, mo * 128:(mo + 1) * 128], hid[0][:, i % 2, c, 0:n]) for c in range(HC)]
                            for c, (lhsT, rhs) in enumerate(pieces):
                                ins = nc.tensor.matmul(hbank[q % HR][:, 0:n], lhsT, rhs, start=c == 0, stop=c == len(pieces) - 1)
                            ins.then_inc(hid_made.sem, 1)
                        if layer == 0 and g == 0 and gate and not shared:
                            turn_scores(s)
                    else:
                        if shared and gate:
                            score_hidden(s, i)
                        mine = [q for q, it in enumerate(yitems) if it[0] == i]
                        turned = False
                        for q in mine:
                            _, j, e = yitems[q]
                            if e is None and not turned:
                                turn_comb(s)
                                ph.hold(pe, comb_kept, o, s)
                                turned = True
                            ph.hold(pe, out_kept, o, slot_owner(YR, YB, q))
                            if e is None:
                                ins = nc.tensor.matmul(ybank[q % YR][0:P, 0:D], combT[:, s, j * P:(j + 1) * P], b2r[:], start=True, stop=True)
                            else:
                                ph.hold(pe, hid_kept, o, hindex[(depth - 1, i, HC - 1)])
                                for c in range(HC):
                                    ins = nc.tensor.matmul(ybank[q % YR][0:P, 0:D], hid[-1][:, i % 2, c, j * P:(j + 1) * P], W2[:, e, c, :], start=c == 0, stop=c == HC - 1)
                            ins.then_inc(out_made.sem, 1)

        @block.scalar
        def _(act):
            hid_kept.open(act)
            for d in (score_kept, grown, comb_kept):
                d.open(act)
            act.wait_ge(loaded, nload)
            if norm:
                act.wait_ge(inverse_ready, 1)
                for i in range(2):
                    nc.scalar.activation(root[i][:], shift[i][:], ACT.Sqrt).then_inc(root_ready, 1)
                act.wait_ge(folded, 1)
            with act.Fori(0, NODE_LOOPS) as o:
                def grow(s):
                    ph.hold(act, centred, o, s)
                    m = RUNS[s][1]
                    nc.scalar.activation(work[:, s, 1, 0:m, :], work[:, s, 0, 0:m, :], ACT.Exp).then_inc(grown.sem, 1)

                for what, layer, i in order:
                    s, g = entries[i]
                    first, m = RUNS[s]
                    n = m * P
                    if what == "h":
                        if layer == 0 and g == 0 and gate and not shared:
                            ph.hold(act, scored, o, s)
                            ph.hold(act, scores_turned, o, s - 2)
                            nc.scalar.activation(logitT[:, s, 0:n], gbank[0:8, 0:n], ACT.Copy).then_inc(score_kept.sem, 1)
                        for mo in range(HC):
                            q = hindex[(layer, i, mo)]
                            ph.hold(act, hid_made, o, q)
                            if mo == 0:
                                back = i - 2
                                reader, r = last_reader(layer, back % len(entries))
                                if back < 0:
                                    r -= HB if reader == "h" else YB
                                ph.hold(act, hid_made if reader == "h" else out_made, o, r)
                            if norm:
                                nc.scalar.activation(hid[layer][:, i % 2, mo, 0:n], hbank[q % HR][:, 0:n], func,
                                                     scale=scale[layer][:, g, mo:mo + 1], bias=shift[layer][:, g, mo:mo + 1]).then_inc(hid_kept.sem, 1)
                            elif b1:
                                nc.scalar.activation(hid[layer][:, i % 2, mo, 0:n], hbank[q % HR][:, 0:n], func,
                                                     bias=b1c[:, g, mo:mo + 1]).then_inc(hid_kept.sem, 1)
                            else:
                                nc.scalar.activation(hid[layer][:, i % 2, mo, 0:n], hbank[q % HR][:, 0:n], func).then_inc(hid_kept.sem, 1)
                        if layer == 0 and g == 0 and gate and not shared:
                            grow(s)
                    elif gate:
                        if shared:
                            grow(s)
                        if b2 and g == 0:
                            ph.hold(act, comb_turned, o, s)
                            bias_items = [q for q, it in enumerate(yitems) if it[2] is None and entries[it[0]][0] == s]
                            ph.hold(act, out_made, o, bias_items[-1] - YB)
                            nc.scalar.activation(combT[:, s, 0:n], gbank[0:8, 0:n], ACT.Copy).then_inc(comb_kept.sem, 1)

        @block.vector
        def _(v):
            out_kept.open(v)
            for d in (centred, routed):
                d.open(v)
            v.wait_ge(loaded, nload)
            base = 0
            if norm:
                chain = Chain(v, chain_sem)
                for i, (b, gname, be, mean, var) in enumerate(norm["columns"]):
                    chain.link(nc.vector.tensor_scalar(bn[var][:], bn[var][:], norm["eps"], None, ALU.add))
                    chain.link(nc.vector.reciprocal(shift[i][:], bn[var][:]))
                nc.vector.tensor_copy(root[0][:, 0:1, 0:1], shift[0][:, 0:1, 0:1]).then_inc(inverse_ready, 1)
                v.wait_ge(root_ready, 2)
                for i, (b, gname, be, mean, var) in enumerate(norm["columns"]):
                    chain.link(nc.vector.tensor_tensor(scale[i][:], root[i][:], root[i][:], ALU.mult))
                    chain.link(nc.vector.tensor_tensor(scale[i][:], scale[i][:], bn[var][:], ALU.mult))
                    chain.link(nc.vector.tensor_scalar(scale[i][:], scale[i][:], -0.5, 1.5, ALU.mult, ALU.add))
                    chain.link(nc.vector.tensor_tensor(scale[i][:], scale[i][:], root[i][:], ALU.mult))
                    chain.link(nc.vector.tensor_tensor(scale[i][:], scale[i][:], bn[gname][:], ALU.mult))
                    chain.link(nc.vector.tensor_tensor(shift[i][:], bn[b][:], bn[mean][:], ALU.subtract))
                    chain.link(nc.vector.tensor_tensor(shift[i][:], shift[i][:], scale[i][:], ALU.mult))
                    chain.link(nc.vector.tensor_tensor(shift[i][:], shift[i][:], bn[be][:], ALU.add))
                nc.vector.tensor_copy(root[0][:, 0:1, 0:1], shift[0][:, 0:1, 0:1]).then_inc(folded, 1)
                base = chain.n
            per_body = 2 * routing(kind) if gate else 0
            with v.Fori(0, NODE_LOOPS) as o:
                chain = Chain(v, chain_sem, per_body, o, base)

                def link(ins):
                    chain.link(ins)
                    v.sem_inc(ph.spent, 1)

                def route(s):
                    m = RUNS[s][1]
                    full = [P, m, 8]
                    z, ex, eq, val, pick, rest, pick2, both = (work[:, s, i, 0:m, :] for i in range(8))
                    top, den, low, _ = (col[:, s, i, 0:m] for i in range(4))
                    wide = lambda c: bcast_last(c, full)
                    logits = gbank[0:P, 400:400 + 8 * m].rearrange("p (j e) -> p j e", e=8)

                    def first_of(scores, picked):
                        link(nc.vector.tensor_reduce(top, scores, AX.X, ALU.max))
                        link(nc.vector.tensor_tensor(eq, scores, wide(top), ALU.is_equal))
                        link(nc.vector.scalar_tensor_tensor(val, eq, -8.0, bcast_mid(core.iota8[:], full), ALU.mult, ALU.add))
                        link(nc.vector.tensor_reduce(low, val, AX.X, ALU.min))
                        link(nc.vector.tensor_tensor(picked, val, wide(low), ALU.is_equal))

                    ph.hold(v, scores_turned, o, s)
                    if gate[1]:
                        link(nc.vector.tensor_tensor(rest, logits, bcast_mid(bg[:], full), ALU.add))
                    else:
                        link(nc.vector.tensor_scalar(rest, logits, 0.0, None, ALU.add))
                    link(nc.vector.tensor_reduce(top, rest, AX.X, ALU.max))
                    chain(nc.vector.tensor_tensor(z, rest, wide(top), ALU.subtract))
                    chain.settle()
                    v.sem_inc(centred.sem, 1)
                    ph.hold(v, grown, o, s)
                    if kind == "top2logit":
                        first_of(rest, pick)
                        link(nc.vector.scalar_tensor_tensor(rest, pick, -3e38, rest, ALU.mult, ALU.add))
                        first_of(rest, pick2)
                        link(nc.vector.tensor_tensor(both, pick, pick2, ALU.add))
                        link(nc.vector.tensor_tensor(both, both, ex, ALU.mult))
                        link(nc.vector.tensor_reduce(den, both, AX.X, ALU.add))
                        link(nc.vector.reciprocal(den, den))
                        answer, by = both, den
                    else:
                        link(nc.vector.tensor_reduce(den, ex, AX.X, ALU.add))
                        link(nc.vector.reciprocal(den, den))
                        link(nc.vector.tensor_tensor(ex, ex, wide(den), ALU.mult))
                        if kind == "argmax":
                            first_of(ex, pick)
                        elif kind == "top2prob":
                            first_of(ex, pick)
                            link(nc.vector.scalar_tensor_tensor(rest, pick, -2.0, ex, ALU.mult, ALU.add))
                            first_of(rest, pick2)
                            link(nc.vector.tensor_tensor(both, pick, pick2, ALU.add))
                            link(nc.vector.tensor_tensor(both, both, ex, ALU.mult))
                            link(nc.vector.tensor_reduce(den, both, AX.X, ALU.add))
                            link(nc.vector.tensor_scalar(den, den, 1e-12, None, ALU.max))
                            link(nc.vector.reciprocal(den, den))
                    if b2:
                        ph.hold(v, comb_turned, o, s - 2)
                    out = comb[:, s, 0:m, :]
                    if kind == "soft":
                        return link(nc.vector.tensor_copy(out, ex)) if False else v.sem_inc(ph.spent, 1)
                    if kind == "argmax":
                        link(nc.vector.tensor_tensor(out, ex, pick, ALU.mult))
                    else:
                        link(nc.vector.tensor_tensor(out, both, wide(den), ALU.mult))

                for what, layer, i in order:
                    s, g = entries[i]
                    first, m = RUNS[s]
                    if gate and ((shared and what == "y") or (not shared and what == "h" and layer == 0 and g == 0)):
                        route(s)
                        if kind == "soft":
                            nc.vector.tensor_copy(comb[:, s, 0:m, :], work[:, s, 1, 0:m, :]).then_inc(routed.sem, 1)
                            ph.hold(v, routed, o, s)
                        else:
                            v.sem_inc(routed.sem, 1)
                    if what == "y":
                        for q in [q for q, it in enumerate(yitems) if it[0] == i]:
                            _, j, e = yitems[q]
                            row = target[:, bass.ds(o * BODY + first + j, 1), :]
                            made = ybank[q % YR][0:P, 0:D].unsqueeze(1)
                            ph.hold(v, out_made, o, q)
                            if last_update(q) is not None:
                                ph.hold(v, out_kept, o, last_update(q))
                            if e is None or not gate:
                                nc.vector.tensor_tensor(row, made, row, ALU.add).then_inc(out_kept.sem, 1)
                            else:
                                nc.vector.scalar_tensor_tensor(row, made, comb[:, s, j, e:e + 1], row, ALU.mult, ALU.add).then_inc(out_kept.sem, 1)
                if gate:
                    assert chain.n == per_body, (chain.n, per_body)


def mix0(core):
    with Phase(core.nc, "m0") as ph:
        mid = ph.sb("mid", [P, NT, D])
        midT = ph.sb("midT", [128, DC, N])
        start_rows(core, "m0_start", mid, core.xn, "L0_mix_bo")
        linear_attention(core, "m0_att", "L0_mix_Wq", [("L0_mix_Wk", None), ("L0_mix_Wv", None)], "L0_mix_Wo", mid,
                         bias=("L0_mix_bq", "L0_mix_bk", "L0_mix_bv"), plus=1e-6)

        def before():
            layer_norm(core, "m0_ln1", mid, mid, midT, token_affine=("L0_mix_ln1_g", "L0_mix_ln1_b"))
            start_rows(core, "m0_bias", mid, None, "L0_mix_b2")

        ffn(core, "m0_ff", [midT], 1024, "L0_mix_W1", "L0_mix_b1", ACT.Relu, "L0_mix_W2", mid, before=before)
        layer_norm(core, "m0_ln2", mid, mid, token_affine=("L0_mix_ln2_g", "L0_mix_ln2_b"), add_to_x=True)


def ffn0(core):
    ffn(core, "f0", [core.xnT], 1024, "L0_ffn_W1", "L0_ffn_b1", ACT.Gelu, "L0_ffn_Wd", core.x, experts=8, shared=True,
        gate=("L0_ffn_Wg", "L0_ffn_bg"), kind="argmax", b2="L0_ffn_bd", tables=core.sums[1],
        before=lambda: layer_norm(core, "ln0b", core.x, None, core.xnT, rows=False))


def ffn1(core):
    ffn(core, "f1", [core.xnT], 512, "L1_ffn_W1", "L1_ffn_b1", ACT.Gelu, "L1_ffn_W2", core.x, experts=8,
        gate=("L1_ffn_Wr", "L1_ffn_br"), kind="top2logit", b2="L1_ffn_b2", tables=core.sums[2],
        before=lambda: layer_norm(core, "ln1b", core.x, None, core.xnT, rows=False, feature_affine=("L1_ffn_gamma", "L1_ffn_beta")))


def mix2(core):
    start_rows(core, "m2_start", core.x, None, "L2_mix_bproj")
    linear_attention(core, "m2_att", "L2_mix_Wq", [("L2_mix_Wkv", None)], "L2_mix_Wproj", core.x, clamp=1e-6)


def ffn2(core):
    ffn(core, "f2", [core.xnT], 256, "L2_ffn_W1", None, ACT.Relu, "L2_ffn_Wo", core.x, experts=8,
        gate=("L2_ffn_Wr", "L2_ffn_br"), kind="soft", b2="L2_ffn_bo", tables=core.sums[3],
        norm={"w": "L2_ffn_W2", "eps": 1e-3, "columns": [[f"L2_ffn_{n}{i}" for n in ("b", "g", "be", "m", "v")] for i in (1, 2)]},
        before=lambda: layer_norm(core, "ln2b", core.x, None, core.xnT, rows=False))


def gnn3(core):
    support = core.table("support3", N, D)
    tables = core.sums[3]
    with Phase(core.nc, "g3") as ph:
        dest = ph.sb("s", [P, NT, D])
        project(core, "proj3", core.xnT, [("L3_gnn_weight", D)], dest, D, table=support)
    spread(core, "spread3", support, core.dst, core.a["src_rows"], core.srcf, core.src_once, tables, weight=core.weight)
    finish_plain(core, "fin3", tables, elu=False)


def mix3(core):
    with Phase(core.nc, "m3") as ph:
        mid = ph.sb("mid", [P, NT, D])
        midT = ph.sb("midT", [128, DC, N])
        linear_attention(core, "m3_att", "L3_mix_Wq", [("L3_mix_Wk", None), ("L3_mix_Wv", None)], "L3_mix_Wm", mid,
                         plus=1e-6, length=float(N), add=False)

        def before():
            layer_norm(core, "m3_ln1", mid, None, midT, rows=False, token_affine=("L3_mix_g1", "L3_mix_b1"))
            clear_rows(core, "m3_clear", mid)

        ffn(core, "m3_ff", [core.xnT, midT], 512, "L3_mix_W1", None, ACT.Relu, "L3_mix_W2", mid, before=before)
        layer_norm(core, "m3_ln2", mid, mid, token_affine=("L3_mix_g2", "L3_mix_b2"), add_to_x=True, add_xn=True)


def clear_rows(core, name, target):
    with Phase(core.nc, name) as ph:
        block = ph.block()

        @block.vector
        def _(v):
            core.nc.vector.memset(target[:], 0.0)


def ffn3(core):
    ffn(core, "f3", [core.xnT], 256, "L3_ffn_w1", "L3_ffn_b1", ACT.Gelu, "L3_ffn_w2", core.x, experts=8,
        gate=("L3_ffn_router_w", None), kind="top2prob", b2="L3_ffn_b2",
        before=lambda: layer_norm(core, "ln3b", core.x, None, core.xnT, rows=False, add_to_x=True))


def transpose_rows(core, name, buf, outT):
    nc = core.nc
    with Phase(nc, name) as ph:
        tile = ph.sb("tile", [P, BODY, D])
        staged, turned, stored = ph.done("staged", BODY), ph.done("turned", BODY), ph.done("stored", BODY)
        banks = [ph.ps(f"bank{k}") for k in range(BODY)]
        block = ph.block()

        @block.gpsimd
        def _(pool):
            staged.open(pool)
            with pool.Fori(0, NODE_LOOPS) as o:
                for k in range(BODY):
                    ph.hold(pool, turned, o, k - BODY)
                    nc.gpsimd.tensor_copy(tile[:, k:k + 1, :], buf[:, bass.ds(o * BODY + k, 1), :]).then_inc(staged.sem, 1)

        @block.tensor
        def _(pe):
            turned.open(pe)
            with pe.Fori(0, NODE_LOOPS) as o:
                for k in range(BODY):
                    ph.hold(pe, staged, o, k)
                    ph.hold(pe, stored, o, k - BODY)
                    for c in range(DC):
                        ins = nc.tensor.transpose(banks[k][:, c * P:(c + 1) * P], tile[:, k, c * 128:(c + 1) * 128], core.ident[0:P, 0:P])
                    ins.then_inc(turned.sem, 1)

        @block.scalar
        def _(act):
            stored.open(act)
            with act.Fori(0, NODE_LOOPS) as o:
                for k in range(BODY):
                    ph.hold(act, turned, o, k)
                    nc.scalar.activation(outT[:, :, columns(o * BODY + k)], banks[k][:, 0:DC * P].rearrange("p (c n) -> p c n", c=DC), ACT.Copy).then_inc(stored.sem, 1)


def edge_scores(core, name, left, left_index, right, right_index, left_width, width, stages, score, stash, kept_columns, types=None, mark=None):
    nc, a = core.nc, core.a
    with Phase(nc, name) as ph:
        left_at, right_at = ph.sb("left_at", [P, EBODY], I32), ph.sb("right_at", [P, EBODY], I32)
        lrow, rrow = ph.sb("lrow", [P, EBODY, left_width]), ph.sb("rrow", [P, EBODY, width])
        rows_in = [ph.sem(f"rows_in{k}") for k in range(EBODY)]
        stashed = [ph.sem(f"stashed{k}") for k in range(EBODY)]
        index_set, used = ph.done("index_set", EBODY), ph.done("used", EBODY)
        chain_sem, const, scaled = ph.sem("chain"), ph.sem("const"), ph.sem("scaled")
        if types:
            tw = a[types[1]].shape[1]
            trow = ph.sb("trow", [64, EBODY, P], I32)
            which = ph.sb("which", [64, EBODY, P])
            number = ph.sb("number", [64, 1])
            rel = ph.sb("rel", [64, tw])
            types_in = [ph.sem(f"types_in{k}") for k in range(EBODY)]
            compared, picked = ph.done("compared", EBODY), ph.done("picked", EBODY)
            banks = [ph.ps(f"bank{k}") for k in range(EBANKS)]
        if mark:
            keys = ph.sb("keys", [P, EBODY, P], I32)
            keys_in = ph.sem("keys_in")
            marks = Marks(core, ph, mark[1], mark[2])
        block = ph.block()

        @block.sync
        def _(sp):
            if types:
                sp.dma_start(number[:], a["c_types"]).then_inc(const, 16)
                sp.dma_start(rel[:], a[types[1]]).then_inc(const, 16)
            if mark:
                marks.load(sp)
            with sp.Fori(0, EDGE_LOOPS) as o:
                if types:
                    for k in range(EBODY):
                        ph.hold(sp, compared, o, k - EBODY)
                        sp.dma_start(trow[:, k, :], a[types[0]][bass.ds((o * EBODY + k) * P, P)].partition_broadcast(64)).then_inc(types_in[k], 16)
                if mark:
                    ph.hold(sp, marks.marked, o, -1)
                    sp.dma_start(keys[:], mark[0][bass.ds(o * EBODY * P, EBODY * P)].partition_broadcast(P)
                                 .rearrange("p (k e) -> p k e", k=EBODY)).then_inc(keys_in, 16)
                for k in range(EBODY):
                    ph.hold_dma(sp, rows_in[k], o, 2)
                    sp.dma_start(stash[bass.ds((o * EBODY + k) * P, P), :], lrow[:, k, kept_columns]).then_inc(stashed[k], 16)
            for k in range(EBODY):
                sp.wait_ge(stashed[k], 16 * EDGE_LOOPS)

        if types:
            @block.tensor
            def _(pe):
                picked.open(pe)
                pe.wait_ge(scaled, 1)
                with pe.Fori(0, EDGE_LOOPS) as o:
                    for k in range(EBODY):
                        ph.hold(pe, compared, o, k)
                        ph.hold(pe, used, o, slot_owner(EBANKS, EBODY, k))
                        nc.tensor.matmul(banks[k % EBANKS][0:P, 0:tw], which[:, k, :], rel[:], start=True, stop=True).then_inc(picked.sem, 1)

        @block.scalar
        def _(act):
            index_set.open(act)

            def set_index(o, k):
                ph.hold(act, used, o, k - EBODY)
                if not (isinstance(o, int) and o == 0):
                    ph.hold_dma(act, stashed[k], o - 1)
                one = bass.ds(o * EBODY + k, 1)
                nc.scalar.activation(left_at[:, k:k + 1], left_index[:, one], ACT.Copy)
                nc.scalar.activation(right_at[:, k:k + 1], right_index[:, one], ACT.Copy).then_inc(index_set.sem, 1)

            for k in range(EBODY):
                set_index(0, k)
            with act.Fori(1, EDGE_LOOPS) as o:
                for k in range(EBODY):
                    set_index(o, k)

        @block.gpsimd
        def _(pool):
            with pool.Fori(0, EDGE_LOOPS) as o:
                for k in range(EBODY):
                    ph.hold(pool, index_set, o, k)
                    nc.gpsimd.indirect_dma_start(lrow[:, k, :], None, left, bass.IndirectOffsetOnAxis(ap=left_at[:, k:k + 1], axis=0)).then_inc(rows_in[k], 16)
                    nc.gpsimd.indirect_dma_start(rrow[:, k, :], None, right, bass.IndirectOffsetOnAxis(ap=right_at[:, k:k + 1], axis=0)).then_inc(rows_in[k], 16)

        @block.vector
        def _(v):
            used.open(v)
            if types:
                compared.open(v)
                v.wait_ge(const, 32)
                nc.vector.tensor_scalar(rel[:], rel[:], types[2], None, ALU.mult).then_inc(scaled, 1)
            if mark:
                marks.marked.open(v)
                v.wait_ge(marks.const, 32)
            with v.Fori(0, EDGE_LOOPS) as o:
                if types:
                    for k in range(EBODY):
                        ph.hold_dma(v, types_in[k], o)
                        ph.hold(v, picked, o, k - EBODY)
                        nc.vector.tensor_scalar(which[:, k, :], trow[:, k, :], number[:, 0:1], None, ALU.is_equal).then_inc(compared.sem, 1)
                steps = (stages - 1) * EBODY + (Marks.LINKS if mark else 0)
                chain = Chain(v, chain_sem, steps, o)
                first = {}
                for turn in range(EBODY + stages - 1):
                    for stage in range(stages):
                        k = turn - stage
                        if not 0 <= k < EBODY:
                            continue
                        if stage == 0:
                            ph.hold_dma(v, rows_in[k], o, 2)
                            if types:
                                ph.hold(v, picked, o, k)
                        else:
                            chain.settle(first[k])
                            v.sem_inc(ph.spent, 1)
                        ins = score(stage, lrow[:, k, :], rrow[:, k, :], banks[k % EBANKS][0:P, 0:tw] if types else None, o * EBODY + k)
                        if stage == stages - 1:
                            ins.then_inc(used.sem, 1)
                        else:
                            chain(ins)
                            first[k] = chain.n
                if mark:
                    ph.hold_dma(v, keys_in, o)
                    for k in range(EBODY):
                        marks.compare(chain, keys[:, k, :], o, k)
                    marks.finish(v, chain, o)
                assert chain.n == steps
            v.wait_ge(used.sem, used.at(EDGE_LOOPS - 1, EBODY - 1))
            if mark:
                v.wait_ge(marks.marked.sem, marks.marked.at(EDGE_LOOPS - 1, 0))


def spread_row(v_engine, nc, out, column):
    return nc.vector.tensor_scalar(out, column[0], column[1], None, ALU.mult)


def segment_softmax(core, name, scores, factor, alpha, heads):
    nc, a = core.nc, core.a
    LOW = -1e38
    with Phase(nc, name) as ph:
        starts = ph.sb("starts", [P, ET])
        forward = ph.sb("forward", [P, heads, ET])
        backward = ph.sb("backward", [P, heads, ET])
        mask = ph.sb("mask", [P, 2, ET])
        near = ph.sb("near", [P, ET])
        ends = ph.sb("ends", [P, 2 + 2 * heads])
        diag = ph.sb("diag", [P, 2 + 2 * heads, P])
        rows = ph.sb("rows", [P, 2 + 2 * heads, P])
        ones = ph.sb("ones", [P, P])
        equal = ph.sb("equal", [P, 2, 2, P])
        cand = ph.sb("cand", [P, heads, 2, P])
        best = ph.sb("best", [P, 2, heads])
        chain_sem, diag_set, spread_done, shifted = ph.sem("chain"), ph.sem("diag_set"), ph.sem("spread_done"), ph.sem("shifted")
        nv = 2 + 2 * heads
        per = 4
        banks = [ph.ps(f"bank{i}") for i in range((nv + per - 1) // per)]
        key = core.dstf
        block = ph.block()

        @block.vector
        def _(v):
            chain = Chain(v, chain_sem)
            link = chain.link
            chain(nc.vector.memset(ones[:], 1.0))
            chain(nc.vector.memset(starts[:, 0:1], 0.0))
            link(nc.vector.tensor_tensor(starts[:, 1:ET], key[:, 1:ET], key[:, 0:ET - 1], ALU.not_equal))
            link(nc.vector.tensor_scalar(starts[:], starts[:], LOW, None, ALU.mult))
            for h in range(heads):
                chain(nc.vector.tensor_tensor_scan(forward[:, h, :], starts[:], scores[:, h, :], 2 * LOW, ALU.add, ALU.max))
            chain.settle()
            for h in range(heads):
                chain(nc.vector.tensor_copy(backward[:, h, ET - 1:ET], scores[:, h, ET - 1:ET]))
                link(nc.vector.tensor_tensor_scan(backward[:, h, ET - 2::-1], starts[:, ET - 1:0:-1], scores[:, h, ET - 2::-1],
                                                  scores[:, h, ET - 1:ET], ALU.add, ALU.max))
            chain(nc.vector.tensor_copy(ends[:, 0:1], key[:, 0:1]))
            chain(nc.vector.tensor_copy(ends[:, 1:2], key[:, ET - 1:ET]))
            chain(nc.vector.tensor_copy(ends[:, 2:2 + heads], backward[:, :, 0:1].rearrange("p h o -> p (h o)")))
            link(nc.vector.tensor_copy(ends[:, 2 + heads:nv], forward[:, :, ET - 1:ET].rearrange("p h o -> p (h o)")))
            link(nc.vector.tensor_tensor(forward[:], forward[:], backward[:], ALU.max))
            for i in range(nv):
                ins = nc.vector.tensor_scalar(diag[:, i, :], core.ident[0:P, 0:P], ends[:, i:i + 1], None, ALU.mult)
                if i < nv - 1:
                    chain(ins)
            chain.settle()
            ins.then_inc(diag_set, 1)
            v.wait_ge(spread_done, 1)
            for i in range(nv):
                chain(nc.vector.tensor_copy(rows[:, i, :], banks[i // per][0:P, (i % per) * P:(i % per + 1) * P]))
            chain.settle()
            for side in range(2):
                link(nc.vector.tensor_scalar(equal[:, side], rows[:, 0:2, :], ends[:, side:side + 1], None, ALU.is_equal))
                link(nc.vector.tensor_scalar(equal[:, side], equal[:, side], 1.0, -LOW, ALU.subtract, ALU.mult))
                for h in range(heads):
                    chain(nc.vector.tensor_tensor(cand[:, h, 0, :], rows[:, 2 + h, :], equal[:, side, 0, :], ALU.add))
                    chain(nc.vector.tensor_tensor(cand[:, h, 1, :], rows[:, 2 + heads + h, :], equal[:, side, 1, :], ALU.add))
                chain.settle()
                link(nc.vector.tensor_reduce(best[:, side, :], cand[:], AX.XY, ALU.max))
                link(nc.vector.tensor_scalar(mask[:, side, :], key[:], ends[:, side:side + 1], None, ALU.is_equal))
                link(nc.vector.tensor_scalar(mask[:, side, :], mask[:, side, :], 1.0, -LOW, ALU.subtract, ALU.mult))
                for h in range(heads):
                    link(nc.vector.scalar_tensor_tensor(forward[:, h, :], mask[:, side, :], best[:, side, h:h + 1], forward[:, h, :], ALU.add, ALU.max))
            nc.vector.tensor_tensor(forward[:], scores[:], forward[:], ALU.subtract).then_inc(shifted, 1)

        @block.tensor
        def _(pe):
            pe.wait_ge(diag_set, 1)
            for b in range(len(banks)):
                n = min(per, nv - per * b)
                ins = nc.tensor.matmul(banks[b][0:P, 0:n * P], ones[:], diag[:, per * b:per * b + n, :], start=True, stop=True)
            ins.then_inc(spread_done, 1)

        @block.scalar
        def _(act):
            act.wait_ge(shifted, 1)
            nc.scalar.activation(alpha[:].rearrange("p e h -> p h e"), forward[:], ACT.Exp, scale=factor)


def gnn1(core):
    nc, a = core.nc, core.a
    heads, dim = 4, 64
    q, kv, val = core.table("q1", N, D), core.table("kv1", N, 2 * D), core.table("val1", ET * P, D)
    tables = core.sums[1]
    with Phase(nc, "g1a") as outer:
        enhT = outer.sb("enhT", [128, DC, N])
        dest = outer.sb("dest", [P, NT, 2 * D])
        with Phase(nc, "g1_enh") as ph:
            emb = ph.sb("emb", [128, DC])
            loaded, chain_sem = ph.sem("loaded"), ph.sem("chain")
            block = ph.block()

            @block.sync
            def _(sp):
                sp.dma_start(emb[:], a["L1_gnn_query_emb"]).then_inc(loaded, 16)
                sp.wait_ge(loaded, 16)

            @block.vector
            def _(v):
                chain = Chain(v, chain_sem)
                v.wait_ge(loaded, 16)
                chain.link(nc.vector.tensor_scalar(emb[:], emb[:], 0.1, None, ALU.mult))
                for c in range(DC):
                    chain(nc.vector.tensor_scalar(enhT[:, c, :], core.xnT[:, c, :], emb[:, c:c + 1], None, ALU.add))
        project(core, "g1_kv", enhT, [("L1_gnn_Wk", D), ("L1_gnn_Wv", D)], dest, 2 * D, bias=[("L1_gnn_bk", D), ("L1_gnn_bv", D)], table=kv)
        project(core, "g1_q", enhT, [("L1_gnn_Wq", D)], dest[:, :, 0:D], D, bias=[("L1_gnn_bq", D)], table=q)
    with Phase(nc, "g1b") as outer:
        alpha = outer.sb("alpha", [P, ET, heads])
        scores = outer.sb("scores", [P, heads, ET])

        def score(stage, krow, qrow, rel, edge):
            krow = krow[:, 0:D]
            kh = krow.rearrange("p (h d) -> p h d", h=heads)
            if stage == 0:
                return nc.vector.tensor_tensor(kh, kh, bcast_mid(rel, [P, heads, dim]), ALU.add)
            if stage == 1:
                return nc.vector.tensor_tensor(krow, krow, qrow, ALU.mult)
            return nc.vector.tensor_reduce(scores[:, :, bass.ds(edge, 1)].rearrange("p h o -> p (h o)"), kh, AX.X, ALU.add)

        edge_scores(core, "g1_sc", kv, core.src, q, core.dst, 2 * D, D, 3, score, val, slice(D, 2 * D), types=("type_rows", "L1_gnn_rel_w", 0.2),
                    mark=(a["dst_rows"], core.dstf, core.dst_once))
        segment_softmax(core, "g1_sm", scores, dim ** -0.5, alpha, heads)
        spread(core, "g1_sp", val, None, a["dst_rows"], core.dstf, core.dst_once, tables, alpha=alpha, heads=heads)
    with Phase(nc, "g1c") as outer:
        mid = outer.sb("mid", [P, NT, D])
        with Phase(nc, "g1_fin") as ph:
            table_sum = TableSum(ph, tables, D + heads)
            parts = table_sum.parts
            some = ph.sb("some", [P, NT, heads])
            den = ph.sb("den", [P, NT, heads])
            back, chain_sem = ph.sem("back"), ph.sem("chain")
            block = ph.block()

            @block.sync
            def _(sp):
                table_sum.load(sp)
                sp.dma_start(mid[:], nodes(kv[:, D:2 * D])).then_inc(back, 16)
                sp.wait_ge(back, 16)

            @block.vector
            def _(v):
                chain = Chain(v, chain_sem)
                link = chain.link
                table_sum.add(v, nc)
                total = parts[0][:, :, D:D + heads]
                wide = [P, NT, heads, dim]
                hd = lambda ap: ap.rearrange("p t (h d) -> p t h d", h=heads)
                link(nc.vector.tensor_scalar(some[:], total, 0.0, None, ALU.is_le))
                link(nc.vector.tensor_tensor(den[:], total, some[:], ALU.add))
                link(nc.vector.reciprocal(den[:], den[:]))
                link(nc.vector.tensor_tensor(hd(parts[0][:, :, 0:D]), hd(parts[0][:, :, 0:D]), bcast_last(den[:], wide), ALU.mult))
                v.wait_ge(back, 16)
                link(nc.vector.tensor_tensor(hd(mid[:]), hd(mid[:]), bcast_last(some[:], wide), ALU.mult))
                link(nc.vector.tensor_tensor(mid[:], mid[:], parts[0][:, :, 0:D], ALU.add))

        midT = outer.sb("midT", [128, DC, N])
        transpose_rows(core, "g1_turn", mid, midT)
        project(core, "g1_out", midT, [("L1_gnn_Wo", D)], mid, D, bias=[("L1_gnn_bo", D)])
        add_rows(core, "g1_res", mid, core.xn)
        layer_norm(core, "g1_ln", mid, mid, token_affine=("L1_gnn_gamma", "L1_gnn_beta"), add_to_x=True)


def add_rows(core, name, target, source):
    with Phase(core.nc, name) as ph:
        block = ph.block()

        @block.vector
        def _(v):
            core.nc.vector.tensor_tensor(target[:], target[:], source[:], ALU.add)


def row_lengths(core, name, buf, inverse):
    nc = core.nc
    with Phase(nc, name) as ph:
        square = ph.sb("square", [P, NT, D])
        total, root, part = ph.sb("total", [P, NT]), ph.sb("root", [P, NT]), ph.sb("part", [P, NT])
        summed, rooted, chain_sem = ph.sem("summed"), ph.sem("rooted"), ph.sem("chain")
        block = ph.block()

        @block.vector
        def _(v):
            link = Chain(v, chain_sem).link
            link(nc.vector.tensor_tensor(square[:], buf[:], buf[:], ALU.mult))
            nc.vector.tensor_reduce(total[:], square[:], AX.X, ALU.add).then_inc(summed, 1)
            v.wait_ge(summed, 1)
            v.wait_ge(rooted, 1)
            link(nc.vector.tensor_scalar(root[:], root[:], 1e-12, None, ALU.max))
            link(nc.vector.reciprocal(part[:], root[:]))
            link(nc.vector.tensor_tensor(part[:], part[:], total[:], ALU.mult))
            link(nc.vector.tensor_tensor(root[:], root[:], part[:], ALU.add))
            link(nc.vector.tensor_scalar(root[:], root[:], 0.5, 1e-12, ALU.mult, ALU.max))
            link(nc.vector.reciprocal(inverse[:], root[:]))
            link(nc.vector.tensor_scalar(inverse[:], inverse[:], float(D) ** 0.5, None, ALU.mult))

        @block.scalar
        def _(act):
            act.wait_ge(summed, 1)
            nc.scalar.activation(root[:], total[:], ACT.Sqrt).then_inc(rooted, 1)


def mix1(core):
    nc, a = core.nc, core.a
    heads, dim, mem = 4, 32, 4
    H = heads * dim
    with Phase(nc, "m1") as outer:
        qkv = outer.sb("qkv", [P, NT, 3 * H])
        context = outer.sb("context", [128, H])
        inverse = outer.sb("inverse", [P, NT])
        mid = outer.sb("mid", [P, NT, D])
        row_lengths(core, "m1_len", core.xn, inverse)
        project(core, "m1_qkv", core.xnT, [("L1_mix_w_qkv", 3 * H)], qkv, 3 * H, feature_scale="L1_mix_g_pre", row_scale=inverse)

        with Phase(nc, "m1_sm") as ph:
            top, den = ph.sb("top", [P, NT, heads]), ph.sb("den", [P, NT, heads])
            kbest = ph.sb("kbest", [P, H])
            kcol = ph.sb("kcol", [128, 1])
            diag, ones = ph.sb("diag", [128, H]), ph.sb("ones", [128, P])
            krow = ph.sb("krow", [P, H])
            memkv = ph.sb("memkv", [mem, 2 * H])
            tile = ph.sb("tile", [P, BODY, 2 * H + 1])
            memk, memv = ph.sb("memk", [mem, H]), ph.sb("memv", [mem, H + 1])
            inv = ph.sb("inv", [128, 1])
            loaded, chain_sem = ph.sem("loaded"), ph.sem("chain")
            qshift, qgrown, kmax_set, kturned, diag_set, spread_done = (ph.sem(n) for n in ("qshift", "qgrown", "kmax_set", "kturned", "diag_set", "spread_done"))
            kshift, kgrown, closed, ones_set = (ph.sem(n) for n in ("kshift", "kgrown", "closed", "ones_set"))
            staged, added = ph.done("staged", BODY), ph.done("added", BODY)
            tbank, rbank, cbank = ph.ps("turn"), ph.ps("row"), ph.ps("ctx")
            block = ph.block()
            qs = qkv[:, :, 0:H].rearrange("p t (h d) -> p t h d", h=heads)
            ks = qkv[:, :, H:2 * H]
            wide = [P, NT, heads, dim]

            @block.sync
            def _(sp):
                sp.dma_start(memkv[:].rearrange("m (k c) -> m k c", k=2), a["L1_mix_mem_kv"]).then_inc(loaded, 16)
                sp.wait_ge(loaded, 16)

            @block.vector
            def _(v):
                chain = Chain(v, chain_sem)
                link = chain.link
                link(nc.vector.memset(ones[:], 1.0))
                nc.vector.tensor_reduce(kbest[:], ks.rearrange("p t c -> p c t"), AX.X, ALU.max).then_inc(kmax_set, 1)
                link(nc.vector.tensor_reduce(top[:], qs, AX.X, ALU.max))
                nc.vector.tensor_tensor(qs, qs, bcast_last(top[:], wide), ALU.subtract).then_inc(qshift, 1)
                v.wait_ge(kturned, 1)
                link(nc.vector.tensor_reduce(kcol[:], tbank[:, 0:P + mem], AX.X, ALU.max))
                nc.vector.tensor_scalar(diag[:], core.ident[:], kcol[:, 0:1], None, ALU.mult).then_inc(diag_set, 1)
                v.wait_ge(spread_done, 1)
                link(nc.vector.tensor_copy(krow[:], rbank[0:P, 0:H]))
                link(nc.vector.tensor_tensor(memk[:], memkv[:, 0:H], krow[0:mem, :], ALU.subtract))
                link(nc.vector.tensor_copy(memv[:, 0:H], memkv[:, H:2 * H]))
                link(nc.vector.memset(memv[:, H:H + 1], 1.0))
                nc.vector.tensor_tensor(ks, ks, bcast_mid(krow[:], [P, NT, H]), ALU.subtract).then_inc(kshift, 1)
                v.wait_ge(qgrown, 1)
                link(nc.vector.tensor_reduce(den[:], qs, AX.X, ALU.add))
                link(nc.vector.reciprocal(den[:], den[:]))
                link(nc.vector.tensor_scalar(den[:], den[:], dim ** -0.5, None, ALU.mult))
                link(nc.vector.tensor_tensor(qs, qs, bcast_last(den[:], wide), ALU.mult))
                v.wait_ge(closed, 1)
                link(nc.vector.reciprocal(inv[:], cbank[:, H:H + 1]))
                link(nc.vector.scalar_tensor_tensor(context[:], cbank[:, 0:H], inv[:, 0:1], core.heads[:], ALU.mult, ALU.mult))

            @block.scalar
            def _(act):
                act.wait_ge(qshift, 1)
                nc.scalar.activation(qs, qs, ACT.Exp).then_inc(qgrown, 1)
                act.wait_ge(kshift, 1)
                nc.scalar.activation(memk[:], memk[:], ACT.Exp).then_inc(kgrown, 1)
                nc.scalar.activation(ks, ks, ACT.Exp).then_inc(kgrown, 1)

            @block.gpsimd
            def _(pool):
                staged.open(pool)
                nc.gpsimd.memset(tile[:, :, 2 * H:2 * H + 1], 1.0).then_inc(ones_set, 1)
                pool.wait_ge(kgrown, 2)
                with pool.Fori(0, NODE_LOOPS) as o:
                    for k in range(BODY):
                        ph.hold(pool, added, o, k - BODY)
                        nc.gpsimd.tensor_copy(tile[:, k:k + 1, 0:2 * H], qkv[:, bass.ds(o * BODY + k, 1), H:3 * H]).then_inc(staged.sem, 1)

            @block.tensor
            def _(pe):
                added.open(pe)
                pe.wait_ge(kmax_set, 1)
                pe.wait_ge(loaded, 16)
                nc.tensor.transpose(tbank[:, 0:P], kbest[:], core.ident[0:P, 0:P])
                nc.tensor.transpose(tbank[:, P:P + mem], memkv[:, 0:H], core.ident[0:mem, 0:mem]).then_inc(kturned, 1)
                pe.wait_ge(diag_set, 1)
                nc.tensor.matmul(rbank[0:P, 0:H], ones[:], diag[:], start=True, stop=True).then_inc(spread_done, 1)
                pe.wait_ge(kgrown, 2)
                pe.wait_ge(ones_set, 1)
                nc.tensor.matmul(cbank[:, 0:H + 1], memk[:], memv[:], start=True, stop=False, skip_group_check=True)
                with pe.Fori(0, NODE_LOOPS) as o:
                    for k in range(BODY):
                        ph.hold(pe, staged, o, k)
                        nc.tensor.matmul(cbank[:, 0:H + 1], tile[:, k, 0:H], tile[:, k, H:2 * H + 1], start=False, stop=False, skip_group_check=True).then_inc(added.sem, 1)
                nc.tensor.matmul(cbank[:, 0:H + 1], core.zero[0:P, 0:128], core.zero[0:P, 0:H + 1], start=False, stop=True, skip_group_check=True).then_inc(closed, 1)

        with Phase(nc, "m1_read") as ph:
            wout = ph.sb("wout", [128, D])
            b = ph.sb("b", [P, D])
            tile = ph.sb("tile", [P, BODY, H])
            qT, outT = ph.sb("qT", [128, BODY, P]), ph.sb("outT", [128, BODY, P])
            loaded = ph.sem("loaded")
            staged, turned, qkept, read, okept, result, kept = (ph.done(n, BODY) for n in ("staged", "turned", "qkept", "read", "okept", "result", "kept"))
            banks = [ph.ps(f"bank{k}") for k in range(BODY)]
            block = ph.block()

            @block.sync
            def _(sp):
                sp.dma_start(wout[:], a["L1_mix_w_out"]).then_inc(loaded, 16)
                sp.dma_start(b[:], a["L1_mix_b_out"].partition_broadcast(P)).then_inc(loaded, 16)
                sp.wait_ge(loaded, 32)

            @block.gpsimd
            def _(pool):
                staged.open(pool)
                with pool.Fori(0, NODE_LOOPS) as o:
                    for k in range(BODY):
                        ph.hold(pool, turned, o, k - BODY)
                        nc.gpsimd.tensor_copy(tile[:, k:k + 1, :], qkv[:, bass.ds(o * BODY + k, 1), 0:H]).then_inc(staged.sem, 1)

            @block.tensor
            def _(pe):
                for d in (turned, read, result):
                    d.open(pe)
                pe.wait_ge(loaded, 32)
                with pe.Fori(0, NODE_LOOPS) as o:
                    for k in range(BODY):
                        ph.hold(pe, staged, o, k)
                        ph.hold(pe, kept, o, k - BODY)
                        nc.tensor.transpose(banks[k][:, 0:P], tile[:, k, :], core.ident[0:P, 0:P]).then_inc(turned.sem, 1)
                    for k in range(BODY):
                        ph.hold(pe, qkept, o, k)
                        nc.tensor.matmul(banks[k][:, 128:128 + P], context[:], qT[:, k, :], start=True, stop=True).then_inc(read.sem, 1)
                    for k in range(BODY):
                        ph.hold(pe, okept, o, k)
                        nc.tensor.matmul(banks[k][0:P, 256:512], outT[:, k, :], wout[:], start=True, stop=True).then_inc(result.sem, 1)

            @block.scalar
            def _(act):
                qkept.open(act)
                okept.open(act)
                with act.Fori(0, NODE_LOOPS) as o:
                    for k in range(BODY):
                        ph.hold(act, turned, o, k)
                        ph.hold(act, read, o, k - BODY)
                        nc.scalar.activation(qT[:, k, :], banks[k][:, 0:P], ACT.Copy).then_inc(qkept.sem, 1)
                    for k in range(BODY):
                        ph.hold(act, read, o, k)
                        ph.hold(act, result, o, k - BODY)
                        nc.scalar.activation(outT[:, k, :], banks[k][:, 128:128 + P], ACT.Copy).then_inc(okept.sem, 1)

            @block.vector
            def _(v):
                kept.open(v)
                v.wait_ge(loaded, 32)
                with v.Fori(0, NODE_LOOPS) as o:
                    for k in range(BODY):
                        ph.hold(v, result, o, k)
                        nc.vector.tensor_tensor(mid[:, bass.ds(o * BODY + k, 1), :], banks[k][0:P, 256:512].unsqueeze(1), b[:].unsqueeze(1), ALU.add).then_inc(kept.sem, 1)

        row_lengths(core, "m1_len2", mid, inverse)
        with Phase(nc, "m1_end") as ph:
            g = ph.sb("g", [P, D])
            loaded, chain_sem = ph.sem("loaded"), ph.sem("chain")
            block = ph.block()

            @block.sync
            def _(sp):
                sp.dma_start(g[:], a["L1_mix_g_out"].partition_broadcast(P)).then_inc(loaded, 16)
                sp.wait_ge(loaded, 16)

            @block.vector
            def _(v):
                link = Chain(v, chain_sem).link
                link(nc.vector.tensor_tensor(mid[:], mid[:], bcast_last(inverse[:], [P, NT, D]), ALU.mult))
                v.wait_ge(loaded, 16)
                link(nc.vector.tensor_tensor(mid[:], mid[:], bcast_mid(g[:], [P, NT, D]), ALU.mult))
                link(nc.vector.tensor_tensor(mid[:], mid[:], core.xn[:], ALU.add))
                link(nc.vector.tensor_tensor(core.x[:], core.x[:], mid[:], ALU.add))


def gnn2(core):
    nc, a = core.nc, core.a
    heads, dim = 8, 32
    full = D + 2 * heads
    table, logits, kept = core.table("h2", N, full), core.table("logits2", N, 2 * heads), core.table("kept2", ET * P, D)
    tables = core.sums[2]
    wide = [P, NT, heads, dim]
    with Phase(nc, "g2") as outer:
        alpha = outer.sb("alpha", [P, ET, heads])
        own = outer.sb("own", [P, NT, heads])
        with Phase(nc, "g2a") as inner:
            dest = inner.sb("dest", [P, NT, D])
            project(core, "g2_h", core.xnT, [("L2_gnn_W", D)], dest, D, bias=[("L2_gnn_b", D)], table=table[:, 0:D])
            with Phase(nc, "g2_logit") as ph:
                prod = ph.sb("prod", [P, NT, D])
                av = ph.sb("av", [P, 2, D])
                both = ph.sb("both", [P, NT, 2 * heads])
                loaded, made, saved, chain_sem = ph.sem("loaded"), ph.sem("made"), ph.sem("saved"), ph.sem("chain")
                block = ph.block()

                @block.sync
                def _(sp):
                    for i, n in enumerate(("src", "trg")):
                        sp.dma_start(av[:, i, :], a["L2_gnn_a_" + n].partition_broadcast(P)).then_inc(loaded, 16)
                    sp.wait_ge(loaded, 32)
                    sp.wait_ge(made, 1)
                    sp.dma_start(nodes(logits), both[:]).then_inc(saved, 16)
                    sp.dma_start(nodes(table[:, D:full]), both[:]).then_inc(saved, 16)
                    sp.wait_ge(saved, 32)

                @block.vector
                def _(v):
                    link = Chain(v, chain_sem).link
                    v.wait_ge(loaded, 32)
                    for i in range(2):
                        link(nc.vector.tensor_tensor(prod[:], dest[:], bcast_mid(av[:, i, :], [P, NT, D]), ALU.mult))
                        link(nc.vector.tensor_reduce(both[:, :, i * heads:(i + 1) * heads], prod[:].rearrange("p t (h d) -> p t h d", h=heads), AX.X, ALU.add))
                    nc.vector.tensor_tensor(own[:], both[:, :, 0:heads], both[:, :, heads:2 * heads], ALU.add).then_inc(made, 1)

        def score(stage, srow, drow, _, edge):
            return nc.vector.tensor_tensor(alpha[:, bass.ds(edge, 1), :], srow[:, D:D + heads].unsqueeze(1), drow[:, heads:2 * heads].unsqueeze(1), ALU.add)

        edge_scores(core, "g2_sc", table, core.src, logits, core.dst, full, 2 * heads, 1, score, kept, slice(0, D))
        with Phase(nc, "g2_exp") as ph:
            best = ph.sb("best", [P, 2])
            diag, ones = ph.sb("diag", [P, 2, P]), ph.sb("ones", [P, P])
            top = ph.sb("top", [P, 1])
            chain_sem, diag_set, spread_done, shifted = ph.sem("chain"), ph.sem("diag_set"), ph.sem("spread_done"), ph.sem("shifted")
            bank = ph.ps("bank")
            block = ph.block()

            @block.vector
            def _(v):
                link = Chain(v, chain_sem).link
                link(nc.vector.memset(ones[:], 1.0))
                for ap, i in ((alpha, 0), (own, 1)):
                    link(nc.vector.scalar_tensor_tensor(ap[:], ap[:], 0.2, ap[:], ALU.mult, ALU.max))
                    link(nc.vector.tensor_reduce(best[:, i:i + 1], ap[:], AX.XY, ALU.max))
                link(nc.vector.tensor_scalar(diag[:, 0, :], core.ident[0:P, 0:P], best[:, 0:1], None, ALU.mult))
                nc.vector.tensor_scalar(diag[:, 1, :], core.ident[0:P, 0:P], best[:, 1:2], None, ALU.mult).then_inc(diag_set, 1)
                v.wait_ge(spread_done, 1)
                link(nc.vector.tensor_reduce(top[:], bank[0:P, 0:2 * P], AX.X, ALU.max))
                link(nc.vector.tensor_scalar(own[:], own[:], top[:, 0:1], None, ALU.subtract))
                nc.vector.tensor_scalar(alpha[:], alpha[:], top[:, 0:1], None, ALU.subtract).then_inc(shifted, 1)

            @block.tensor
            def _(pe):
                pe.wait_ge(diag_set, 1)
                nc.tensor.matmul(bank[0:P, 0:2 * P], ones[:], diag[:], start=True, stop=True).then_inc(spread_done, 1)

            @block.scalar
            def _(act):
                act.wait_ge(shifted, 1)
                nc.scalar.activation(alpha[:], alpha[:], ACT.Exp)
                nc.scalar.activation(own[:], own[:], ACT.Exp)

        spread(core, "g2_sp", kept, None, a["dst_rows"], core.dstf, core.dst_once, tables, alpha=alpha, heads=heads)
        own_kept = own
        with Phase(nc, "g2_fin") as ph:
            table_sum = TableSum(ph, tables, D + heads)
            parts = table_sum.parts
            den = ph.sb("den", [P, NT, heads])
            back, chain_sem = ph.sem("back"), ph.sem("chain")
            block = ph.block()
            hprime = parts[1][:, :, 0:D]

            @block.sync
            def _(sp):
                table_sum.load(sp)
                sp.wait_ge(table_sum.added, len(tables) - 1)
                sp.dma_start(hprime, nodes(table[:, 0:D])).then_inc(back, 16)
                sp.wait_ge(back, 16)

            @block.vector
            def _(v):
                link = Chain(v, chain_sem).link
                hd = lambda ap: ap.rearrange("p t (h d) -> p t h d", h=heads)
                table_sum.add(v, nc)
                link(nc.vector.tensor_tensor(den[:], parts[0][:, :, D:D + heads], own[:], ALU.add))
                link(nc.vector.tensor_scalar(den[:], den[:], 1e-10, None, ALU.add))
                link(nc.vector.reciprocal(den[:], den[:]))
                v.wait_ge(back, 16)
                link(nc.vector.tensor_tensor(hd(hprime), hd(hprime), bcast_last(own[:], wide), ALU.mult))
                link(nc.vector.tensor_tensor(parts[0][:, :, 0:D], parts[0][:, :, 0:D], hprime, ALU.add))
                link(nc.vector.tensor_tensor(hd(parts[0][:, :, 0:D]), hd(parts[0][:, :, 0:D]), bcast_last(den[:], wide), ALU.mult))
                link(nc.vector.tensor_tensor(core.x[:], core.x[:], parts[0][:, :, 0:D], ALU.add))


def norm_of(layer):
    return lambda core: layer_norm(core, f"ln{layer}", core.x, core.xn, core.xnT, rows=layer != 2, tables=core.sums[0] if layer == 0 else ())


COLUMNS = ["L0_mix_bq", "L0_mix_b1", "L0_ffn_b1", "L1_ffn_gamma", "L1_ffn_beta", "L1_gnn_query_emb", "L1_mix_g_pre"]
EXPERT_COLUMNS = ["L1_ffn_b1", "L3_ffn_b1"] + [f"L2_ffn_{n}{i}" for i in (1, 2) for n in ("b", "g", "be", "m", "v")]
PHASES = [
    ("load", load_all),
    ("ln0", norm_of(0)), ("gnn0", gnn0), ("mix0", mix0), ("ffn0", ffn0),
    ("ln1", norm_of(1)), ("gnn1", gnn1), ("mix1", mix1), ("ffn1", ffn1),
    ("ln2", norm_of(2)), ("gnn2", gnn2), ("mix2", mix2), ("ffn2", ffn2),
    ("ln3", norm_of(3)), ("gnn3", gnn3), ("mix3", mix3), ("ffn3", ffn3),
]


def program(nc, a, out, stop=None):
    with ExitStack() as stack:
        core = Core(nc, a, stack)
        for name, phase in PHASES:
            phase(core)
            if name == stop:
                break
        with Phase(nc, "store") as ph:
            stored = ph.sem("stored")
            block = ph.block()

            @block.sync
            def _(sp):
                sp.dma_start(nodes(out), core.x[:]).then_inc(stored, 16)
                sp.wait_ge(stored, 16)


def kernel(**inputs):
    import numpy as np
    import concourse.bacc as bacc
    from concourse.bass_utils import run_bass_kernel_spmd as run

    def column(v):
        return v.reshape(-1, 128).T

    arrays = {name: np.asarray(v) for name, v in inputs.items()}
    arrays["src_rows"] = arrays["src"].reshape(P, ET).T.reshape(-1)
    arrays["dst_rows"] = arrays["dst"].reshape(P, ET).T.reshape(-1)
    arrays["type_rows"] = arrays["edge_type_64"].reshape(P, ET).T.reshape(-1)
    for name in ("src", "dst", "edge_weight"):
        arrays[name] = arrays[name].reshape(P, ET)
    for name in ("L0_gnn_W", "L2_mix_Wq", "L2_mix_Wkv", "L2_mix_Wproj", "L3_ffn_router_w"):
        arrays[name] = arrays[name].T
    arrays["L1_mix_mem_kv"] = arrays["L1_mix_mem_kv"].reshape(2, 128, 4).transpose(2, 0, 1)
    for name in ("L2_gnn_a_src", "L2_gnn_a_trg"):
        arrays[name] = arrays[name].reshape(D)
    for name in COLUMNS:
        arrays[name] = column(arrays[name])
    for name in EXPERT_COLUMNS:
        v = arrays[name]
        arrays[name] = v.reshape(v.shape[0], -1, 128).transpose(2, 0, 1)
    arrays["c_ident"] = np.eye(128, dtype=np.float32)
    arrays["c_heads"] = np.kron(np.eye(4), np.ones((32, 32))).astype(np.float32)
    arrays["c_iota8"] = np.tile(np.arange(8, dtype=np.float32), (P, 1))
    arrays["c_earlier"] = np.tril(np.ones((P, P), np.float32), -1)
    arrays["c_spare"] = (N + np.arange(P, dtype=np.float32))[:, None]
    arrays["c_types"] = np.arange(64, dtype=np.float32)[:, None]

    nc = bacc.Bacc("TRN2", target_bir_lowering=False, num_devices=1)
    given, a = {}, {}
    for name, v in arrays.items():
        if name == "L1_mix_t":
            continue
        v = np.ascontiguousarray(v)
        given["in_" + name] = v
        a[name] = nc.dram_tensor("in_" + name, v.shape, mybir.dt.from_np(v.dtype), kind="ExternalInput").ap()
    out = nc.dram_tensor("out", (N, D), F32, kind="ExternalOutput").ap()
    program(nc, a, out)
    result = run(nc, [given], core_ids=[0])
    return result.results[0]["out"]
```

```python
from contextlib import ExitStack

import concourse.bass as bass
from concourse import mybir

F32 = mybir.dt.float32
I32 = mybir.dt.int32
ALU = mybir.AluOpType
ACT = mybir.ActivationFunctionType
AX = mybir.AxisListType

N = 3125
D = 256
P = 125
NT = N // P
NE = 53125
ET = NE // P
DC = D // 128
BODY = 5
NODE_LOOPS = NT // BODY
EBODY = 17
EDGE_LOOPS = ET // EBODY
EBANKS = 5
RUNS = [(0, 3), (3, 2)]
RUNMAX = 3 * P
TABLES = [5, 6, 6]
PARTS = 3
LN_EPS = 1e-5
BANK = 512


class Done:

    def __init__(self, sem, per_body):
        self.sem, self.per_body = sem, per_body

    def open(self, eng):
        eng.sem_inc(self.sem, self.per_body)

    def at(self, step, index):
        return (step + 1) * self.per_body + (index + 1)


class Chain:

    def __init__(self, eng, sem, per_body=0, step=None, base=0):
        self.eng, self.sem, self.per_body, self.step, self.base, self.n = eng, sem, per_body, step, base, 0

    def __call__(self, ins):
        ins.then_inc(self.sem, 1)
        self.n += 1

    def settle(self, count=None):
        value = self.base + (self.n if count is None else count)
        if self.step is not None:
            value = self.step * self.per_body + value
        self.eng.wait_ge(self.sem, value)

    def link(self, ins):
        self(ins)
        self.settle()


class Phase:

    def __init__(self, nc, name):
        self.nc, self.name, self.stack = nc, name, ExitStack()

    def __enter__(self):
        self.stack.__enter__()
        self.sems = []
        self.stack.callback(self.release)
        self.spent = self.sem("spent")
        return self

    def release(self):
        self.nc.clear_and_free_semaphores(self.sems)
        self.nc.all_engine_barrier()

    def __exit__(self, *a):
        return self.stack.__exit__(*a)

    def sb(self, name, shape, dtype=F32):
        return self.stack.enter_context(self.nc.sbuf_tensor(f"{self.name}_{name}", shape, dtype))

    def ps(self, name):
        return self.stack.enter_context(self.nc.psum_tensor(f"{self.name}_{name}", [128, BANK], F32))

    def sem(self, name):
        self.sems.append(self.nc.alloc_semaphore(name=f"{self.name}_{name}"))
        return self.sems[-1]

    def done(self, name, per_body):
        return Done(self.sem(name), per_body)

    def block(self):
        return self.stack.enter_context(self.nc.Block())

    def hold(self, eng, done, step, index):
        eng.wait_ge(done.sem, done.at(step, index))
        eng.sem_inc(self.spent, 1)

    def hold_dma(self, eng, sem, step, count=1):
        eng.wait_ge(sem, step * 16 * count + 16 * count)
        eng.sem_inc(self.spent, 1)


def slot_owner(slots, per_body, index):
    if index >= slots:
        return index - slots
    return max(i for i in range(per_body) if i % slots == index % slots) - per_body


def bcast_mid(ap, shape):
    return ap.unsqueeze(1).to_broadcast(shape)


def bcast_last(ap, shape):
    return ap.unsqueeze(len(shape) - 1).to_broadcast(shape)


def columns(tile, count=1):
    return bass.ds(tile * P, count * P)


def feature_rows(w):
    return w.rearrange("(c p) n -> p c n", p=128)


class Core:

    def __init__(self, nc, a, stack):
        self.nc, self.a = nc, a

        def sb(name, shape, dtype=F32):
            return stack.enter_context(nc.sbuf_tensor(name, shape, dtype))

        self.x = sb("x", [P, NT, D])
        self.xn = sb("xn", [P, NT, D])
        self.xnT = sb("xnT", [128, DC, N])
        self.ident = sb("ident", [128, 128])
        self.heads = sb("heads", [128, 128])
        self.iota8 = sb("iota8", [P, 8])
        self.zero = sb("zero", [P, 264])
        self.src = sb("src", [P, ET], I32)
        self.dst = sb("dst", [P, ET], I32)
        self.srcf = sb("srcf", [P, ET])
        self.dstf = sb("dstf", [P, ET])
        self.pair_once = sb("pair_once", [P, ET], I32)
        self.pair_weight = sb("pair_weight", [P, ET])
        self.adjacency = self.table("adjacency", N * (N + 1), 1)
        self.dst_once = sb("dst_once", [P, ET], I32)
        self.weight = sb("weight", [P, ET])
        self.sums = [[self.table(f"sum{layer}_{i}", N + P, D + heads) for i in range(TABLES[layer])] for layer, heads in enumerate((0, 4, 8))]

    def table(self, name, rows, width):
        return self.nc.dram_tensor(name, (rows, width), F32, kind="Internal").ap()


def nodes(ap):
    return ap.rearrange("(p t) d -> p t d", t=NT)


def load_all(core):
    nc, a = core.nc, core.a
    with Phase(nc, "load") as ph:
        loaded, zeroed, converted = ph.sem("loaded"), ph.sem("zeroed"), ph.sem("converted")
        block = ph.block()

        @block.sync
        def _(sp):
            sp.dma_start(core.x[:], nodes(a["x"])).then_inc(loaded, 16)
            for buf, name in ((core.src, "src"), (core.dst, "dst"), (core.weight, "edge_weight"), (core.ident, "c_ident"),
                              (core.heads, "c_heads"), (core.iota8, "c_iota8")):
                sp.dma_start(buf[:], a[name]).then_inc(loaded, 16)
            sp.wait_ge(loaded, 16 * 7)

        @block.vector
        def _(v):
            nc.vector.memset(core.zero[:], 0.0).then_inc(zeroed, 1)
            v.wait_ge(loaded, 16 * 7)
            nc.vector.tensor_copy(core.srcf[:], core.src[:]).then_inc(converted, 1)
            nc.vector.tensor_copy(core.dstf[:], core.dst[:]).then_inc(converted, 1)


class Marks:

    LINKS = EBODY + 4

    def __init__(self, core, ph, keyf, once, of="", spare="c_spare"):
        self.core, self.ph, self.keyf, self.once, self.spare_name = core, ph, keyf, once, spare
        self.earlier, self.spare = ph.sb(of + "earlier", [P, P]), ph.sb(of + "spare", [P, 1])
        self.before = ph.sb(of + "before", [P, EBODY, P])
        self.count, self.shift = ph.sb(of + "count", [P, EBODY]), ph.sb(of + "shift", [P, EBODY])
        self.const, self.marked = ph.sem(of + "mark_const"), ph.done(of + "marked", 1)

    def load(self, sp):
        sp.dma_start(self.earlier[:], self.core.a["c_earlier"]).then_inc(self.const, 16)
        sp.dma_start(self.spare[:], self.core.a[self.spare_name]).then_inc(self.const, 16)
        sp.wait_ge(self.const, 32)

    def compare(self, chain, keys, o, k):
        chain(self.core.nc.vector.scalar_tensor_tensor(self.before[:, k, :], keys, self.keyf[:, bass.ds(o * EBODY + k, 1)], self.earlier[:],
                                                       ALU.is_equal, ALU.mult))

    def finish(self, v, chain, o):
        nc = self.core.nc
        mine = bass.ds(o * EBODY, EBODY)

        def link(ins):
            chain.link(ins)
            v.sem_inc(self.ph.spent, 1)

        chain.settle()
        v.sem_inc(self.ph.spent, 1)
        link(nc.vector.tensor_reduce(self.count[:], self.before[:], AX.X, ALU.add))
        chain(nc.vector.tensor_scalar(self.count[:], self.count[:], 0.0, None, ALU.is_gt))
        link(nc.vector.tensor_scalar(self.shift[:], self.keyf[:, mine], self.spare[:, 0:1], -1.0, ALU.subtract, ALU.mult))
        link(nc.vector.tensor_tensor(self.shift[:], self.shift[:], self.count[:], ALU.mult))
        nc.vector.tensor_tensor(self.once[:, mine], self.keyf[:, mine], self.shift[:], ALU.add).then_inc(self.marked.sem, 1)


def clear(core, sp, tables, cleared):
    for t in tables:
        width = t.shape[1]
        sp.dma_start(t.rearrange("(p t) d -> p t d", p=P),
                     core.zero[:, 0:width].unsqueeze(1).to_broadcast([P, NT + 1, width])).then_inc(cleared, 16)
    if tables:
        sp.wait_ge(cleared, 16 * len(tables))


def layer_norm(core, name, buf, out, outT=None, rows=True, token_affine=None, feature_affine=None, add_to_x=False, add_xn=False, tables=()):
    nc, a = core.nc, core.a
    with Phase(nc, name) as ph:
        halves = ph.sb("halves", [P, NT, 6])
        stat = ph.sb("stat", [P, 5, NT])
        tile = ph.sb("tile", [P, BODY, D])
        mean, var, rstd, half, gap = (stat[:, i, :] for i in range(5))
        gamma = beta = gcol = bcol = None
        loads = []
        if token_affine:
            gamma, beta = ph.sb("gamma", [P, D]), ph.sb("beta", [P, D])
            loads = [(gamma, a[token_affine[0]].partition_broadcast(P)), (beta, a[token_affine[1]].partition_broadcast(P))]
        if feature_affine:
            gcol, bcol = ph.sb("gcol", [128, DC]), ph.sb("bcol", [128, DC])
            loads = [(gcol, a[feature_affine[0]]), (bcol, a[feature_affine[1]])]
        loaded, chain_sem, cleared = ph.sem("loaded"), ph.sem("chain"), ph.sem("cleared")
        inverse_ready, root_ready = ph.sem("inverse_ready"), ph.sem("root_ready")
        measured, normed = ph.done("measured", BODY), ph.done("normed", BODY)
        staged, turned, stored, taken = (ph.done(n, BODY) for n in ("staged", "turned", "stored", "taken"))
        banks = [ph.ps(f"bank{k}") for k in range(BODY)] if outT is not None else []
        block = ph.block()

        @block.sync
        def _(sp):
            for to, what in loads:
                sp.dma_start(to[:], what).then_inc(loaded, 16)
            if loads:
                sp.wait_ge(loaded, 16 * len(loads))
            clear(core, sp, tables, cleared)

        @block.vector
        def _(v):
            measured.open(v)
            with v.Fori(0, NODE_LOOPS) as o:
                for k in range(BODY):
                    one = bass.ds(o * BODY + k, 1)
                    nc.vector.bn_stats(halves[:, one, :].rearrange("p o s -> p (o s)"), buf[:, one, :].rearrange("p o d -> p (o d)")).then_inc(measured.sem, 1)
            v.wait_ge(measured.sem, measured.at(NODE_LOOPS - 1, BODY - 1))
            chain = Chain(v, chain_sem)
            link = chain.link
            mean_e, dev_e, mean_o, dev_o = (halves[:, :, i] for i in (1, 2, 4, 5))
            chain(nc.vector.tensor_tensor(mean, mean_e, mean_o, ALU.add))
            chain(nc.vector.tensor_tensor(gap, mean_e, mean_o, ALU.subtract))
            link(nc.vector.tensor_tensor(var, dev_e, dev_o, ALU.add))
            chain(nc.vector.tensor_scalar(mean, mean, 0.5, None, ALU.mult))
            chain(nc.vector.tensor_tensor(gap, gap, gap, ALU.mult))
            link(nc.vector.tensor_scalar(var, var, 1.0 / D, LN_EPS, ALU.mult, ALU.add))
            link(nc.vector.scalar_tensor_tensor(var, gap, 0.25, var, ALU.mult, ALU.add))
            nc.vector.reciprocal(half, var).then_inc(inverse_ready, 1)
            v.wait_ge(root_ready, 1)
            link(nc.vector.tensor_tensor(half, rstd, rstd, ALU.mult))
            link(nc.vector.tensor_tensor(half, half, var, ALU.mult))
            link(nc.vector.tensor_scalar(half, half, -0.5, 1.5, ALU.mult, ALU.add))
            link(nc.vector.tensor_tensor(rstd, rstd, half, ALU.mult))
            if loads:
                v.wait_ge(loaded, 16 * len(loads))
            if outT is None:
                normed.open(v)
                with v.Fori(0, NODE_LOOPS) as o:
                    for k in range(BODY):
                        one = bass.ds(o * BODY + k, 1)
                        nc.vector.tensor_scalar(out[:, one, :], buf[:, one, :], mean[:, one], rstd[:, one], ALU.subtract, ALU.mult).then_inc(normed.sem, 1)
                v.wait_ge(normed.sem, normed.at(NODE_LOOPS - 1, BODY - 1))
                shape = [P, NT, D]
                if token_affine:
                    link(nc.vector.tensor_tensor(out[:], out[:], bcast_mid(gamma[:], shape), ALU.mult))
                    link(nc.vector.tensor_tensor(out[:], out[:], bcast_mid(beta[:], shape), ALU.add))
                if add_xn:
                    link(nc.vector.tensor_tensor(out[:], out[:], core.xn[:], ALU.add))
                if add_to_x:
                    link(nc.vector.tensor_tensor(core.x[:], core.x[:], out[:], ALU.add))
                return
            staged.open(v)
            taken.open(v)
            base = chain.n
            per_body = 2 * BODY if token_affine else 0
            with v.Fori(0, NODE_LOOPS) as o:
                chain = Chain(v, chain_sem, per_body, o, base)
                for k in range(BODY):
                    one = bass.ds(o * BODY + k, 1)
                    ph.hold(v, turned, o, k - BODY)
                    if rows or add_to_x:
                        ph.hold(v, taken, o, k - BODY)
                    ins = nc.vector.tensor_scalar(tile[:, k:k + 1, :], buf[:, one, :], mean[:, one], rstd[:, one], ALU.subtract, ALU.mult)
                    if token_affine:
                        chain(ins)
                    else:
                        ins.then_inc(staged.sem, 1)
                if token_affine:
                    for k in range(BODY):
                        chain.settle(k + 1)
                        v.sem_inc(ph.spent, 1)
                        chain(nc.vector.tensor_tensor(tile[:, k, :], tile[:, k, :], gamma[:], ALU.mult))
                    for k in range(BODY):
                        chain.settle(BODY + k + 1)
                        v.sem_inc(ph.spent, 1)
                        nc.vector.tensor_tensor(tile[:, k, :], tile[:, k, :], beta[:], ALU.add).then_inc(staged.sem, 1)
                for k in range(BODY):
                    one = bass.ds(o * BODY + k, 1)
                    if rows or add_to_x:
                        ph.hold(v, staged, o, k)
                    if rows:
                        nc.vector.tensor_copy(out[:, one, :], tile[:, k:k + 1, :]).then_inc(taken.sem, 1)
                    if add_to_x:
                        nc.vector.tensor_tensor(core.x[:, one, :], core.x[:, one, :], tile[:, k:k + 1, :], ALU.add).then_inc(taken.sem, 1)
                assert chain.n == per_body

        @block.scalar
        def _(act):
            act.wait_ge(inverse_ready, 1)
            nc.scalar.activation(rstd, half, ACT.Sqrt).then_inc(root_ready, 1)
            if outT is None:
                return
            stored.open(act)
            if loads:
                act.wait_ge(loaded, 16 * len(loads))
            with act.Fori(0, NODE_LOOPS) as o:
                for k in range(BODY):
                    ph.hold(act, turned, o, k)
                    there = outT[:, :, columns(o * BODY + k)]
                    if feature_affine:
                        for c in range(DC):
                            ins = nc.scalar.activation(there[:, c, :], banks[k][:, c * P:(c + 1) * P], ACT.Identity,
                                                       scale=gcol[:, c:c + 1], bias=bcol[:, c:c + 1])
                    else:
                        ins = nc.scalar.activation(there, banks[k][:, 0:DC * P].rearrange("p (c n) -> p c n", c=DC), ACT.Copy)
                    ins.then_inc(stored.sem, 1)

        if outT is None:
            return

        @block.tensor
        def _(pe):
            turned.open(pe)
            with pe.Fori(0, NODE_LOOPS) as o:
                for k in range(BODY):
                    ph.hold(pe, staged, o, k)
                    ph.hold(pe, stored, o, k - BODY)
                    for c in range(DC):
                        ins = nc.tensor.transpose(banks[k][:, c * P:(c + 1) * P], tile[:, k, c * 128:(c + 1) * 128], core.ident[0:P, 0:P])
                    ins.then_inc(turned.sem, 1)


def project(core, name, inT, weights, dest, width, bias=None, table=None, feature_scale=None, row_scale=None):
    nc, a = core.nc, core.a
    with Phase(nc, name) as ph:
        w = ph.sb("w", [128, DC, width])
        tile = ph.sb("tile", [128, BODY, DC, P])
        b = ph.sb("b", [P, width]) if bias else None
        fs = ph.sb("fs", [128, DC]) if feature_scale else None
        loaded, saved, scaled = ph.sem("loaded"), ph.sem("saved"), ph.sem("scaled")
        staged, product, kept = ph.done("staged", BODY), ph.done("product", BODY), ph.done("kept", BODY)
        banks = [ph.ps(f"bank{k}") for k in range(BODY)]
        nload = len(weights) + (len(bias) if bias else 0) + (1 if feature_scale else 0)
        block = ph.block()

        @block.sync
        def _(sp):
            at = 0
            for wname, n in weights:
                sp.dma_start(w[:, :, at:at + n], feature_rows(a[wname])).then_inc(loaded, 16)
                at += n
            at = 0
            for bname, n in bias or []:
                sp.dma_start(b[:, at:at + n], a[bname].partition_broadcast(P)).then_inc(loaded, 16)
                at += n
            if feature_scale:
                sp.dma_start(fs[:], a[feature_scale]).then_inc(loaded, 16)
            sp.wait_ge(loaded, 16 * nload)
            if table is not None:
                sp.wait_ge(kept.sem, kept.at(NODE_LOOPS - 1, BODY - 1))
                sp.dma_start(nodes(table), dest[:]).then_inc(saved, 16)
                sp.wait_ge(saved, 16)

        @block.gpsimd
        def _(pool):
            staged.open(pool)
            with pool.Fori(0, NODE_LOOPS) as o:
                for k in range(BODY):
                    ph.hold(pool, product, o, k - BODY)
                    nc.gpsimd.tensor_copy(tile[:, k, :, :], inT[:, :, columns(o * BODY + k)]).then_inc(staged.sem, 1)

        @block.tensor
        def _(pe):
            product.open(pe)
            pe.wait_ge(loaded, 16 * nload)
            if feature_scale:
                pe.wait_ge(scaled, DC)
            with pe.Fori(0, NODE_LOOPS) as o:
                for k in range(BODY):
                    ph.hold(pe, staged, o, k)
                    ph.hold(pe, kept, o, k - BODY)
                    for c in range(DC):
                        ins = nc.tensor.matmul(banks[k][0:P, 0:width], tile[:, k, c, :], w[:, c, :], start=c == 0, stop=c == DC - 1)
                    ins.then_inc(product.sem, 1)

        if row_scale is not None:
            @block.vector
            def _(v):
                kept.open(v)
                v.wait_ge(loaded, 16 * nload)
                for c in range(DC):
                    nc.vector.tensor_scalar(w[:, c, :], w[:, c, :], fs[:, c:c + 1], None, ALU.mult).then_inc(scaled, 1)
                with v.Fori(0, NODE_LOOPS) as o:
                    for k in range(BODY):
                        ph.hold(v, product, o, k)
                        nc.vector.tensor_scalar(dest[:, bass.ds(o * BODY + k, 1), :], banks[k][0:P, 0:width].unsqueeze(1),
                                                row_scale[:, bass.ds(o * BODY + k, 1)], None, ALU.mult).then_inc(kept.sem, 1)
        elif bias:
            @block.vector
            def _(v):
                kept.open(v)
                v.wait_ge(loaded, 16 * nload)
                with v.Fori(0, NODE_LOOPS) as o:
                    for k in range(BODY):
                        ph.hold(v, product, o, k)
                        nc.vector.tensor_tensor(dest[:, bass.ds(o * BODY + k, 1), :], banks[k][0:P, 0:width].unsqueeze(1),
                                                b[:].unsqueeze(1), ALU.add).then_inc(kept.sem, 1)
        else:
            @block.scalar
            def _(act):
                kept.open(act)
                with act.Fori(0, NODE_LOOPS) as o:
                    for k in range(BODY):
                        ph.hold(act, product, o, k)
                        nc.scalar.activation(dest[:, bass.ds(o * BODY + k, 1), :], banks[k][0:P, 0:width].unsqueeze(1),
                                             ACT.Copy).then_inc(kept.sem, 1)


def spread(core, name, table, gather_index, key_rows, keyf, once, tables, weight=None, alpha=None, heads=0, mark=False, pairs=None):
    nc, a = core.nc, core.a
    width = D + heads
    with Phase(nc, name) as ph:
        gather_at = ph.sb("gather_at", [P, EBODY], I32)
        scatter_at = ph.sb("scatter_at", [P, EBODY], I32)
        rows = ph.sb("rows", [P, EBODY, D])
        keys = ph.sb("keys", [P, EBODY, P], I32)
        same = ph.sb("same", [P, EBODY, P])
        message = ph.sb("message", [P, EBODY, width]) if heads else rows
        total = ph.sb("total", [P, EBODY, width])
        gathered = [ph.sem(f"gathered{k}") for k in range(EBODY)]
        keys_in = ph.sem("keys_in")
        scattered = [ph.sem(f"scattered{k}") for k in range(EBODY)]
        gather_set, scatter_set = ph.done("gather_set", EBODY), ph.done("scatter_set", EBODY)
        compared, scaled = ph.done("compared", EBODY), ph.done("scaled", EBODY)
        summed, total_set = ph.done("summed", EBODY), ph.done("total_set", EBODY)
        banks = [ph.ps(f"bank{k}") for k in range(EBANKS)]
        marks = Marks(core, ph, keyf, once) if mark else None
        if pairs:
            pair_marks = Marks(core, ph, pairs[1], core.pair_once, "pair_", "c_pair_spare")
            pair_keys = ph.sb("pair_keys", [P, EBODY, P])
            pair_same = ph.sb("pair_same", [P, EBODY, P])
            wide_zero = ph.sb("wide_zero", [P, N * (N + 1) // (P * EDGE_LOOPS)])
            pair_keys_in, zeroed, cleared = ph.sem("pair_keys_in"), ph.sem("zeroed"), ph.sem("cleared")
            pair_compared, pair_summed, pair_kept = ph.done("pair_compared", EBODY), ph.done("pair_summed", EBODY), ph.done("pair_kept", 1)
            pair_bank = ph.ps("pair_bank")
        chain_sem = ph.sem("chain")
        gathers = gather_index is not None
        last = EDGE_LOOPS - 1
        table_of = table_turns(len(tables))
        block = ph.block()

        @block.sync
        def _(sp):
            if mark:
                marks.load(sp)
            if pairs:
                pair_marks.load(sp)
                sp.wait_ge(zeroed, 1)
            with sp.Fori(0, EDGE_LOOPS) as o:
                ph.hold(sp, compared, o, -1)
                sp.dma_start(keys[:], key_rows[bass.ds(o * EBODY * P, EBODY * P)].partition_broadcast(P)
                             .rearrange("p (k e) -> p k e", k=EBODY)).then_inc(keys_in, 16)
                if pairs:
                    ph.hold(sp, pair_marks.marked, o, -1)
                    sp.dma_start(pair_keys[:], pairs[0][bass.ds(o * EBODY * P, EBODY * P)].partition_broadcast(P)
                                 .rearrange("p (k e) -> p k e", k=EBODY)).then_inc(pair_keys_in, 16)
                    sp.dma_start(core.adjacency.rearrange("(p t r) o -> p t (r o)", p=P, t=EDGE_LOOPS)[:, bass.ds(o, 1), :], wide_zero[:].unsqueeze(1)).then_inc(cleared, 16)
                if not gathers:
                    for k in range(EBODY):
                        ph.hold(sp, scaled if heads else summed, o, k - EBODY)
                        sp.dma_start(rows[:, k, :], table[bass.ds((o * EBODY + k) * P, P), :]).then_inc(gathered[k], 16)
            if pairs:
                sp.wait_ge(cleared, 16 * EDGE_LOOPS)

        @block.gpsimd
        def _(pool):
            def gather(k):
                nc.gpsimd.indirect_dma_start(rows[:, k, :], None, table, bass.IndirectOffsetOnAxis(ap=gather_at[:, k:k + 1], axis=0)).then_inc(gathered[k], 16)

            def scatter(o, k):
                ph.hold(pool, scatter_set, o, k)
                ph.hold(pool, total_set, o, k)
                before = max((j for j in range(k) if table_of[j] == table_of[k]), default=None)
                if before is not None:
                    ph.hold_dma(pool, scattered[before], o)
                elif not (isinstance(o, int) and o == 0):
                    ph.hold_dma(pool, scattered[max(j for j in range(EBODY) if table_of[j] == table_of[k])], o - 1)
                nc.gpsimd.indirect_dma_start(tables[table_of[k]], bass.IndirectOffsetOnAxis(ap=scatter_at[:, k:k + 1], axis=0),
                                             total[:, k, :], None, compute_op=ALU.add).then_inc(scattered[k], 16)

            def next_gather(o, k):
                ph.hold(pool, gather_set, o + 1, k)
                ph.hold(pool, scaled if heads else summed, o, k)
                gather(k)

            if gathers:
                for k in range(EBODY):
                    ph.hold(pool, gather_set, 0, k)
                    gather(k)
            for k in range(EBODY):
                scatter(0, k)
                if gathers:
                    next_gather(0, k)
            with pool.Fori(1, last) as o:
                for k in range(EBODY):
                    scatter(o, k)
                    if gathers:
                        next_gather(o, k)
            for k in range(EBODY):
                scatter(last, k)
            for k in range(EBODY):
                pool.wait_ge(scattered[k], 16 * EDGE_LOOPS)

        @block.vector
        def _(v):
            compared.open(v)
            if heads:
                scaled.open(v)
            if mark:
                marks.marked.open(v)
                v.wait_ge(marks.const, 32)
            links = Marks.LINKS * (2 if pairs else 1)
            if pairs:
                nc.vector.memset(wide_zero[:], 0.0).then_inc(zeroed, 1)
                pair_marks.marked.open(v)
                pair_compared.open(v)
                v.wait_ge(pair_marks.const, 32)
            with v.Fori(0, EDGE_LOOPS) as o:
                chain = Chain(v, chain_sem, links, o)
                ph.hold_dma(v, keys_in, o)
                for k in range(EBODY):
                    one = bass.ds(o * EBODY + k, 1)
                    if mark:
                        marks.compare(chain, keys[:, k, :], o, k)
                    ph.hold(v, summed, o, k - EBODY)
                    if heads:
                        nc.vector.tensor_scalar(same[:, k, :], keys[:, k, :], keyf[:, one], None, ALU.is_equal).then_inc(compared.sem, 1)
                        ph.hold_dma(v, gathered[k], o)
                        nc.vector.tensor_copy(message[:, k:k + 1, D:width], alpha[:, one, :])
                        nc.vector.tensor_tensor(message[:, k, 0:D].rearrange("p (h d) -> p h d", h=heads), rows[:, k, :].rearrange("p (h d) -> p h d", h=heads),
                                                alpha[:, one, :].rearrange("p o h -> p (o h)").unsqueeze(2).to_broadcast([P, heads, D // heads]), ALU.mult).then_inc(scaled.sem, 1)
                    else:
                        nc.vector.tensor_scalar(same[:, k, :], keys[:, k, :], keyf[:, one], weight[:, one], ALU.is_equal, ALU.mult).then_inc(compared.sem, 1)
                if mark:
                    marks.finish(v, chain, o)
                if pairs:
                    ph.hold_dma(v, pair_keys_in, o)
                    for k in range(EBODY):
                        pair_marks.compare(chain, pair_keys[:, k, :], o, k)
                        ph.hold(v, pair_summed, o, k - EBODY)
                        nc.vector.tensor_scalar(pair_same[:, k, :], pair_keys[:, k, :], pairs[1][:, bass.ds(o * EBODY + k, 1)], None, ALU.is_equal).then_inc(pair_compared.sem, 1)
                    pair_marks.finish(v, chain, o)
                    assert chain.n == links

        @block.tensor
        def _(pe):
            summed.open(pe)
            if pairs:
                pair_summed.open(pe)
            with pe.Fori(0, EDGE_LOOPS) as o:
                for k in range(EBODY):
                    ph.hold(pe, compared, o, k)
                    if heads:
                        ph.hold(pe, scaled, o, k)
                    else:
                        ph.hold_dma(pe, gathered[k], o)
                    ph.hold(pe, total_set, o, slot_owner(EBANKS, EBODY, k))
                    nc.tensor.matmul(banks[k % EBANKS][0:P, 0:width], same[:, k, :], message[:, k, :], start=True, stop=True).then_inc(summed.sem, 1)
                if pairs:
                    ph.hold(pe, pair_kept, o, -1)
                    for k in range(EBODY):
                        ph.hold(pe, pair_compared, o, k)
                        nc.tensor.matmul(pair_bank[0:P, k:k + 1], pair_same[:, k, :], weight[:, bass.ds(o * EBODY + k, 1)], start=True, stop=True).then_inc(pair_summed.sem, 1)

        @block.scalar
        def _(act):
            gather_set.open(act)
            scatter_set.open(act)
            total_set.open(act)

            def set_gather(o, k):
                nc.scalar.activation(gather_at[:, k:k + 1], gather_index[:, bass.ds(o * EBODY + k, 1)], ACT.Copy).then_inc(gather_set.sem, 1)

            def finish(o, k):
                if not (isinstance(o, int) and o == 0):
                    ph.hold_dma(act, scattered[k], o - 1)
                if mark and k == 0:
                    ph.hold(act, marks.marked, o, 0)
                nc.scalar.activation(scatter_at[:, k:k + 1], once[:, bass.ds(o * EBODY + k, 1)], ACT.Copy).then_inc(scatter_set.sem, 1)
                ph.hold(act, summed, o, k)
                nc.scalar.activation(total[:, k, :], banks[k % EBANKS][0:P, 0:width], ACT.Copy).then_inc(total_set.sem, 1)

            def keep_pairs(o):
                if pairs:
                    ph.hold(act, pair_summed, o, EBODY - 1)
                    nc.scalar.activation(core.pair_weight[:, bass.ds(o * EBODY, EBODY)], pair_bank[0:P, 0:EBODY], ACT.Copy).then_inc(pair_kept.sem, 1)

            if pairs:
                pair_kept.open(act)
            if gathers:
                for k in range(EBODY):
                    set_gather(0, k)
            for k in range(EBODY):
                finish(0, k)
                if gathers:
                    set_gather(1, k)
            keep_pairs(0)
            with act.Fori(1, last) as o:
                for k in range(EBODY):
                    finish(o, k)
                    if gathers:
                        set_gather(o + 1, k)
                keep_pairs(o)
            for k in range(EBODY):
                finish(last, k)
            keep_pairs(last)


def table_turns(count):
    if EBODY % (count - 1) == 1:
        return [k % (count - 1) for k in range(EBODY - 1)] + [count - 1]
    return [k % count for k in range(EBODY)]


class TableSum:

    def __init__(self, ph, tables, width):
        self.tables = tables
        self.parts = [ph.sb(f"part{i}", [P, NT, width]) for i in range(PARTS)]
        self.part_in = [ph.sem(f"part_in{i}") for i in range(PARTS)]
        self.added = ph.sem("added")
        self.total = self.parts[0]

    def slot(self, i):
        return 0 if i == 0 else 1 + (i - 1) % (PARTS - 1)

    def load(self, sp):
        for i, t in enumerate(self.tables):
            if i >= PARTS:
                sp.wait_ge(self.added, i - (PARTS - 1))
            sp.dma_start(self.parts[self.slot(i)][:], nodes(t[0:N, :])).then_inc(self.part_in[self.slot(i)], 16)

    def add(self, v, nc):
        v.wait_ge(self.part_in[0], 16)
        for i in range(1, len(self.tables)):
            v.wait_ge(self.part_in[self.slot(i)], 16 * (1 + (i - 1) // (PARTS - 1)))
            nc.vector.tensor_tensor(self.total[:], self.total[:], self.parts[self.slot(i)][:], ALU.add).then_inc(self.added, 1)
            v.wait_ge(self.added, i)


def finish_elu(core, name, tables):
    nc = core.nc
    with Phase(nc, name) as ph:
        table_sum = TableSum(ph, tables, D)
        parts = table_sum.parts
        low_ready, grown, chain_sem = ph.sem("low_ready"), ph.sem("grown"), ph.sem("chain")
        block = ph.block()

        @block.sync
        def _(sp):
            table_sum.load(sp)

        @block.vector
        def _(v):
            chain = Chain(v, chain_sem)
            table_sum.add(v, nc)
            nc.vector.tensor_scalar(parts[1][:], parts[0][:], 0.0, None, ALU.min).then_inc(low_ready, 1)
            chain.link(nc.vector.scalar_tensor_tensor(core.x[:], parts[0][:], 0.0, core.x[:], ALU.max, ALU.add))
            v.wait_ge(grown, 1)
            chain.link(nc.vector.scalar_tensor_tensor(core.x[:], parts[1][:], -1.0, core.x[:], ALU.add, ALU.add))

        @block.scalar
        def _(act):
            act.wait_ge(low_ready, 1)
            nc.scalar.activation(parts[1][:], parts[1][:], ACT.Exp).then_inc(grown, 1)


def pair_keys(core, pairf, pair_rows):
    nc, a = core.nc, core.a
    ROUND = 1.5 * 2.0 ** 23
    assert N * (N + 1) < 2 ** 24
    with Phase(nc, "keys") as ph:
        raw = ph.sb("raw", [P, 2, ET], I32)
        ends = ph.sb("ends", [P, 2, 2, ET])
        high, low = ph.sb("high", [P, 2, ET]), ph.sb("low", [P, 2, ET])
        key = ph.sb("key", [P, 2, ET])
        loaded, made, saved, chain_sem = ph.sem("loaded"), ph.sem("made"), ph.sem("saved"), ph.sem("chain")
        block = ph.block()

        @block.sync
        def _(sp):
            for i, name in enumerate(("src_rows", "dst_rows")):
                sp.dma_start(raw[:, i, :], a[name].rearrange("(p e) -> p e", p=P)).then_inc(loaded, 16)
            sp.wait_ge(made, 1)
            sp.dma_start(pair_rows.rearrange("(p e) -> p e", p=P), key[:, 1, :]).then_inc(saved, 16)
            sp.wait_ge(saved, 16)

        @block.vector
        def _(v):
            chain = Chain(v, chain_sem)
            link = chain.link
            chain(nc.vector.tensor_copy(ends[:, 0, 0, :], core.srcf[:]))
            chain(nc.vector.tensor_copy(ends[:, 1, 0, :], core.dstf[:]))
            v.wait_ge(loaded, 32)
            link(nc.vector.tensor_copy(ends[:, :, 1, :], raw[:]))
            src, dst = ends[:, 0], ends[:, 1]
            link(nc.vector.tensor_scalar(high[:], src, (NT - 1) / 2, 1.0 / NT, ALU.subtract, ALU.mult))
            link(nc.vector.tensor_scalar(high[:], high[:], ROUND, None, ALU.add))
            link(nc.vector.tensor_scalar(high[:], high[:], ROUND, None, ALU.subtract))
            link(nc.vector.scalar_tensor_tensor(low[:], high[:], -float(NT), src, ALU.mult, ALU.add))
            link(nc.vector.scalar_tensor_tensor(high[:], low[:], float(P), high[:], ALU.mult, ALU.add))
            link(nc.vector.scalar_tensor_tensor(key[:], dst, float(N), high[:], ALU.mult, ALU.add))
            chain(nc.vector.tensor_copy(pairf[:], key[:, 0, :]))
            chain.settle()
            v.sem_inc(made, 1)


class AdjacencyBuild:

    def __init__(self, core, steps):
        self.core, self.steps = core, steps

    def place(self, ph):
        self.ph = ph
        self.element, self.weight = ph.sb("element", [P, 2], I32), ph.sb("edge_weight", [P, 2])
        self.landed, self.set_ = ph.sem("landed"), ph.done("element_set", EBODY)

    def run(self, pool):
        nc, core, first = self.core.nc, self.core, self.steps[0]
        self.set_.open(pool)
        with pool.Fori(*self.steps) as o:
            for k in range(EBODY):
                slot = k % 2
                one = bass.ds(o * EBODY + k, 1)
                nc.gpsimd.tensor_copy(self.element[:, slot:slot + 1], core.pair_once[:, one])
                nc.gpsimd.tensor_copy(self.weight[:, slot:slot + 1], core.pair_weight[:, one]).then_inc(self.set_.sem, 1)
                self.ph.hold(pool, self.set_, o - first, k)
                if k:
                    pool.wait_ge(self.landed, ((o - first) * EBODY + k) * 16)
                    pool.sem_inc(self.ph.spent, 1)
                nc.gpsimd.indirect_dma_start(core.adjacency, bass.IndirectOffsetOnAxis(ap=self.element[:, slot:slot + 1], axis=0),
                                             self.weight[:, slot:slot + 1], None, compute_op=ALU.add).then_inc(self.landed, 16)
            pool.wait_ge(self.landed, ((o - first) * EBODY + EBODY) * 16)
            pool.sem_inc(self.ph.spent, 1)


def gnn0(core):
    h, pair_rows = core.table("h0", N, D), core.nc.dram_tensor("pair_rows", (ET * P,), F32, kind="Internal").ap()
    with Phase(core.nc, "g0") as ph:
        src_once, pairf = ph.sb("src_once", [P, ET], I32), ph.sb("pairf", [P, ET])
        pair_keys(core, pairf, pair_rows)
        with Phase(core.nc, "g0_h") as inner:
            dest = inner.sb("h", [P, NT, D])
            project(core, "proj0", core.xnT, [("L0_gnn_W", D)], dest, D, bias=[("L0_gnn_b", D)], table=h)
        spread(core, "spread0", h, core.dst, core.a["src_rows"], core.srcf, src_once, core.sums[0], weight=core.weight, mark=True,
               pairs=(pair_rows, pairf))
    finish_elu(core, "fin0", core.sums[0])


def linear_attention(core, name, wq, wkv, wo, target, bias=None, clamp=None, plus=None, length=1.0, add=True, beside=None):
    nc, a = core.nc, core.a
    KV = 2 * D
    with Phase(nc, name) as ph:
        context, keysum = ph.sb("context", [128, DC, 128]), ph.sb("keysum", [128, DC, 128])
        wk = ph.sb("wk", [128, DC, KV])
        b = ph.sb("b", [P, KV]) if bias else None
        tile = ph.sb("tile", [128, BODY, DC, P])
        kv = ph.sb("kv", [P, BODY, KV + 1])
        klow, kgrown, keymap = (ph.sb(n, [P, BODY, D]) for n in ("klow", "kgrown", "keymap"))
        w, wout, bq = ph.sb("w", [128, DC, D]), ph.sb("wout", [128, DC, D]), ph.sb("bq", [128, DC])
        low, pos, grown, query = (ph.sb(n, [128, 2, DC, RUNMAX]) for n in ("low", "pos", "grown", "query"))
        inverse = ph.sb("inverse", [128, 2, RUNMAX])
        outT = ph.sb("outT", [128, 2, DC, RUNMAX])
        if beside:
            beside.place(ph)
        loaded, ones, closed, context_ready, chain_sem = (ph.sem(n) for n in ("loaded", "ones", "closed", "context_ready", "chain"))
        staged, product, kkept = ph.done("staged", BODY), ph.done("product", BODY), ph.done("kkept", BODY)
        klow_set, kgrown_set, kmapped, added = (ph.done(n, BODY) for n in ("klow_set", "kgrown_set", "kmapped", "added"))
        projected, low_set, grown_set, mapped = (ph.done(n, 4) for n in ("projected", "low_set", "grown_set", "mapped"))
        read, divided, result, kept = ph.done("read", 4), ph.done("divided", 4), ph.done("result", BODY), ph.done("kept", BODY)
        banks = [ph.ps(f"bank{k}") for k in range(BODY)]
        sums = [ph.ps(f"sums{k}") for k in range(DC)]
        qbank, numbank, denbank, obank = banks[0:4], banks[4], ph.ps("den"), sums
        nload = len(wkv) + 2 + (3 if bias else 0)
        block = ph.block()

        @block.sync
        def _(sp):
            for i, (wname, cols) in enumerate(wkv):
                n = KV // len(wkv)
                sp.dma_start(wk[:, :, i * n:(i + 1) * n], feature_rows(a[wname] if cols is None else a[wname][:, cols])).then_inc(loaded, 16)
            if bias:
                for i in range(2):
                    sp.dma_start(b[:, i * D:(i + 1) * D], a[bias[1 + i]].partition_broadcast(P)).then_inc(loaded, 16)
                sp.dma_start(bq[:], a[bias[0]]).then_inc(loaded, 16)
            sp.dma_start(w[:], feature_rows(a[wq])).then_inc(loaded, 16)
            sp.dma_start(wout[:], feature_rows(a[wo])).then_inc(loaded, 16)
            sp.wait_ge(loaded, 16 * nload)
            if beside:
                beside.store(sp)

        @block.gpsimd
        def _(pool):
            staged.open(pool)
            nc.gpsimd.memset(kv[:, :, KV:KV + 1], 1.0).then_inc(ones, 1)
            with pool.Fori(0, NODE_LOOPS) as o:
                if beside:
                    beside.gather(pool, o)
                for k in range(BODY):
                    ph.hold(pool, product, o, k - BODY)
                    nc.gpsimd.tensor_copy(tile[:, k, :, :], core.xnT[:, :, columns(o * BODY + k)]).then_inc(staged.sem, 1)
            if beside:
                with pool.Fori(NODE_LOOPS, EDGE_LOOPS) as o:
                    beside.gather(pool, o)

        @block.tensor
        def _(pe):
            for d in (product, added, projected, read, result):
                d.open(pe)
            pe.wait_ge(loaded, 16 * nload)
            for c in range(DC):
                nc.tensor.matmul(sums[c][:, 0:D + 1], core.zero[:, 0:128], core.zero[:, 0:D + 1], start=True, stop=False, skip_group_check=True)
            pe.wait_ge(ones, 1)
            with pe.Fori(0, NODE_LOOPS) as o:
                for k in range(BODY):
                    ph.hold(pe, staged, o, k)
                    ph.hold(pe, kkept, o, k - BODY)
                    for c in range(DC):
                        ins = nc.tensor.matmul(banks[k][0:P, :], tile[:, k, c, :], wk[:, c, :], start=c == 0, stop=c == DC - 1)
                    ins.then_inc(product.sem, 1)
                for k in range(BODY):
                    ph.hold(pe, kmapped, o, k)
                    for c in range(DC):
                        ins = nc.tensor.matmul(sums[c][:, 0:D + 1], keymap[:, k, c * 128:(c + 1) * 128], kv[:, k, D:KV + 1],
                                               start=False, stop=False, skip_group_check=True)
                    ins.then_inc(added.sem, 1)
            for c in range(DC):
                ins = nc.tensor.matmul(sums[c][:, 0:D + 1], core.zero[:, 0:128], core.zero[:, 0:D + 1], start=False, stop=True, skip_group_check=True)
            ins.then_inc(closed, 1)
            pe.wait_ge(context_ready, DC)
            with pe.Fori(0, NODE_LOOPS) as o:
                for s, (first, m) in enumerate(RUNS):
                    for mo in range(DC):
                        i = s * DC + mo
                        ph.hold(pe, mapped, o, i - 4)
                        for c in range(DC):
                            ins = nc.tensor.matmul(qbank[i][:, 0:m * P], w[:, c, mo * 128:(mo + 1) * 128],
                                                   core.xnT[:, c, columns(o * BODY + first, m)], start=c == 0, stop=c == DC - 1)
                        ins.then_inc(projected.sem, 1)
                for s, (first, m) in enumerate(RUNS):
                    for c in range(DC):
                        i = s * DC + c
                        ph.hold(pe, mapped, o, i)
                        ph.hold(pe, divided, o, i - 1)
                        nc.tensor.matmul(numbank[:, 0:m * P], context[:, c, :], query[:, s, c, 0:m * P], start=True, stop=True)
                        nc.tensor.matmul(denbank[:, 0:m * P], keysum[:, c, :], query[:, s, c, 0:m * P], start=True, stop=True).then_inc(read.sem, 1)
                for s, (first, m) in enumerate(RUNS):
                    ph.hold(pe, divided, o, s * DC + DC - 1)
                    for j in range(m):
                        i = first + j
                        ph.hold(pe, kept, o, i - 2)
                        for c in range(DC):
                            ins = nc.tensor.matmul(obank[i % 2][0:P, 0:D], outT[:, s, c, j * P:(j + 1) * P], wout[:, c, :], start=c == 0, stop=c == DC - 1)
                        ins.then_inc(result.sem, 1)

        @block.vector
        def _(v):
            for d in (kkept, klow_set, kmapped, low_set, mapped, divided, kept):
                d.open(v)
            v.wait_ge(loaded, 16 * nload)
            with v.Fori(0, NODE_LOOPS) as o:
                for k in range(BODY):
                    ph.hold(v, product, o, k)
                    ph.hold(v, added, o, k - BODY)
                    if bias:
                        nc.vector.tensor_tensor(kv[:, k, 0:KV], banks[k][0:P, :], b[:], ALU.add).then_inc(kkept.sem, 1)
                    else:
                        nc.vector.tensor_copy(kv[:, k, 0:KV], banks[k][0:P, :]).then_inc(kkept.sem, 1)
                    ph.hold(v, kkept, o, k)
                    nc.vector.tensor_scalar(klow[:, k, :], kv[:, k, 0:D], 0.0, None, ALU.min).then_inc(klow_set.sem, 1)
                for k in range(BODY):
                    ph.hold(v, kgrown_set, o, k)
                    nc.vector.scalar_tensor_tensor(keymap[:, k, :], kv[:, k, 0:D], 0.0, kgrown[:, k, :], ALU.max, ALU.add).then_inc(kmapped.sem, 1)
            v.wait_ge(closed, 1)
            for c in range(DC):
                nc.vector.scalar_tensor_tensor(context[:, c, :], sums[c][:, c * 128:(c + 1) * 128], 1.0 / length, core.heads[:], ALU.mult, ALU.mult)
                nc.vector.tensor_scalar(keysum[:, c, :], core.heads[:], sums[c][:, D:D + 1], None, ALU.mult).then_inc(context_ready, 1)
            per_body = 2 * 4 + 4
            with v.Fori(0, NODE_LOOPS) as o:
                chain = Chain(v, chain_sem, per_body, o)
                for s, (first, m) in enumerate(RUNS):
                    for mo in range(DC):
                        i, n = s * DC + mo, m * P
                        ph.hold(v, projected, o, i)
                        bcol = bq[:, mo:mo + 1] if bias else 0.0
                        chain(nc.vector.tensor_scalar(pos[:, s, mo, 0:n], qbank[i][:, 0:n], bcol, 0.0, ALU.add, ALU.max))
                        nc.vector.tensor_scalar(low[:, s, mo, 0:n], qbank[i][:, 0:n], bcol, 0.0, ALU.add, ALU.min).then_inc(low_set.sem, 1)
                for s, (first, m) in enumerate(RUNS):
                    for mo in range(DC):
                        i, n = s * DC + mo, m * P
                        ph.hold(v, grown_set, o, i)
                        ph.hold(v, read, o, i - 4)
                        nc.vector.tensor_tensor(query[:, s, mo, 0:n], pos[:, s, mo, 0:n], grown[:, s, mo, 0:n], ALU.add).then_inc(mapped.sem, 1)
                for s, (first, m) in enumerate(RUNS):
                    for c in range(DC):
                        i, n = s * DC + c, m * P
                        ph.hold(v, read, o, i)
                        if clamp is not None:
                            chain(nc.vector.tensor_scalar(inverse[:, s, 0:n], denbank[:, 0:n], clamp, None, ALU.max))
                        else:
                            chain(nc.vector.tensor_scalar(inverse[:, s, 0:n], denbank[:, 0:n], plus, None, ALU.add))
                        chain.settle()
                        v.sem_inc(ph.spent, 1)
                        chain(nc.vector.reciprocal(inverse[:, s, 0:n], inverse[:, s, 0:n]))
                        chain.settle()
                        v.sem_inc(ph.spent, 1)
                        if c == 0:
                            ph.hold(v, result, o, first + m - 1 - BODY)
                        nc.vector.scalar_tensor_tensor(outT[:, s, c, 0:n], numbank[:, 0:n], length, inverse[:, s, 0:n], ALU.mult, ALU.mult).then_inc(divided.sem, 1)
                for s, (first, m) in enumerate(RUNS):
                    for j in range(m):
                        i = first + j
                        row = target[:, bass.ds(o * BODY + i, 1), :]
                        ph.hold(v, result, o, i)
                        if add:
                            nc.vector.tensor_tensor(row, row, obank[i % 2][0:P, 0:D].unsqueeze(1), ALU.add).then_inc(kept.sem, 1)
                        else:
                            nc.vector.tensor_scalar(row, obank[i % 2][0:P, 0:D].unsqueeze(1), 0.0, None, ALU.add).then_inc(kept.sem, 1)
                assert chain.n == per_body

        @block.scalar
        def _(act):
            kgrown_set.open(act)
            grown_set.open(act)
            if beside:
                beside.begin(act)

            def turn(start):
                return act.Fori(start, start + NODE_LOOPS)

            with turn(1) as o:
                if beside:
                    beside.take(act, o)
                for k in range(BODY):
                    ph.hold(act, klow_set, o - 1, k)
                    ph.hold(act, kmapped, o - 1, k - BODY)
                    nc.scalar.activation(kgrown[:, k, :], klow[:, k, :], ACT.Exp).then_inc(kgrown_set.sem, 1)
            with turn(1 + NODE_LOOPS) as o:
                step = o - (1 + NODE_LOOPS)
                if beside:
                    beside.take(act, o)
                for s, (first, m) in enumerate(RUNS):
                    for mo in range(DC):
                        i, n = s * DC + mo, m * P
                        ph.hold(act, low_set, step, i)
                        ph.hold(act, mapped, step, i - 4)
                        nc.scalar.activation(grown[:, s, mo, 0:n], low[:, s, mo, 0:n], ACT.Exp).then_inc(grown_set.sem, 1)
            if beside:
                with act.Fori(1 + 2 * NODE_LOOPS, EDGE_LOOPS) as o:
                    beside.take(act, o)
                beside.end(act)


def start_rows(core, name, target, source, bias):
    nc, a = core.nc, core.a
    with Phase(nc, name) as ph:
        b = ph.sb("b", [P, D])
        loaded = ph.sem("loaded")
        block = ph.block()

        @block.sync
        def _(sp):
            sp.dma_start(b[:], a[bias].partition_broadcast(P)).then_inc(loaded, 16)
            sp.wait_ge(loaded, 16)

        @block.vector
        def _(v):
            v.wait_ge(loaded, 16)
            nc.vector.tensor_tensor(target[:], (target if source is None else source)[:], bcast_mid(b[:], [P, NT, D]), ALU.add)


def routing(kind):
    first = 5
    return {"soft": 3 + 3, "argmax": 3 + 3 + first + 1, "top2prob": 3 + 3 + 2 * first + 1 + 1 + 5, "top2logit": 3 + 2 * first + 1 + 1 + 4}[kind]


def ffn(core, name, sources, hidden, w1, b1, func, w2, target, experts=1, shared=False, gate=None, kind=None, b2=None, norm=None, before=None, tables=(), build=None):
    nc, a = core.nc, core.a
    KC, HC = DC * len(sources), hidden // 128
    groups = 1 if shared else experts
    depth = 2 if norm else 1
    entries = [(s, g) for s in range(2) for g in range(groups)]
    order = []
    for step in range(len(entries) + depth):
        if step < len(entries):
            order.append(("h", 0, step))
        if depth == 2 and 0 <= step - 1 < len(entries):
            order.append(("h", 1, step - 1))
        if 0 <= step - depth < len(entries):
            order.append(("y", None, step - depth))
    score_run = {0: 0, groups // 2: 1} if gate and not shared else {}
    hitems, yitems = [], []
    for what, layer, i in order:
        s, g = entries[i]
        if what == "h":
            hitems += [(layer, i, mo) for mo in range(HC)]
        else:
            yitems += [(i, j, e) for e in (range(experts) if shared else [g]) for j in range(RUNS[s][1])]
            if gate and b2 and g == 0:
                yitems += [(i, j, None) for j in range(RUNS[s][1])]
    hindex = {it: q for q, it in enumerate(hitems)}
    yindex = {it: q for q, it in enumerate(yitems)}
    HR, YR = 4, 3
    EARLY = 4
    HB, YB = len(hitems), len(yitems)
    def last_reader(layer, i):
        if layer + 1 < depth:
            return "h", hindex[(layer + 1, i, HC - 1)]
        return "y", max(q for q, it in enumerate(yitems) if it[0] == i and it[2] is not None)
    def last_update(q):
        i, j, _ = yitems[q]
        s = entries[i][0]
        return max((r for r in range(q) if entries[yitems[r][0]][0] == s and yitems[r][1] == j), default=None)

    with Phase(nc, name) as ph:
        W1 = ph.sb("W1", [128, groups, KC, hidden])
        W1b = ph.sb("W1b", [128, groups, HC, hidden]) if norm else None
        W2 = ph.sb("W2", [128, experts, HC, D])
        hid = [ph.sb(f"hid{layer}", [128, 2, HC, RUNMAX]) for layer in range(depth)]
        b1c = ph.sb("b1c", [128, groups, HC])
        loads = []
        for g in range(groups):
            loads.append((W1[:, g], (a[w1] if groups == 1 else a[w1][g]).rearrange("(c p) h -> p c h", p=128)))
        if norm:
            for g in range(groups):
                loads.append((W1b[:, g], a[norm["w"]][g].rearrange("(c p) h -> p c h", p=128)))
            bn = {n: ph.sb("bn_" + n, [128, groups, HC]) for layer in norm["columns"] for n in layer}
            for layer in norm["columns"]:
                for n in layer:
                    loads.append((bn[n][:], a[n]))
            scale = [ph.sb(f"scale{i}", [128, groups, HC]) for i in range(2)]
            shift = [ph.sb(f"shift{i}", [128, groups, HC]) for i in range(2)]
            root = [ph.sb(f"root{i}", [128, groups, HC]) for i in range(2)]
        elif b1:
            loads.append((b1c[:, 0] if groups == 1 else b1c[:], a[b1]))
        for e in range(experts):
            loads.append((W2[:, e], (a[w2] if experts == 1 else a[w2][e]).rearrange("(c p) d -> p c d", p=128)))
        if gate:
            wg = ph.sb("wg", [128, HC if shared else DC, 8])
            bg = ph.sb("bg", [P, 8])
            loads.append((wg[:], feature_rows(a[gate[0]])))
            if gate[1]:
                loads.append((bg[:], a[gate[1]].partition_broadcast(P)))
            if b2:
                b2r = ph.sb("b2r", [8, D])
                loads.append((b2r[:], a[b2]))
            logitT = ph.sb("logitT", [8, 2, RUNMAX])
            comb = ph.sb("comb", [P, 2, 3, 8])
            combT = ph.sb("combT", [8, 2, RUNMAX])
            work = ph.sb("work", [P, 2, 8, 3, 8])
            col = ph.sb("col", [P, 2, 4, 3])
        loaded, chain_sem, cleared = ph.sem("loaded"), ph.sem("chain"), ph.sem("cleared")
        hid_made, hid_kept = ph.done("hid_made", HB), ph.done("hid_kept", HB)
        out_made, out_kept = ph.done("out_made", YB), ph.done("out_kept", YB)
        scored, score_kept, scores_turned = ph.done("scored", 2), ph.done("score_kept", 2), ph.done("scores_turned", 2)
        centred, grown, routed = ph.done("centred", 2), ph.done("grown", 2), ph.done("routed", 2)
        comb_turned, comb_kept = ph.done("comb_turned", 2), ph.done("comb_kept", 2)
        inverse_ready, root_ready, folded = ph.sem("inverse_ready"), ph.sem("root_ready"), ph.sem("folded")
        if build:
            build.place(ph)
        nload = 16 * len(loads)
        with nc.Block() as prefetch:
            @prefetch.sync
            def _(sp):
                for to, what in loads:
                    sp.dma_start(to, what).then_inc(loaded, 16)

        if before:
            before()
        hbank = [ph.ps(f"h{i}") for i in range(HR)]
        ybank = [ph.ps(f"y{i}") for i in range(YR)]
        gbank = ph.ps("gate") if gate else None
        block = ph.block()

        @block.sync
        def _(sp):
            clear(core, sp, tables, cleared)
            sp.wait_ge(loaded, nload)

        if build:
            @block.gpsimd
            def _(pool):
                build.run(pool)

        @block.tensor
        def _(pe):
            hid_made.open(pe)
            out_made.open(pe)
            for d in (scored, scores_turned, comb_turned):
                d.open(pe)
            pe.wait_ge(loaded, nload)
            with pe.Fori(0, NODE_LOOPS) as o:
                def score(s):
                    first, m = RUNS[s]
                    ph.hold(pe, comb_kept if b2 else routed, o, s - 1)
                    for c in range(DC):
                        ins = nc.tensor.matmul(gbank[0:8, 0:m * P], wg[:, c, :], sources[0][:, c, columns(o * BODY + first, m)], start=c == 0, stop=c == DC - 1)
                    ins.then_inc(scored.sem, 1)

                def turn_scores(s):
                    ph.hold(pe, score_kept, o, s)
                    for j in range(RUNS[s][1]):
                        ins = nc.tensor.transpose(gbank[0:P, 400 + 8 * j:408 + 8 * j], logitT[:, s, j * P:(j + 1) * P], core.ident[0:8, 0:8])
                    ins.then_inc(scores_turned.sem, 1)

                def score_hidden(s, i):
                    ph.hold(pe, routed, o, s - 1)
                    ph.hold(pe, hid_kept, o, hindex[(0, i, HC - 1)])
                    for j in range(RUNS[s][1]):
                        for c in range(HC):
                            ins = nc.tensor.matmul(gbank[0:P, 400 + 8 * j:408 + 8 * j], hid[0][:, i % 2, c, j * P:(j + 1) * P], wg[:, c, :], start=c == 0, stop=c == HC - 1)
                    ins.then_inc(scores_turned.sem, 1)

                def turn_comb(s):
                    ph.hold(pe, routed, o, s)
                    for j in range(RUNS[s][1]):
                        ins = nc.tensor.transpose(gbank[0:8, j * P:(j + 1) * P], comb[:, s, j, :], core.ident[0:P, 0:P])
                    ins.then_inc(comb_turned.sem, 1)

                for what, layer, i in order:
                    s, g = entries[i]
                    first, m = RUNS[s]
                    n = m * P
                    if what == "h":
                        if layer == 0 and i in score_run:
                            score(score_run[i])
                        for mo in range(HC):
                            if shared and gate and i == 1 and mo == 2:
                                score_hidden(0, 0)
                            q = hindex[(layer, i, mo)]
                            ph.hold(pe, hid_kept, o, slot_owner(HR, HB, q))
                            if layer == 0:
                                pieces = [(W1[:, g, c, mo * 128:(mo + 1) * 128], sources[c // DC][:, c % DC, columns(o * BODY + first, m)]) for c in range(KC)]
                            else:
                                ph.hold(pe, hid_kept, o, hindex[(0, i, HC - 1)])
                                pieces = [(W1b[:, g, c, mo * 128:(mo + 1) * 128], hid[0][:, i % 2, c, 0:n]) for c in range(HC)]
                            for c, (lhsT, rhs) in enumerate(pieces):
                                ins = nc.tensor.matmul(hbank[q % HR][:, 0:n], lhsT, rhs, start=c == 0, stop=c == len(pieces) - 1)
                            ins.then_inc(hid_made.sem, 1)
                        if layer == 0 and i in score_run:
                            turn_scores(score_run[i])
                    else:
                        mine = [q for q, it in enumerate(yitems) if it[0] == i]
                        turned = False
                        for n_done, q in enumerate(mine):
                            _, j, e = yitems[q]
                            if shared and gate and i == 0 and n_done == EARLY:
                                score_hidden(1, 1)
                            if e is None and not turned:
                                turn_comb(s)
                                ph.hold(pe, comb_kept, o, s)
                                turned = True
                            ph.hold(pe, out_kept, o, slot_owner(YR, YB, q))
                            if e is None:
                                ins = nc.tensor.matmul(ybank[q % YR][0:P, 0:D], combT[:, s, j * P:(j + 1) * P], b2r[:], start=True, stop=True)
                            else:
                                ph.hold(pe, hid_kept, o, hindex[(depth - 1, i, HC - 1)])
                                for c in range(HC):
                                    ins = nc.tensor.matmul(ybank[q % YR][0:P, 0:D], hid[-1][:, i % 2, c, j * P:(j + 1) * P], W2[:, e, c, :], start=c == 0, stop=c == HC - 1)
                            ins.then_inc(out_made.sem, 1)

        @block.scalar
        def _(act):
            hid_kept.open(act)
            for d in (score_kept, grown, comb_kept):
                d.open(act)
            act.wait_ge(loaded, nload)
            if norm:
                act.wait_ge(inverse_ready, 1)
                for i in range(2):
                    nc.scalar.activation(root[i][:], shift[i][:], ACT.Sqrt).then_inc(root_ready, 1)
                act.wait_ge(folded, 1)
            with act.Fori(0, NODE_LOOPS) as o:
                def grow(s):
                    ph.hold(act, centred, o, s)
                    m = RUNS[s][1]
                    nc.scalar.activation(work[:, s, 1, 0:m, :], work[:, s, 0, 0:m, :], ACT.Exp).then_inc(grown.sem, 1)

                for what, layer, i in order:
                    s, g = entries[i]
                    first, m = RUNS[s]
                    n = m * P
                    if what == "h":
                        if layer == 0 and i in score_run:
                            r = score_run[i]
                            width = RUNS[r][1] * P
                            ph.hold(act, scored, o, r)
                            ph.hold(act, scores_turned, o, r - 2)
                            nc.scalar.activation(logitT[:, r, 0:width], gbank[0:8, 0:width], ACT.Copy).then_inc(score_kept.sem, 1)
                        for mo in range(HC):
                            q = hindex[(layer, i, mo)]
                            ph.hold(act, hid_made, o, q)
                            if mo == 0:
                                back = i - 2
                                reader, r = last_reader(layer, back % len(entries))
                                if back < 0:
                                    r -= HB if reader == "h" else YB
                                ph.hold(act, hid_made if reader == "h" else out_made, o, r)
                            if norm:
                                nc.scalar.activation(hid[layer][:, i % 2, mo, 0:n], hbank[q % HR][:, 0:n], func,
                                                     scale=scale[layer][:, g, mo:mo + 1], bias=shift[layer][:, g, mo:mo + 1]).then_inc(hid_kept.sem, 1)
                            elif b1:
                                nc.scalar.activation(hid[layer][:, i % 2, mo, 0:n], hbank[q % HR][:, 0:n], func,
                                                     bias=b1c[:, g, mo:mo + 1]).then_inc(hid_kept.sem, 1)
                                if shared and gate and i == 1 and mo == 3:
                                    grow(0)
                            else:
                                nc.scalar.activation(hid[layer][:, i % 2, mo, 0:n], hbank[q % HR][:, 0:n], func).then_inc(hid_kept.sem, 1)
                        if layer == 0 and i in score_run:
                            grow(score_run[i])
                    elif gate:
                        if shared and i == 0:
                            grow(1)
                        if b2 and g == 0:
                            ph.hold(act, comb_turned, o, s)
                            bias_items = [q for q, it in enumerate(yitems) if it[2] is None and entries[it[0]][0] == s]
                            ph.hold(act, out_made, o, bias_items[-1] - YB)
                            nc.scalar.activation(combT[:, s, 0:n], gbank[0:8, 0:n], ACT.Copy).then_inc(comb_kept.sem, 1)

        @block.vector
        def _(v):
            out_kept.open(v)
            for d in (centred, routed):
                d.open(v)
            v.wait_ge(loaded, nload)
            base = 0
            if norm:
                chain = Chain(v, chain_sem)
                for i, (b, gname, be, mean, var) in enumerate(norm["columns"]):
                    chain.link(nc.vector.tensor_scalar(bn[var][:], bn[var][:], norm["eps"], None, ALU.add))
                    chain.link(nc.vector.reciprocal(shift[i][:], bn[var][:]))
                nc.vector.tensor_copy(root[0][:, 0:1, 0:1], shift[0][:, 0:1, 0:1]).then_inc(inverse_ready, 1)
                v.wait_ge(root_ready, 2)
                for i, (b, gname, be, mean, var) in enumerate(norm["columns"]):
                    chain.link(nc.vector.tensor_tensor(scale[i][:], root[i][:], root[i][:], ALU.mult))
                    chain.link(nc.vector.tensor_tensor(scale[i][:], scale[i][:], bn[var][:], ALU.mult))
                    chain.link(nc.vector.tensor_scalar(scale[i][:], scale[i][:], -0.5, 1.5, ALU.mult, ALU.add))
                    chain.link(nc.vector.tensor_tensor(scale[i][:], scale[i][:], root[i][:], ALU.mult))
                    chain.link(nc.vector.tensor_tensor(scale[i][:], scale[i][:], bn[gname][:], ALU.mult))
                    chain.link(nc.vector.tensor_tensor(shift[i][:], bn[b][:], bn[mean][:], ALU.subtract))
                    chain.link(nc.vector.tensor_tensor(shift[i][:], shift[i][:], scale[i][:], ALU.mult))
                    chain.link(nc.vector.tensor_tensor(shift[i][:], shift[i][:], bn[be][:], ALU.add))
                nc.vector.tensor_copy(root[0][:, 0:1, 0:1], shift[0][:, 0:1, 0:1]).then_inc(folded, 1)
                base = chain.n
            per_body = 2 * routing(kind) if gate else 0
            with v.Fori(0, NODE_LOOPS) as o:
                chain = Chain(v, chain_sem, per_body, o, base)

                def link(ins):
                    chain.link(ins)
                    v.sem_inc(ph.spent, 1)

                def route(s):
                    m = RUNS[s][1]
                    full = [P, m, 8]
                    z, ex, eq, val, pick, rest, pick2, both = (work[:, s, i, 0:m, :] for i in range(8))
                    top, den, low, _ = (col[:, s, i, 0:m] for i in range(4))
                    wide = lambda c: bcast_last(c, full)
                    logits = gbank[0:P, 400:400 + 8 * m].rearrange("p (j e) -> p j e", e=8)

                    def first_of(scores, picked):
                        link(nc.vector.tensor_reduce(top, scores, AX.X, ALU.max))
                        link(nc.vector.tensor_tensor(eq, scores, wide(top), ALU.is_equal))
                        link(nc.vector.scalar_tensor_tensor(val, eq, -8.0, bcast_mid(core.iota8[:], full), ALU.mult, ALU.add))
                        link(nc.vector.tensor_reduce(low, val, AX.X, ALU.min))
                        link(nc.vector.tensor_tensor(picked, val, wide(low), ALU.is_equal))

                    ph.hold(v, scores_turned, o, s)
                    if gate[1]:
                        link(nc.vector.tensor_tensor(rest, logits, bcast_mid(bg[:], full), ALU.add))
                    else:
                        link(nc.vector.tensor_scalar(rest, logits, 0.0, None, ALU.add))
                    link(nc.vector.tensor_reduce(top, rest, AX.X, ALU.max))
                    chain(nc.vector.tensor_tensor(z, rest, wide(top), ALU.subtract))
                    chain.settle()
                    v.sem_inc(centred.sem, 1)
                    ph.hold(v, grown, o, s)
                    if kind == "top2logit":
                        first_of(rest, pick)
                        link(nc.vector.scalar_tensor_tensor(rest, pick, -3e38, rest, ALU.mult, ALU.add))
                        first_of(rest, pick2)
                        link(nc.vector.tensor_tensor(both, pick, pick2, ALU.add))
                        link(nc.vector.tensor_tensor(both, both, ex, ALU.mult))
                        link(nc.vector.tensor_reduce(den, both, AX.X, ALU.add))
                        link(nc.vector.reciprocal(den, den))
                        answer, by = both, den
                    else:
                        link(nc.vector.tensor_reduce(den, ex, AX.X, ALU.add))
                        link(nc.vector.reciprocal(den, den))
                        link(nc.vector.tensor_tensor(ex, ex, wide(den), ALU.mult))
                        if kind == "argmax":
                            first_of(ex, pick)
                        elif kind == "top2prob":
                            first_of(ex, pick)
                            link(nc.vector.scalar_tensor_tensor(rest, pick, -2.0, ex, ALU.mult, ALU.add))
                            first_of(rest, pick2)
                            link(nc.vector.tensor_tensor(both, pick, pick2, ALU.add))
                            link(nc.vector.tensor_tensor(both, both, ex, ALU.mult))
                            link(nc.vector.tensor_reduce(den, both, AX.X, ALU.add))
                            link(nc.vector.tensor_scalar(den, den, 1e-12, None, ALU.max))
                            link(nc.vector.reciprocal(den, den))
                    if b2:
                        ph.hold(v, comb_turned, o, s - 2)
                    out = comb[:, s, 0:m, :]
                    if kind == "soft":
                        return
                    if kind == "argmax":
                        link(nc.vector.tensor_tensor(out, ex, pick, ALU.mult))
                    else:
                        link(nc.vector.tensor_tensor(out, both, wide(den), ALU.mult))

                for what, layer, i in order:
                    s, g = entries[i]
                    first, m = RUNS[s]
                    if gate and what == "h" and layer == 0 and (i == 1 if shared else i in score_run):
                        r = 0 if shared else score_run[i]
                        route(r)
                        if kind == "soft":
                            width = RUNS[r][1]
                            nc.vector.tensor_copy(comb[:, r, 0:width, :], work[:, r, 1, 0:width, :]).then_inc(routed.sem, 1)
                            ph.hold(v, routed, o, r)
                        else:
                            v.sem_inc(routed.sem, 1)
                    if what == "y":
                        for n_done, q in enumerate(q for q, it in enumerate(yitems) if it[0] == i):
                            if shared and gate and i == 0 and n_done == EARLY:
                                route(1)
                                v.sem_inc(routed.sem, 1)
                            _, j, e = yitems[q]
                            row = target[:, bass.ds(o * BODY + first + j, 1), :]
                            made = ybank[q % YR][0:P, 0:D].unsqueeze(1)
                            ph.hold(v, out_made, o, q)
                            if last_update(q) is not None:
                                ph.hold(v, out_kept, o, last_update(q))
                            if e is None or not gate:
                                nc.vector.tensor_tensor(row, made, row, ALU.add).then_inc(out_kept.sem, 1)
                            else:
                                nc.vector.scalar_tensor_tensor(row, made, comb[:, s, j, e:e + 1], row, ALU.mult, ALU.add).then_inc(out_kept.sem, 1)
                if gate:
                    assert chain.n == per_body, (chain.n, per_body)


def mix0(core):
    with Phase(core.nc, "m0") as ph:
        mid = ph.sb("mid", [P, NT, D])
        start_rows(core, "m0_start", mid, core.xn, "L0_mix_bo")
        linear_attention(core, "m0_att", "L0_mix_Wq", [("L0_mix_Wk", None), ("L0_mix_Wv", None)], "L0_mix_Wo", mid,
                         bias=("L0_mix_bq", "L0_mix_bk", "L0_mix_bv"), plus=1e-6)
        midT = ph.sb("midT", [128, DC, N])

        def before():
            layer_norm(core, "m0_ln1", mid, mid, midT, token_affine=("L0_mix_ln1_g", "L0_mix_ln1_b"))
            start_rows(core, "m0_bias", mid, None, "L0_mix_b2")

        ffn(core, "m0_ff", [midT], 1024, "L0_mix_W1", "L0_mix_b1", ACT.Relu, "L0_mix_W2", mid, before=before)
        layer_norm(core, "m0_ln2", mid, mid, token_affine=("L0_mix_ln2_g", "L0_mix_ln2_b"), add_to_x=True)


def ffn0(core):
    ffn(core, "f0", [core.xnT], 1024, "L0_ffn_W1", "L0_ffn_b1", ACT.Gelu, "L0_ffn_Wd", core.x, experts=8, shared=True,
        gate=("L0_ffn_Wg", "L0_ffn_bg"), kind="argmax", b2="L0_ffn_bd", tables=core.sums[1], build=AdjacencyBuild(core, (0, 12)),
        before=lambda: layer_norm(core, "ln0b", core.x, None, core.xnT, rows=False))


def ffn1(core):
    ffn(core, "f1", [core.xnT], 512, "L1_ffn_W1", "L1_ffn_b1", ACT.Gelu, "L1_ffn_W2", core.x, experts=8,
        gate=("L1_ffn_Wr", "L1_ffn_br"), kind="top2logit", b2="L1_ffn_b2", tables=core.sums[2], build=AdjacencyBuild(core, (12, 21)),
        before=lambda: layer_norm(core, "ln1b", core.x, None, core.xnT, rows=False, feature_affine=("L1_ffn_gamma", "L1_ffn_beta")))


def ffn2(core):
    ffn(core, "f2", [core.xnT], 256, "L2_ffn_W1", None, ACT.Relu, "L2_ffn_Wo", core.x, experts=8,
        gate=("L2_ffn_Wr", "L2_ffn_br"), kind="soft", b2="L2_ffn_bo", build=AdjacencyBuild(core, (21, EDGE_LOOPS)),
        norm={"w": "L2_ffn_W2", "eps": 1e-3, "columns": [[f"L2_ffn_{n}{i}" for n in ("b", "g", "be", "m", "v")] for i in (1, 2)]},
        before=lambda: layer_norm(core, "ln2b", core.x, None, core.xnT, rows=False))


def gnn3(core):
    nc = core.nc
    with Phase(nc, "g3") as ph:
        support = ph.sb("support", [P, NT, D])
        project(core, "proj3", core.xnT, [("L3_gnn_weight", D)], support, D)
        half = (NT + 1) // 2
        for first, last in ((0, half), (half, NT)):
            adjacency_sums(core, f"sums{first}", support, first, last)


def adjacency_sums(core, name, support, first, last):
    nc = core.nc
    tiles = last - first
    with Phase(nc, name) as ph:
        rows = ph.sb("rows", [P, BODY, tiles * P])
        rows_in = [ph.sem(f"rows_in{k}") for k in range(BODY)]
        used, zeroed = ph.done("used", BODY), ph.sem("zeroed")
        zeros = ph.sb("zeros", [P, BANK])
        banks = [ph.ps(f"bank{i}") for i in range((tiles + 1) // 2)]
        matrix = core.adjacency[0:N * N, :].rearrange("(p t r) o -> p t (r o)", p=P, t=NT)
        block = ph.block()

        @block.sync
        def _(sp):
            with sp.Fori(0, NODE_LOOPS) as o:
                for k in range(BODY):
                    ph.hold(sp, used, o, k - BODY)
                    sp.dma_start(rows[:, k:k + 1, :], matrix[:, bass.ds(o * BODY + k, 1), first * P:last * P]).then_inc(rows_in[k], 16)

        @block.tensor
        def _(pe):
            used.open(pe)

            def add(o, closes=False):
                for k in range(BODY):
                    ph.hold_dma(pe, rows_in[k], o)
                    for i in range(tiles):
                        ins = nc.tensor.matmul(banks[i // 2][0:P, (i % 2) * D:(i % 2 + 1) * D], rows[:, k, i * P:(i + 1) * P],
                                               support[:, bass.ds(o * BODY + k, 1), :].rearrange("p o d -> p (o d)"),
                                               start=False, stop=closes and k == BODY - 1 and (i % 2 == 1 or i == tiles - 1), skip_group_check=True)
                    ins.then_inc(used.sem, 1)
                return ins

            pe.wait_ge(zeroed, 1)
            for bank in banks:
                nc.tensor.matmul(bank[0:P, :], zeros[:, 0:P], zeros[:], start=True, stop=False, skip_group_check=True)
            with pe.Fori(0, NODE_LOOPS - 1) as o:
                add(o)
            add(NODE_LOOPS - 1, closes=True)

        @block.vector
        def _(v):
            nc.vector.memset(zeros[:], 0.0).then_inc(zeroed, 1)
            v.wait_ge(used.sem, used.at(NODE_LOOPS - 1, BODY - 1))
            for i in range(0, tiles, 2):
                n = min(2, tiles - i)
                there = core.x[:, first + i:first + i + n, :]
                nc.vector.scalar_tensor_tensor(there, banks[i // 2][0:P, 0:n * D].rearrange("p (t d) -> p t d", t=n), 0.0, there, ALU.max, ALU.add)


def mix3(core):
    with Phase(core.nc, "m3") as ph:
        mid = ph.sb("mid", [P, NT, D])
        linear_attention(core, "m3_att", "L3_mix_Wq", [("L3_mix_Wk", None), ("L3_mix_Wv", None)], "L3_mix_Wm", mid,
                         plus=1e-6, length=float(N), add=False)
        midT = ph.sb("midT", [128, DC, N])

        def before():
            layer_norm(core, "m3_ln1", mid, None, midT, rows=False, token_affine=("L3_mix_g1", "L3_mix_b1"))
            clear_rows(core, "m3_clear", mid)

        ffn(core, "m3_ff", [core.xnT, midT], 512, "L3_mix_W1", None, ACT.Relu, "L3_mix_W2", mid, before=before)
        layer_norm(core, "m3_ln2", mid, mid, token_affine=("L3_mix_g2", "L3_mix_b2"), add_to_x=True, add_xn=True)


def clear_rows(core, name, target):
    with Phase(core.nc, name) as ph:
        block = ph.block()

        @block.vector
        def _(v):
            core.nc.vector.memset(target[:], 0.0)


def ffn3(core):
    ffn(core, "f3", [core.xnT], 256, "L3_ffn_w1", "L3_ffn_b1", ACT.Gelu, "L3_ffn_w2", core.x, experts=8,
        gate=("L3_ffn_router_w", None), kind="top2prob", b2="L3_ffn_b2",
        before=lambda: layer_norm(core, "ln3b", core.x, None, core.xnT, rows=False, add_to_x=True))


def transpose_rows(core, name, buf, outT):
    nc = core.nc
    with Phase(nc, name) as ph:
        tile = ph.sb("tile", [P, BODY, D])
        staged, turned, stored = ph.done("staged", BODY), ph.done("turned", BODY), ph.done("stored", BODY)
        banks = [ph.ps(f"bank{k}") for k in range(BODY)]
        block = ph.block()

        @block.gpsimd
        def _(pool):
            staged.open(pool)
            with pool.Fori(0, NODE_LOOPS) as o:
                for k in range(BODY):
                    ph.hold(pool, turned, o, k - BODY)
                    nc.gpsimd.tensor_copy(tile[:, k:k + 1, :], buf[:, bass.ds(o * BODY + k, 1), :]).then_inc(staged.sem, 1)

        @block.tensor
        def _(pe):
            turned.open(pe)
            with pe.Fori(0, NODE_LOOPS) as o:
                for k in range(BODY):
                    ph.hold(pe, staged, o, k)
                    ph.hold(pe, stored, o, k - BODY)
                    for c in range(DC):
                        ins = nc.tensor.transpose(banks[k][:, c * P:(c + 1) * P], tile[:, k, c * 128:(c + 1) * 128], core.ident[0:P, 0:P])
                    ins.then_inc(turned.sem, 1)

        @block.scalar
        def _(act):
            stored.open(act)
            with act.Fori(0, NODE_LOOPS) as o:
                for k in range(BODY):
                    ph.hold(act, turned, o, k)
                    nc.scalar.activation(outT[:, :, columns(o * BODY + k)], banks[k][:, 0:DC * P].rearrange("p (c n) -> p c n", c=DC), ACT.Copy).then_inc(stored.sem, 1)


def edge_scores(core, name, left, left_index, right, right_index, left_width, width, stages, score, stash, kept_columns, types=None, mark=None):
    nc, a = core.nc, core.a
    with Phase(nc, name) as ph:
        left_at, right_at = ph.sb("left_at", [P, EBODY], I32), ph.sb("right_at", [P, EBODY], I32)
        lrow, rrow = ph.sb("lrow", [P, EBODY, left_width]), ph.sb("rrow", [P, EBODY, width])
        rows_in = [ph.sem(f"rows_in{k}") for k in range(EBODY)]
        stashed = [ph.sem(f"stashed{k}") for k in range(EBODY)]
        index_set, used = ph.done("index_set", EBODY), ph.done("used", EBODY)
        chain_sem, const, scaled = ph.sem("chain"), ph.sem("const"), ph.sem("scaled")
        if types:
            tw = a[types[1]].shape[1]
            trow = ph.sb("trow", [64, EBODY, P], I32)
            which = ph.sb("which", [64, EBODY, P])
            number = ph.sb("number", [64, 1])
            rel = ph.sb("rel", [64, tw])
            types_in = [ph.sem(f"types_in{k}") for k in range(EBODY)]
            compared, picked = ph.done("compared", EBODY), ph.done("picked", EBODY)
            banks = [ph.ps(f"bank{k}") for k in range(EBANKS)]
        if mark:
            keys = ph.sb("keys", [P, EBODY, P], I32)
            keys_in = ph.sem("keys_in")
            marks = Marks(core, ph, mark[1], mark[2])
        block = ph.block()

        @block.sync
        def _(sp):
            if types:
                sp.dma_start(number[:], a["c_types"]).then_inc(const, 16)
                sp.dma_start(rel[:], a[types[1]]).then_inc(const, 16)
            if mark:
                marks.load(sp)
            with sp.Fori(0, EDGE_LOOPS) as o:
                if types:
                    for k in range(EBODY):
                        ph.hold(sp, compared, o, k - EBODY)
                        sp.dma_start(trow[:, k, :], a[types[0]][bass.ds((o * EBODY + k) * P, P)].partition_broadcast(64)).then_inc(types_in[k], 16)
                if mark:
                    ph.hold(sp, marks.marked, o, -1)
                    sp.dma_start(keys[:], mark[0][bass.ds(o * EBODY * P, EBODY * P)].partition_broadcast(P)
                                 .rearrange("p (k e) -> p k e", k=EBODY)).then_inc(keys_in, 16)
                for k in range(EBODY):
                    ph.hold_dma(sp, rows_in[k], o, 2)
                    sp.dma_start(stash[bass.ds((o * EBODY + k) * P, P), :], lrow[:, k, kept_columns]).then_inc(stashed[k], 16)
            for k in range(EBODY):
                sp.wait_ge(stashed[k], 16 * EDGE_LOOPS)

        if types:
            @block.tensor
            def _(pe):
                picked.open(pe)
                pe.wait_ge(scaled, 1)
                with pe.Fori(0, EDGE_LOOPS) as o:
                    for k in range(EBODY):
                        ph.hold(pe, compared, o, k)
                        ph.hold(pe, used, o, slot_owner(EBANKS, EBODY, k))
                        nc.tensor.matmul(banks[k % EBANKS][0:P, 0:tw], which[:, k, :], rel[:], start=True, stop=True).then_inc(picked.sem, 1)

        @block.scalar
        def _(act):
            index_set.open(act)

            def set_index(o, k):
                ph.hold(act, used, o, k - EBODY)
                if not (isinstance(o, int) and o == 0):
                    ph.hold_dma(act, stashed[k], o - 1)
                one = bass.ds(o * EBODY + k, 1)
                nc.scalar.activation(left_at[:, k:k + 1], left_index[:, one], ACT.Copy)
                nc.scalar.activation(right_at[:, k:k + 1], right_index[:, one], ACT.Copy).then_inc(index_set.sem, 1)

            for k in range(EBODY):
                set_index(0, k)
            with act.Fori(1, EDGE_LOOPS) as o:
                for k in range(EBODY):
                    set_index(o, k)

        @block.gpsimd
        def _(pool):
            with pool.Fori(0, EDGE_LOOPS) as o:
                for k in range(EBODY):
                    ph.hold(pool, index_set, o, k)
                    nc.gpsimd.indirect_dma_start(lrow[:, k, :], None, left, bass.IndirectOffsetOnAxis(ap=left_at[:, k:k + 1], axis=0)).then_inc(rows_in[k], 16)
                    nc.gpsimd.indirect_dma_start(rrow[:, k, :], None, right, bass.IndirectOffsetOnAxis(ap=right_at[:, k:k + 1], axis=0)).then_inc(rows_in[k], 16)

        @block.vector
        def _(v):
            used.open(v)
            if types:
                compared.open(v)
                v.wait_ge(const, 32)
                nc.vector.tensor_scalar(rel[:], rel[:], types[2], None, ALU.mult).then_inc(scaled, 1)
            if mark:
                marks.marked.open(v)
                v.wait_ge(marks.const, 32)
            with v.Fori(0, EDGE_LOOPS) as o:
                if types:
                    for k in range(EBODY):
                        ph.hold_dma(v, types_in[k], o)
                        ph.hold(v, picked, o, k - EBODY)
                        nc.vector.tensor_scalar(which[:, k, :], trow[:, k, :], number[:, 0:1], None, ALU.is_equal).then_inc(compared.sem, 1)
                steps = (stages - 1) * EBODY + (Marks.LINKS if mark else 0)
                chain = Chain(v, chain_sem, steps, o)
                first = {}
                for turn in range(EBODY + stages - 1):
                    for stage in range(stages):
                        k = turn - stage
                        if not 0 <= k < EBODY:
                            continue
                        if stage == 0:
                            ph.hold_dma(v, rows_in[k], o, 2)
                            if types:
                                ph.hold(v, picked, o, k)
                        else:
                            chain.settle(first[k])
                            v.sem_inc(ph.spent, 1)
                        ins = score(stage, lrow[:, k, :], rrow[:, k, :], banks[k % EBANKS][0:P, 0:tw] if types else None, o * EBODY + k)
                        if stage == stages - 1:
                            ins.then_inc(used.sem, 1)
                        else:
                            chain(ins)
                            first[k] = chain.n
                if mark:
                    ph.hold_dma(v, keys_in, o)
                    for k in range(EBODY):
                        marks.compare(chain, keys[:, k, :], o, k)
                    marks.finish(v, chain, o)
                assert chain.n == steps
            v.wait_ge(used.sem, used.at(EDGE_LOOPS - 1, EBODY - 1))
            if mark:
                v.wait_ge(marks.marked.sem, marks.marked.at(EDGE_LOOPS - 1, 0))


def segment_softmax(core, name, scores, factor, alpha, heads):
    nc, a = core.nc, core.a
    LOW = -1e38
    with Phase(nc, name) as ph:
        starts = ph.sb("starts", [P, ET])
        forward = ph.sb("forward", [P, heads, ET])
        backward = ph.sb("backward", [P, heads, ET])
        mask = ph.sb("mask", [P, 2, ET])
        near = ph.sb("near", [P, ET])
        ends = ph.sb("ends", [P, 2 + 2 * heads])
        diag = ph.sb("diag", [P, 2 + 2 * heads, P])
        rows = ph.sb("rows", [P, 2 + 2 * heads, P])
        ones = ph.sb("ones", [P, P])
        equal = ph.sb("equal", [P, 2, 2, P])
        cand = ph.sb("cand", [P, heads, 2, P])
        best = ph.sb("best", [P, 2, heads])
        chain_sem, diag_set, spread_done, shifted = ph.sem("chain"), ph.sem("diag_set"), ph.sem("spread_done"), ph.sem("shifted")
        nv = 2 + 2 * heads
        per = 4
        banks = [ph.ps(f"bank{i}") for i in range((nv + per - 1) // per)]
        key = core.dstf
        block = ph.block()

        @block.vector
        def _(v):
            chain = Chain(v, chain_sem)
            link = chain.link
            chain(nc.vector.memset(ones[:], 1.0))
            chain(nc.vector.memset(starts[:, 0:1], 0.0))
            link(nc.vector.tensor_tensor(starts[:, 1:ET], key[:, 1:ET], key[:, 0:ET - 1], ALU.not_equal))
            link(nc.vector.tensor_scalar(starts[:], starts[:], LOW, None, ALU.mult))
            for h in range(heads):
                chain(nc.vector.tensor_tensor_scan(forward[:, h, :], starts[:], scores[:, h, :], 2 * LOW, ALU.add, ALU.max))
            chain.settle()
            for h in range(heads):
                chain(nc.vector.tensor_copy(backward[:, h, ET - 1:ET], scores[:, h, ET - 1:ET]))
                link(nc.vector.tensor_tensor_scan(backward[:, h, ET - 2::-1], starts[:, ET - 1:0:-1], scores[:, h, ET - 2::-1],
                                                  scores[:, h, ET - 1:ET], ALU.add, ALU.max))
            chain(nc.vector.tensor_copy(ends[:, 0:1], key[:, 0:1]))
            chain(nc.vector.tensor_copy(ends[:, 1:2], key[:, ET - 1:ET]))
            chain(nc.vector.tensor_copy(ends[:, 2:2 + heads], backward[:, :, 0:1].rearrange("p h o -> p (h o)")))
            link(nc.vector.tensor_copy(ends[:, 2 + heads:nv], forward[:, :, ET - 1:ET].rearrange("p h o -> p (h o)")))
            link(nc.vector.tensor_tensor(forward[:], forward[:], backward[:], ALU.max))
            for i in range(nv):
                ins = nc.vector.tensor_scalar(diag[:, i, :], core.ident[0:P, 0:P], ends[:, i:i + 1], None, ALU.mult)
                if i < nv - 1:
                    chain(ins)
            chain.settle()
            ins.then_inc(diag_set, 1)
            v.wait_ge(spread_done, 1)
            for i in range(nv):
                chain(nc.vector.tensor_copy(rows[:, i, :], banks[i // per][0:P, (i % per) * P:(i % per + 1) * P]))
            chain.settle()
            for side in range(2):
                link(nc.vector.tensor_scalar(equal[:, side], rows[:, 0:2, :], ends[:, side:side + 1], None, ALU.is_equal))
                link(nc.vector.tensor_scalar(equal[:, side], equal[:, side], 1.0, -LOW, ALU.subtract, ALU.mult))
                for h in range(heads):
                    chain(nc.vector.tensor_tensor(cand[:, h, 0, :], rows[:, 2 + h, :], equal[:, side, 0, :], ALU.add))
                    chain(nc.vector.tensor_tensor(cand[:, h, 1, :], rows[:, 2 + heads + h, :], equal[:, side, 1, :], ALU.add))
                chain.settle()
                link(nc.vector.tensor_reduce(best[:, side, :], cand[:], AX.XY, ALU.max))
                link(nc.vector.tensor_scalar(mask[:, side, :], key[:], ends[:, side:side + 1], None, ALU.is_equal))
                link(nc.vector.tensor_scalar(mask[:, side, :], mask[:, side, :], 1.0, -LOW, ALU.subtract, ALU.mult))
                for h in range(heads):
                    link(nc.vector.scalar_tensor_tensor(forward[:, h, :], mask[:, side, :], best[:, side, h:h + 1], forward[:, h, :], ALU.add, ALU.max))
            nc.vector.tensor_tensor(forward[:], scores[:], forward[:], ALU.subtract).then_inc(shifted, 1)

        @block.tensor
        def _(pe):
            pe.wait_ge(diag_set, 1)
            for b in range(len(banks)):
                n = min(per, nv - per * b)
                ins = nc.tensor.matmul(banks[b][0:P, 0:n * P], ones[:], diag[:, per * b:per * b + n, :], start=True, stop=True)
            ins.then_inc(spread_done, 1)

        @block.scalar
        def _(act):
            act.wait_ge(shifted, 1)
            nc.scalar.activation(alpha[:].rearrange("p e h -> p h e"), forward[:], ACT.Exp, scale=factor)


def gnn1(core):
    nc, a = core.nc, core.a
    heads, dim = 4, 64
    q, kv, val = core.table("q1", N, D), core.table("kv1", N, 2 * D), core.table("val1", ET * P, D)
    tables = core.sums[1]
    with Phase(nc, "g1a") as outer:
        enhT = outer.sb("enhT", [128, DC, N])
        dest = outer.sb("dest", [P, NT, 2 * D])
        with Phase(nc, "g1_enh") as ph:
            emb = ph.sb("emb", [128, DC])
            loaded, chain_sem = ph.sem("loaded"), ph.sem("chain")
            block = ph.block()

            @block.sync
            def _(sp):
                sp.dma_start(emb[:], a["L1_gnn_query_emb"]).then_inc(loaded, 16)
                sp.wait_ge(loaded, 16)

            @block.vector
            def _(v):
                chain = Chain(v, chain_sem)
                v.wait_ge(loaded, 16)
                chain.link(nc.vector.tensor_scalar(emb[:], emb[:], 0.1, None, ALU.mult))
                for c in range(DC):
                    chain(nc.vector.tensor_scalar(enhT[:, c, :], core.xnT[:, c, :], emb[:, c:c + 1], None, ALU.add))
        project(core, "g1_kv", enhT, [("L1_gnn_Wk", D), ("L1_gnn_Wv", D)], dest, 2 * D, bias=[("L1_gnn_bk", D), ("L1_gnn_bv", D)], table=kv)
        project(core, "g1_q", enhT, [("L1_gnn_Wq", D)], dest[:, :, 0:D], D, bias=[("L1_gnn_bq", D)], table=q)
    with Phase(nc, "g1b") as outer:
        alpha = outer.sb("alpha", [P, ET, heads])
        scores = outer.sb("scores", [P, heads, ET])

        def score(stage, krow, qrow, rel, edge):
            krow = krow[:, 0:D]
            kh = krow.rearrange("p (h d) -> p h d", h=heads)
            if stage == 0:
                return nc.vector.tensor_tensor(kh, kh, bcast_mid(rel, [P, heads, dim]), ALU.add)
            if stage == 1:
                return nc.vector.tensor_tensor(krow, krow, qrow, ALU.mult)
            return nc.vector.tensor_reduce(scores[:, :, bass.ds(edge, 1)].rearrange("p h o -> p (h o)"), kh, AX.X, ALU.add)

        edge_scores(core, "g1_sc", kv, core.src, q, core.dst, 2 * D, D, 3, score, val, slice(D, 2 * D), types=("type_rows", "L1_gnn_rel_w", 0.2),
                    mark=(a["dst_rows"], core.dstf, core.dst_once))
        segment_softmax(core, "g1_sm", scores, dim ** -0.5, alpha, heads)
        spread(core, "g1_sp", val, None, a["dst_rows"], core.dstf, core.dst_once, tables, alpha=alpha, heads=heads)
    with Phase(nc, "g1c") as outer:
        mid = outer.sb("mid", [P, NT, D])
        with Phase(nc, "g1_fin") as ph:
            table_sum = TableSum(ph, tables, D + heads)
            parts = table_sum.parts
            some = ph.sb("some", [P, NT, heads])
            den = ph.sb("den", [P, NT, heads])
            back, chain_sem = ph.sem("back"), ph.sem("chain")
            block = ph.block()

            @block.sync
            def _(sp):
                table_sum.load(sp)
                sp.dma_start(mid[:], nodes(kv[:, D:2 * D])).then_inc(back, 16)
                sp.wait_ge(back, 16)

            @block.vector
            def _(v):
                chain = Chain(v, chain_sem)
                link = chain.link
                table_sum.add(v, nc)
                total = parts[0][:, :, D:D + heads]
                wide = [P, NT, heads, dim]
                hd = lambda ap: ap.rearrange("p t (h d) -> p t h d", h=heads)
                link(nc.vector.tensor_scalar(some[:], total, 0.0, None, ALU.is_le))
                link(nc.vector.tensor_tensor(den[:], total, some[:], ALU.add))
                link(nc.vector.reciprocal(den[:], den[:]))
                link(nc.vector.tensor_tensor(hd(parts[0][:, :, 0:D]), hd(parts[0][:, :, 0:D]), bcast_last(den[:], wide), ALU.mult))
                v.wait_ge(back, 16)
                link(nc.vector.tensor_tensor(hd(mid[:]), hd(mid[:]), bcast_last(some[:], wide), ALU.mult))
                link(nc.vector.tensor_tensor(mid[:], mid[:], parts[0][:, :, 0:D], ALU.add))

        midT = outer.sb("midT", [128, DC, N])
        transpose_rows(core, "g1_turn", mid, midT)
        project(core, "g1_out", midT, [("L1_gnn_Wo", D)], mid, D, bias=[("L1_gnn_bo", D)])
        add_rows(core, "g1_res", mid, core.xn)
        layer_norm(core, "g1_ln", mid, mid, token_affine=("L1_gnn_gamma", "L1_gnn_beta"), add_to_x=True)


def add_rows(core, name, target, source):
    with Phase(core.nc, name) as ph:
        block = ph.block()

        @block.vector
        def _(v):
            core.nc.vector.tensor_tensor(target[:], target[:], source[:], ALU.add)


def row_lengths(core, name, buf, inverse):
    nc = core.nc
    with Phase(nc, name) as ph:
        square = ph.sb("square", [P, NT, D])
        total, root, part = ph.sb("total", [P, NT]), ph.sb("root", [P, NT]), ph.sb("part", [P, NT])
        summed, rooted, chain_sem = ph.sem("summed"), ph.sem("rooted"), ph.sem("chain")
        block = ph.block()

        @block.vector
        def _(v):
            link = Chain(v, chain_sem).link
            link(nc.vector.tensor_tensor(square[:], buf[:], buf[:], ALU.mult))
            nc.vector.tensor_reduce(total[:], square[:], AX.X, ALU.add).then_inc(summed, 1)
            v.wait_ge(summed, 1)
            v.wait_ge(rooted, 1)
            link(nc.vector.tensor_scalar(root[:], root[:], 1e-12, None, ALU.max))
            link(nc.vector.reciprocal(part[:], root[:]))
            link(nc.vector.tensor_tensor(part[:], part[:], total[:], ALU.mult))
            link(nc.vector.tensor_tensor(root[:], root[:], part[:], ALU.add))
            link(nc.vector.tensor_scalar(root[:], root[:], 0.5, 1e-12, ALU.mult, ALU.max))
            link(nc.vector.reciprocal(inverse[:], root[:]))
            link(nc.vector.tensor_scalar(inverse[:], inverse[:], float(D) ** 0.5, None, ALU.mult))

        @block.scalar
        def _(act):
            act.wait_ge(summed, 1)
            nc.scalar.activation(root[:], total[:], ACT.Sqrt).then_inc(rooted, 1)


def mix1(core):
    nc, a = core.nc, core.a
    heads, dim, mem = 4, 32, 4
    H = heads * dim
    with Phase(nc, "m1") as outer:
        qkv = outer.sb("qkv", [P, NT, 3 * H])
        context = outer.sb("context", [128, H])
        inverse = outer.sb("inverse", [P, NT])
        mid = outer.sb("mid", [P, NT, D])
        row_lengths(core, "m1_len", core.xn, inverse)
        project(core, "m1_qkv", core.xnT, [("L1_mix_w_qkv", 3 * H)], qkv, 3 * H, feature_scale="L1_mix_g_pre", row_scale=inverse)

        with Phase(nc, "m1_sm") as ph:
            top, den = ph.sb("top", [P, NT, heads]), ph.sb("den", [P, NT, heads])
            kbest = ph.sb("kbest", [P, H])
            kcol = ph.sb("kcol", [128, 1])
            diag, ones = ph.sb("diag", [128, H]), ph.sb("ones", [128, P])
            krow = ph.sb("krow", [P, H])
            memkv = ph.sb("memkv", [mem, 2 * H])
            tile = ph.sb("tile", [P, BODY, 2 * H + 1])
            memk, memv = ph.sb("memk", [mem, H]), ph.sb("memv", [mem, H + 1])
            inv = ph.sb("inv", [128, 1])
            loaded, chain_sem = ph.sem("loaded"), ph.sem("chain")
            qshift, qgrown, kmax_set, kturned, diag_set, spread_done = (ph.sem(n) for n in ("qshift", "qgrown", "kmax_set", "kturned", "diag_set", "spread_done"))
            kshift, kgrown, closed, ones_set = (ph.sem(n) for n in ("kshift", "kgrown", "closed", "ones_set"))
            staged, added = ph.done("staged", BODY), ph.done("added", BODY)
            tbank, rbank, cbank = ph.ps("turn"), ph.ps("row"), ph.ps("ctx")
            block = ph.block()
            qs = qkv[:, :, 0:H].rearrange("p t (h d) -> p t h d", h=heads)
            ks = qkv[:, :, H:2 * H]
            wide = [P, NT, heads, dim]

            @block.sync
            def _(sp):
                sp.dma_start(memkv[:].rearrange("m (k c) -> m k c", k=2), a["L1_mix_mem_kv"]).then_inc(loaded, 16)
                sp.wait_ge(loaded, 16)

            @block.vector
            def _(v):
                chain = Chain(v, chain_sem)
                link = chain.link
                link(nc.vector.memset(ones[:], 1.0))
                nc.vector.tensor_reduce(kbest[:], ks.rearrange("p t c -> p c t"), AX.X, ALU.max).then_inc(kmax_set, 1)
                link(nc.vector.tensor_reduce(top[:], qs, AX.X, ALU.max))
                nc.vector.tensor_tensor(qs, qs, bcast_last(top[:], wide), ALU.subtract).then_inc(qshift, 1)
                v.wait_ge(kturned, 1)
                link(nc.vector.tensor_reduce(kcol[:], tbank[:, 0:P + mem], AX.X, ALU.max))
                nc.vector.tensor_scalar(diag[:], core.ident[:], kcol[:, 0:1], None, ALU.mult).then_inc(diag_set, 1)
                v.wait_ge(spread_done, 1)
                link(nc.vector.tensor_copy(krow[:], rbank[0:P, 0:H]))
                link(nc.vector.tensor_tensor(memk[:], memkv[:, 0:H], krow[0:mem, :], ALU.subtract))
                link(nc.vector.tensor_copy(memv[:, 0:H], memkv[:, H:2 * H]))
                link(nc.vector.memset(memv[:, H:H + 1], 1.0))
                nc.vector.tensor_tensor(ks, ks, bcast_mid(krow[:], [P, NT, H]), ALU.subtract).then_inc(kshift, 1)
                v.wait_ge(qgrown, 1)
                link(nc.vector.tensor_reduce(den[:], qs, AX.X, ALU.add))
                link(nc.vector.reciprocal(den[:], den[:]))
                link(nc.vector.tensor_scalar(den[:], den[:], dim ** -0.5, None, ALU.mult))
                link(nc.vector.tensor_tensor(qs, qs, bcast_last(den[:], wide), ALU.mult))
                v.wait_ge(closed, 1)
                link(nc.vector.reciprocal(inv[:], cbank[:, H:H + 1]))
                link(nc.vector.scalar_tensor_tensor(context[:], cbank[:, 0:H], inv[:, 0:1], core.heads[:], ALU.mult, ALU.mult))

            @block.scalar
            def _(act):
                act.wait_ge(qshift, 1)
                nc.scalar.activation(qs, qs, ACT.Exp).then_inc(qgrown, 1)
                act.wait_ge(kshift, 1)
                nc.scalar.activation(memk[:], memk[:], ACT.Exp).then_inc(kgrown, 1)
                nc.scalar.activation(ks, ks, ACT.Exp).then_inc(kgrown, 1)

            @block.gpsimd
            def _(pool):
                staged.open(pool)
                nc.gpsimd.memset(tile[:, :, 2 * H:2 * H + 1], 1.0).then_inc(ones_set, 1)
                pool.wait_ge(kgrown, 2)
                with pool.Fori(0, NODE_LOOPS) as o:
                    for k in range(BODY):
                        ph.hold(pool, added, o, k - BODY)
                        nc.gpsimd.tensor_copy(tile[:, k:k + 1, 0:2 * H], qkv[:, bass.ds(o * BODY + k, 1), H:3 * H]).then_inc(staged.sem, 1)

            @block.tensor
            def _(pe):
                added.open(pe)
                pe.wait_ge(kmax_set, 1)
                pe.wait_ge(loaded, 16)
                nc.tensor.transpose(tbank[:, 0:P], kbest[:], core.ident[0:P, 0:P])
                nc.tensor.transpose(tbank[:, P:P + mem], memkv[:, 0:H], core.ident[0:mem, 0:mem]).then_inc(kturned, 1)
                pe.wait_ge(diag_set, 1)
                nc.tensor.matmul(rbank[0:P, 0:H], ones[:], diag[:], start=True, stop=True).then_inc(spread_done, 1)
                pe.wait_ge(kgrown, 2)
                pe.wait_ge(ones_set, 1)
                nc.tensor.matmul(cbank[:, 0:H + 1], memk[:], memv[:], start=True, stop=False, skip_group_check=True)
                with pe.Fori(0, NODE_LOOPS) as o:
                    for k in range(BODY):
                        ph.hold(pe, staged, o, k)
                        nc.tensor.matmul(cbank[:, 0:H + 1], tile[:, k, 0:H], tile[:, k, H:2 * H + 1], start=False, stop=False, skip_group_check=True).then_inc(added.sem, 1)
                nc.tensor.matmul(cbank[:, 0:H + 1], core.zero[0:P, 0:128], core.zero[0:P, 0:H + 1], start=False, stop=True, skip_group_check=True).then_inc(closed, 1)

        with Phase(nc, "m1_read") as ph:
            wout = ph.sb("wout", [128, D])
            b = ph.sb("b", [P, D])
            tile = ph.sb("tile", [P, BODY, H])
            qT, outT = ph.sb("qT", [128, BODY, P]), ph.sb("outT", [128, BODY, P])
            loaded = ph.sem("loaded")
            staged, turned, qkept, read, okept, result, kept = (ph.done(n, BODY) for n in ("staged", "turned", "qkept", "read", "okept", "result", "kept"))
            banks = [ph.ps(f"bank{k}") for k in range(BODY)]
            block = ph.block()

            @block.sync
            def _(sp):
                sp.dma_start(wout[:], a["L1_mix_w_out"]).then_inc(loaded, 16)
                sp.dma_start(b[:], a["L1_mix_b_out"].partition_broadcast(P)).then_inc(loaded, 16)
                sp.wait_ge(loaded, 32)

            @block.gpsimd
            def _(pool):
                staged.open(pool)
                with pool.Fori(0, NODE_LOOPS) as o:
                    for k in range(BODY):
                        ph.hold(pool, turned, o, k - BODY)
                        nc.gpsimd.tensor_copy(tile[:, k:k + 1, :], qkv[:, bass.ds(o * BODY + k, 1), 0:H]).then_inc(staged.sem, 1)

            @block.tensor
            def _(pe):
                for d in (turned, read, result):
                    d.open(pe)
                pe.wait_ge(loaded, 32)
                with pe.Fori(0, NODE_LOOPS) as o:
                    for k in range(BODY):
                        ph.hold(pe, staged, o, k)
                        ph.hold(pe, kept, o, k - BODY)
                        nc.tensor.transpose(banks[k][:, 0:P], tile[:, k, :], core.ident[0:P, 0:P]).then_inc(turned.sem, 1)
                    for k in range(BODY):
                        ph.hold(pe, qkept, o, k)
                        nc.tensor.matmul(banks[k][:, 128:128 + P], context[:], qT[:, k, :], start=True, stop=True).then_inc(read.sem, 1)
                    for k in range(BODY):
                        ph.hold(pe, okept, o, k)
                        nc.tensor.matmul(banks[k][0:P, 256:512], outT[:, k, :], wout[:], start=True, stop=True).then_inc(result.sem, 1)

            @block.scalar
            def _(act):
                qkept.open(act)
                okept.open(act)
                with act.Fori(0, NODE_LOOPS) as o:
                    for k in range(BODY):
                        ph.hold(act, turned, o, k)
                        ph.hold(act, read, o, k - BODY)
                        nc.scalar.activation(qT[:, k, :], banks[k][:, 0:P], ACT.Copy).then_inc(qkept.sem, 1)
                    for k in range(BODY):
                        ph.hold(act, read, o, k)
                        ph.hold(act, result, o, k - BODY)
                        nc.scalar.activation(outT[:, k, :], banks[k][:, 128:128 + P], ACT.Copy).then_inc(okept.sem, 1)

            @block.vector
            def _(v):
                kept.open(v)
                v.wait_ge(loaded, 32)
                with v.Fori(0, NODE_LOOPS) as o:
                    for k in range(BODY):
                        ph.hold(v, result, o, k)
                        nc.vector.tensor_tensor(mid[:, bass.ds(o * BODY + k, 1), :], banks[k][0:P, 256:512].unsqueeze(1), b[:].unsqueeze(1), ALU.add).then_inc(kept.sem, 1)

        row_lengths(core, "m1_len2", mid, inverse)
        with Phase(nc, "m1_end") as ph:
            g = ph.sb("g", [P, D])
            loaded, chain_sem = ph.sem("loaded"), ph.sem("chain")
            block = ph.block()

            @block.sync
            def _(sp):
                sp.dma_start(g[:], a["L1_mix_g_out"].partition_broadcast(P)).then_inc(loaded, 16)
                sp.wait_ge(loaded, 16)

            @block.vector
            def _(v):
                link = Chain(v, chain_sem).link
                link(nc.vector.tensor_tensor(mid[:], mid[:], bcast_last(inverse[:], [P, NT, D]), ALU.mult))
                v.wait_ge(loaded, 16)
                link(nc.vector.tensor_tensor(mid[:], mid[:], bcast_mid(g[:], [P, NT, D]), ALU.mult))
                link(nc.vector.tensor_tensor(mid[:], mid[:], core.xn[:], ALU.add))
                link(nc.vector.tensor_tensor(core.x[:], core.x[:], mid[:], ALU.add))


class LogitGather:

    def __init__(self, core, table, logits, stash, by_src, by_dst, heads):
        self.core, self.table, self.logits, self.stash, self.heads = core, table, logits, stash, heads
        self.by_src, self.by_dst = by_src, by_dst

    def place(self, ph):
        self.ph = ph
        self.src_at, self.dst_at = ph.sb("src_at", [P, EBODY], I32), ph.sb("dst_at", [P, EBODY], I32)
        self.row, self.dst_row = ph.sb("row", [P, EBODY, D + 2 * self.heads]), ph.sb("dst_row", [P, EBODY, 2 * self.heads])
        self.rows_in = [ph.sem(f"rows_in{k}") for k in range(EBODY)]
        self.stashed = [ph.sem(f"stashed{k}") for k in range(EBODY)]
        self.index_set, self.taken = ph.done("index_set", EBODY), ph.done("taken", EBODY)

    def gather(self, pool, o):
        nc = self.core.nc
        for k in range(EBODY):
            self.ph.hold(pool, self.index_set, o, k)
            for to, table, at in ((self.row, self.table, self.src_at), (self.dst_row, self.logits, self.dst_at)):
                nc.gpsimd.indirect_dma_start(to[:, k, :], None, table, bass.IndirectOffsetOnAxis(ap=at[:, k:k + 1], axis=0)).then_inc(self.rows_in[k], 16)

    def store(self, sp):
        with sp.Fori(0, EDGE_LOOPS) as o:
            for k in range(EBODY):
                self.ph.hold_dma(sp, self.rows_in[k], o, 2)
                sp.dma_start(self.stash[bass.ds((o * EBODY + k) * P, P), :], self.row[:, k, 0:D]).then_inc(self.stashed[k], 16)
        for k in range(EBODY):
            sp.wait_ge(self.stashed[k], 16 * EDGE_LOOPS)

    def set_index(self, act, o, k):
        nc, core = self.core.nc, self.core
        one = bass.ds(o * EBODY + k, 1)
        nc.scalar.activation(self.src_at[:, k:k + 1], core.src[:, one], ACT.Copy)
        nc.scalar.activation(self.dst_at[:, k:k + 1], core.dst[:, one], ACT.Copy).then_inc(self.index_set.sem, 1)

    def keep(self, act, o, k):
        nc, heads = self.core.nc, self.heads
        one = bass.ds(o * EBODY + k, 1)
        self.ph.hold_dma(act, self.rows_in[k], o, 2)
        nc.scalar.activation(self.by_src[:, one, :], self.row[:, k:k + 1, D:D + heads], ACT.Copy)
        nc.scalar.activation(self.by_dst[:, one, :], self.dst_row[:, k:k + 1, heads:2 * heads], ACT.Copy).then_inc(self.taken.sem, 1)

    def begin(self, act):
        self.index_set.open(act)
        self.taken.open(act)
        for k in range(EBODY):
            self.set_index(act, 0, k)

    def take(self, act, o):
        for k in range(EBODY):
            self.keep(act, o - 1, k)
            self.ph.hold(act, self.taken, o - 1, k)
            self.ph.hold_dma(act, self.stashed[k], o - 1)
            self.set_index(act, o, k)

    def end(self, act):
        for k in range(EBODY):
            self.keep(act, EDGE_LOOPS - 1, k)


def gnn2_mix2(core):
    nc, a = core.nc, core.a
    heads, dim = 8, 32
    full = D + 2 * heads
    table, logits, kept = core.table("h2", N, full), core.table("logits2", N, 2 * heads), core.table("kept2", ET * P, D)
    tables = core.sums[2]
    wide = [P, NT, heads, dim]
    with Phase(nc, "g2") as outer:
        alpha = outer.sb("alpha", [P, ET, heads])
        own = outer.sb("own", [P, NT, heads])
        with Phase(nc, "g2a") as inner:
            dest = inner.sb("dest", [P, NT, D])
            project(core, "g2_h", core.xnT, [("L2_gnn_W", D)], dest, D, bias=[("L2_gnn_b", D)], table=table[:, 0:D])
            with Phase(nc, "g2_logit") as ph:
                prod = ph.sb("prod", [P, NT, D])
                av = ph.sb("av", [P, 2, D])
                both = ph.sb("both", [P, NT, 2 * heads])
                loaded, made, saved, chain_sem = ph.sem("loaded"), ph.sem("made"), ph.sem("saved"), ph.sem("chain")
                block = ph.block()

                @block.sync
                def _(sp):
                    for i, n in enumerate(("src", "trg")):
                        sp.dma_start(av[:, i, :], a["L2_gnn_a_" + n].partition_broadcast(P)).then_inc(loaded, 16)
                    sp.wait_ge(loaded, 32)
                    sp.wait_ge(made, 1)
                    sp.dma_start(nodes(logits), both[:]).then_inc(saved, 16)
                    sp.dma_start(nodes(table[:, D:full]), both[:]).then_inc(saved, 16)
                    sp.wait_ge(saved, 32)

                @block.vector
                def _(v):
                    link = Chain(v, chain_sem).link
                    v.wait_ge(loaded, 32)
                    for i in range(2):
                        link(nc.vector.tensor_tensor(prod[:], dest[:], bcast_mid(av[:, i, :], [P, NT, D]), ALU.mult))
                        link(nc.vector.tensor_reduce(both[:, :, i * heads:(i + 1) * heads], prod[:].rearrange("p t (h d) -> p t h d", h=heads), AX.X, ALU.add))
                    nc.vector.tensor_tensor(own[:], both[:, :, 0:heads], both[:, :, heads:2 * heads], ALU.add).then_inc(made, 1)

        by_dst = core.xn[:].rearrange("p t d -> p (t d)")[:, 0:ET * heads].rearrange("p (e h) -> p e h", h=heads)
        start_rows(core, "m2_start", core.x, None, "L2_mix_bproj")
        linear_attention(core, "m2_att", "L2_mix_Wq", [("L2_mix_Wkv", None)], "L2_mix_Wproj", core.x, clamp=1e-6,
                         beside=LogitGather(core, table, logits, kept, alpha, by_dst, heads))
        with Phase(nc, "g2_exp") as ph:
            best = ph.sb("best", [P, 2])
            diag, ones = ph.sb("diag", [P, 2, P]), ph.sb("ones", [P, P])
            top = ph.sb("top", [P, 1])
            chain_sem, diag_set, spread_done, shifted = ph.sem("chain"), ph.sem("diag_set"), ph.sem("spread_done"), ph.sem("shifted")
            bank = ph.ps("bank")
            block = ph.block()

            @block.vector
            def _(v):
                chain = Chain(v, chain_sem)
                link = chain.link
                chain(nc.vector.memset(ones[:], 1.0))
                link(nc.vector.tensor_tensor(alpha[:], alpha[:], by_dst, ALU.add))
                for ap, i in ((alpha, 0), (own, 1)):
                    link(nc.vector.scalar_tensor_tensor(ap[:], ap[:], 0.2, ap[:], ALU.mult, ALU.max))
                    link(nc.vector.tensor_reduce(best[:, i:i + 1], ap[:], AX.XY, ALU.max))
                link(nc.vector.tensor_scalar(diag[:, 0, :], core.ident[0:P, 0:P], best[:, 0:1], None, ALU.mult))
                nc.vector.tensor_scalar(diag[:, 1, :], core.ident[0:P, 0:P], best[:, 1:2], None, ALU.mult).then_inc(diag_set, 1)
                v.wait_ge(spread_done, 1)
                link(nc.vector.tensor_reduce(top[:], bank[0:P, 0:2 * P], AX.X, ALU.max))
                link(nc.vector.tensor_scalar(own[:], own[:], top[:, 0:1], None, ALU.subtract))
                nc.vector.tensor_scalar(alpha[:], alpha[:], top[:, 0:1], None, ALU.subtract).then_inc(shifted, 1)

            @block.tensor
            def _(pe):
                pe.wait_ge(diag_set, 1)
                nc.tensor.matmul(bank[0:P, 0:2 * P], ones[:], diag[:], start=True, stop=True).then_inc(spread_done, 1)

            @block.scalar
            def _(act):
                act.wait_ge(shifted, 1)
                nc.scalar.activation(alpha[:], alpha[:], ACT.Exp)
                nc.scalar.activation(own[:], own[:], ACT.Exp)

        spread(core, "g2_sp", kept, None, a["dst_rows"], core.dstf, core.dst_once, tables, alpha=alpha, heads=heads)
        own_kept = own
        with Phase(nc, "g2_fin") as ph:
            table_sum = TableSum(ph, tables, D + heads)
            parts = table_sum.parts
            den = ph.sb("den", [P, NT, heads])
            back, chain_sem = ph.sem("back"), ph.sem("chain")
            block = ph.block()
            hprime = parts[1][:, :, 0:D]

            @block.sync
            def _(sp):
                table_sum.load(sp)
                sp.wait_ge(table_sum.added, len(tables) - 1)
                sp.dma_start(hprime, nodes(table[:, 0:D])).then_inc(back, 16)
                sp.wait_ge(back, 16)

            @block.vector
            def _(v):
                link = Chain(v, chain_sem).link
                hd = lambda ap: ap.rearrange("p t (h d) -> p t h d", h=heads)
                table_sum.add(v, nc)
                link(nc.vector.tensor_tensor(den[:], parts[0][:, :, D:D + heads], own[:], ALU.add))
                link(nc.vector.tensor_scalar(den[:], den[:], 1e-10, None, ALU.add))
                link(nc.vector.reciprocal(den[:], den[:]))
                v.wait_ge(back, 16)
                link(nc.vector.tensor_tensor(hd(hprime), hd(hprime), bcast_last(own[:], wide), ALU.mult))
                link(nc.vector.tensor_tensor(parts[0][:, :, 0:D], parts[0][:, :, 0:D], hprime, ALU.add))
                link(nc.vector.tensor_tensor(hd(parts[0][:, :, 0:D]), hd(parts[0][:, :, 0:D]), bcast_last(den[:], wide), ALU.mult))
                link(nc.vector.tensor_tensor(core.x[:], core.x[:], parts[0][:, :, 0:D], ALU.add))


def norm_of(layer):
    return lambda core: layer_norm(core, f"ln{layer}", core.x, core.xn, core.xnT, rows=layer != 2, tables=core.sums[0] if layer == 0 else ())


COLUMNS = ["L0_mix_bq", "L0_mix_b1", "L0_ffn_b1", "L1_ffn_gamma", "L1_ffn_beta", "L1_gnn_query_emb", "L1_mix_g_pre"]
EXPERT_COLUMNS = ["L1_ffn_b1", "L3_ffn_b1"] + [f"L2_ffn_{n}{i}" for i in (1, 2) for n in ("b", "g", "be", "m", "v")]
PHASES = [
    ("load", load_all),
    ("ln0", norm_of(0)), ("gnn0", gnn0), ("mix0", mix0), ("ffn0", ffn0),
    ("ln1", norm_of(1)), ("gnn1", gnn1), ("mix1", mix1), ("ffn1", ffn1),
    ("ln2", norm_of(2)), ("gnn2", gnn2_mix2), ("ffn2", ffn2),
    ("ln3", norm_of(3)), ("gnn3", gnn3), ("mix3", mix3), ("ffn3", ffn3),
]


def program(nc, a, out, stop=None):
    with ExitStack() as stack:
        core = Core(nc, a, stack)
        for name, phase in PHASES:
            phase(core)
            if name == stop:
                break
        with Phase(nc, "store") as ph:
            stored = ph.sem("stored")
            block = ph.block()

            @block.sync
            def _(sp):
                sp.dma_start(nodes(out), core.x[:]).then_inc(stored, 16)
                sp.wait_ge(stored, 16)


def kernel(**inputs):
    import numpy as np
    import concourse.bacc as bacc
    from concourse.bass_utils import run_bass_kernel_spmd as run

    def column(v):
        return v.reshape(-1, 128).T

    arrays = {name: np.asarray(v) for name, v in inputs.items()}
    arrays["src_rows"] = arrays["src"].reshape(P, ET).T.reshape(-1)
    arrays["dst_rows"] = arrays["dst"].reshape(P, ET).T.reshape(-1)
    arrays["type_rows"] = arrays["edge_type_64"].reshape(P, ET).T.reshape(-1)
    for name in ("src", "dst", "edge_weight"):
        arrays[name] = arrays[name].reshape(P, ET)
    for name in ("L0_gnn_W", "L2_mix_Wq", "L2_mix_Wkv", "L2_mix_Wproj", "L3_ffn_router_w"):
        arrays[name] = arrays[name].T
    arrays["L1_mix_mem_kv"] = arrays["L1_mix_mem_kv"].reshape(2, 128, 4).transpose(2, 0, 1)
    for name in ("L2_gnn_a_src", "L2_gnn_a_trg"):
        arrays[name] = arrays[name].reshape(D)
    for name in COLUMNS:
        arrays[name] = column(arrays[name])
    for name in EXPERT_COLUMNS:
        v = arrays[name]
        arrays[name] = v.reshape(v.shape[0], -1, 128).transpose(2, 0, 1)
    arrays["c_ident"] = np.eye(128, dtype=np.float32)
    arrays["c_heads"] = np.kron(np.eye(4), np.ones((32, 32))).astype(np.float32)
    arrays["c_iota8"] = np.tile(np.arange(8, dtype=np.float32), (P, 1))
    arrays["c_earlier"] = np.tril(np.ones((P, P), np.float32), -1)
    arrays["c_spare"] = (N + np.arange(P, dtype=np.float32))[:, None]
    arrays["c_pair_spare"] = (N * N + np.arange(P, dtype=np.float32))[:, None]
    arrays["c_types"] = np.arange(64, dtype=np.float32)[:, None]

    nc = bacc.Bacc("TRN2", target_bir_lowering=False, num_devices=1)
    given, a = {}, {}
    for name, v in arrays.items():
        if name == "L1_mix_t":
            continue
        v = np.ascontiguousarray(v)
        given["in_" + name] = v
        a[name] = nc.dram_tensor("in_" + name, v.shape, mybir.dt.from_np(v.dtype), kind="ExternalInput").ap()
    out = nc.dram_tensor("out", (N, D), F32, kind="ExternalOutput").ap()
    program(nc, a, out)
    result = run(nc, [given], core_ids=[0])
    return result.results[0]["out"]
```
